# Optimizing a Trainium2 kernel written in Bass

```python
import numpy as np
import jax
import jax.numpy as jnp

def _softmax(x, axis=-1):
    return jax.nn.softmax(x, axis=axis)

def _gelu(x):
    return jax.nn.gelu(x, approximate=True)

def _silu(x):
    return jax.nn.silu(x)

def _sigmoid(x):
    return jax.nn.sigmoid(x)

def _layernorm(x, axis=-1, eps=1e-05):
    m = jnp.mean(x, axis=axis, keepdims=True)
    v = jnp.var(x, axis=axis, keepdims=True)
    return (x - m) / jnp.sqrt(v + eps)

def _scatter_add(tgt, idx, src, axis=0):
    return tgt.at[idx].add(src)

def _segment_sum(src, seg, n):
    return jax.ops.segment_sum(src, seg, n)
kernel_name = 'mk_decoder_postln_d1_seqx_r4_e9d6dc'

def setup_inputs(seed: int=0):
    np.random.seed(seed)
    _w = jnp.asarray

    def _rec_inputs():
        import jax
        import jax.numpy as jnp
        _rk = jax.random.key(seed)
        x = -0.0002928 + 1 * jax.random.normal(jax.random.fold_in(_rk, 1), (8, 112, 256), jnp.float32)
        _lenS = 112 - jax.random.randint(jax.random.fold_in(_rk, 7), (8,), 0, max(1, 112 // 4) + 1, jnp.int32)
        _lenS2 = 375 - jax.random.randint(jax.random.fold_in(_rk, 8), (8,), 0, max(1, 375 // 4) + 1, jnp.int32)
        _ctx_1024P = jax.random.normal(jax.random.fold_in(_rk, 11), (8, 16, 256), jnp.float32)
        _ctx_1024c = jax.random.dirichlet(jax.random.fold_in(_rk, 511), 0.3 * jnp.ones((16,), jnp.float32), (8, 375))
        _ctx_1024t = jnp.einsum('bsk,bkd->bsd', _ctx_1024c, _ctx_1024P)
        _ctx_1024t = _ctx_1024t * jax.lax.rsqrt(jnp.mean(jnp.square(_ctx_1024t)) + 1e-12) * 0.953939
        ctx_1024 = 4.13588e-05 + 0.999923 * (_ctx_1024t + 0.3 * jax.random.normal(jax.random.fold_in(_rk, 611), (8, 375, 256), jnp.float32))
        return (x, ctx_1024)
    x, ctx_1024 = _rec_inputs()

    def _L0_attn_setup():
        import jax, jax.numpy as jnp
        import numpy as np
        DIM = 256
        NHEAD = 16
        HEAD_DIM = DIM // NHEAD

        def _rotate_half(t):
            h = t.shape[-1] // 2
            return jnp.concatenate([-t[..., h:], t[..., :h]], axis=-1)
        key = jax.random.key(seed)
        ks = jax.random.split(key, 5)
        B, N = (4, 512)
        return {'x': jax.random.normal(ks[0], (B, N, DIM), dtype=jnp.float32), 'qkv_w': jax.random.normal(ks[1], (3 * DIM, DIM), dtype=jnp.float32) * 0.02, 'qkv_b': jax.random.normal(ks[2], (3 * DIM,), dtype=jnp.float32) * 0.02, 'proj_w': jax.random.normal(ks[3], (DIM, DIM), dtype=jnp.float32) * 0.02, 'proj_b': jax.random.normal(ks[4], (DIM,), dtype=jnp.float32) * 0.02}
    _L0_attn_all = _L0_attn_setup()
    _L0_attn_in = {k: v for k, v in _L0_attn_all.items() if k in ('qkv_w', 'qkv_b', 'proj_w', 'proj_b')}
    del _L0_attn_all

    def _L0_xattn_setup():
        import jax, jax.numpy as jnp
        import numpy as np
        DIM = 256
        NUM_HEADS = 16
        DIM_HEAD = 64
        INNER = NUM_HEADS * DIM_HEAD
        SCALE = DIM_HEAD ** (-0.5)

        def _layernorm(x, gamma, beta, eps=1e-05):
            mu = jnp.mean(x, axis=-1, keepdims=True)
            var = jnp.mean(jnp.square(x - mu), axis=-1, keepdims=True)
            return (x - mu) * jax.lax.rsqrt(var + eps) * gamma + beta
        key = jax.random.key(seed)
        ks = jax.random.split(key, 8)
        B, SQ, SK = (2, 512, 1024)
        x = jax.random.normal(ks[0], (B, SQ, DIM), dtype=jnp.float32)
        context = jax.random.normal(ks[1], (B, SK, DIM), dtype=jnp.float32)
        ln_gamma = jnp.ones((DIM,), jnp.float32)
        ln_beta = jnp.zeros((DIM,), jnp.float32)
        w_q = jax.random.normal(ks[2], (DIM, INNER), dtype=jnp.float32) / np.sqrt(DIM)
        w_kv = jax.random.normal(ks[3], (DIM, 2 * INNER), dtype=jnp.float32) / np.sqrt(DIM)
        w_out = jax.random.normal(ks[4], (INNER, DIM), dtype=jnp.float32) / np.sqrt(INNER)
        b_out = jnp.zeros((DIM,), jnp.float32)
        gate = jnp.array([0.5], jnp.float32)
        return {'x': x, 'context': context, 'ln_gamma': ln_gamma, 'ln_beta': ln_beta, 'w_q': w_q, 'w_kv': w_kv, 'w_out': w_out, 'b_out': b_out, 'gate': gate}
    _L0_xattn_all = _L0_xattn_setup()
    _L0_xattn_in = {k: v for k, v in _L0_xattn_all.items() if k in ('ln_gamma', 'ln_beta', 'w_q', 'w_kv', 'w_out', 'b_out', 'gate')}
    del _L0_xattn_all

    def _L0_ffn_setup():
        import jax, jax.numpy as jnp
        import numpy as np
        EXPERTS = 8
        TOP_K = 2

        def swiglu(x, w1, w2, w3):
            h = x @ w1
            return h * jax.nn.sigmoid(h) * (x @ w2) @ w3
        key = jax.random.key(seed)
        ks = jax.random.split(key, 9)
        B, S, D = (4, 512, 256)
        H = 2 * D
        s = 0.02
        x = jax.random.normal(ks[0], (B, S, D), dtype=jnp.float32)
        gate_w = jax.random.normal(ks[1], (D, EXPERTS), dtype=jnp.float32) * s
        ew1 = jax.random.normal(ks[2], (EXPERTS, D, H), dtype=jnp.float32) * s
        ew2 = jax.random.normal(ks[3], (EXPERTS, D, H), dtype=jnp.float32) * s
        ew3 = jax.random.normal(ks[4], (EXPERTS, H, D), dtype=jnp.float32) * s
        sw1 = jax.random.normal(ks[5], (D, H), dtype=jnp.float32) * s
        sw2 = jax.random.normal(ks[6], (D, H), dtype=jnp.float32) * s
        sw3 = jax.random.normal(ks[7], (H, D), dtype=jnp.float32) * s
        return {'x': x, 'gate_w': gate_w, 'ew1': ew1, 'ew2': ew2, 'ew3': ew3, 'sw1': sw1, 'sw2': sw2, 'sw3': sw3}
    _L0_ffn_all = _L0_ffn_setup()
    _L0_ffn_in = {k: v for k, v in _L0_ffn_all.items() if k in ('gate_w', 'ew1', 'ew2', 'ew3', 'sw1', 'sw2', 'sw3')}
    del _L0_ffn_all
    return {'x': x, 'ctx_1024': ctx_1024, 'L0_attn_qkv_w': _L0_attn_in['qkv_w'], 'L0_attn_qkv_b': _L0_attn_in['qkv_b'], 'L0_attn_proj_w': _L0_attn_in['proj_w'], 'L0_attn_proj_b': _L0_attn_in['proj_b'], 'L0_xattn_ln_gamma': _L0_xattn_in['ln_gamma'], 'L0_xattn_ln_beta': _L0_xattn_in['ln_beta'], 'L0_xattn_w_q': _L0_xattn_in['w_q'], 'L0_xattn_w_kv': _L0_xattn_in['w_kv'], 'L0_xattn_w_out': _L0_xattn_in['w_out'], 'L0_xattn_b_out': _L0_xattn_in['b_out'], 'L0_xattn_gate': _L0_xattn_in['gate'], 'L0_ffn_gate_w': _L0_ffn_in['gate_w'], 'L0_ffn_ew1': _L0_ffn_in['ew1'], 'L0_ffn_ew2': _L0_ffn_in['ew2'], 'L0_ffn_ew3': _L0_ffn_in['ew3'], 'L0_ffn_sw1': _L0_ffn_in['sw1'], 'L0_ffn_sw2': _L0_ffn_in['sw2'], 'L0_ffn_sw3': _L0_ffn_in['sw3']}

def reference(x, ctx_1024, L0_attn_qkv_w, L0_attn_qkv_b, L0_attn_proj_w, L0_attn_proj_b, L0_xattn_ln_gamma, L0_xattn_ln_beta, L0_xattn_w_q, L0_xattn_w_kv, L0_xattn_w_out, L0_xattn_b_out, L0_xattn_gate, L0_ffn_gate_w, L0_ffn_ew1, L0_ffn_ew2, L0_ffn_ew3, L0_ffn_sw1, L0_ffn_sw2, L0_ffn_sw3):
    import jax
    import jax.numpy as jnp

    def _L0_attn_ref(x, qkv_w, qkv_b, proj_w, proj_b):
        import jax, jax.numpy as jnp
        import numpy as np
        DIM = 256
        NHEAD = 16
        HEAD_DIM = DIM // NHEAD

        def _rotate_half(t):
            h = t.shape[-1] // 2
            return jnp.concatenate([-t[..., h:], t[..., :h]], axis=-1)
        B, N, D = x.shape
        H, hd = (NHEAD, HEAD_DIM)
        qkv = x @ qkv_w.T + qkv_b
        qkv = jnp.transpose(qkv.reshape(B, N, 3, H, hd), (2, 0, 3, 1, 4))
        q, k, v = (qkv[0], qkv[1], qkv[2])
        inv_freq = 1.0 / 10000.0 ** (jnp.arange(0, hd, 2, dtype=x.dtype) / hd)
        pos = jnp.arange(N, dtype=x.dtype)
        freqs = pos[:, None] * inv_freq[None, :]
        emb = jnp.concatenate([freqs, freqs], axis=-1)
        cos = jnp.cos(emb)[None, None, None]
        sin = jnp.sin(emb)[None, None, None]
        q = q * cos + _rotate_half(q) * sin
        k = k * cos + _rotate_half(k) * sin
        scale = hd ** (-0.5)
        attn = jnp.einsum('abhqd,abhkd->abhqk', q, k) * scale
        attn = jax.nn.softmax(attn, axis=-1)
        out = jnp.einsum('abhqk,bhkd->abhqd', attn, v)
        out = jnp.swapaxes(out, 1, 2).reshape(B, N, D)
        out = out @ proj_w.T + proj_b
        return out

    def _L0_xattn_ref(x, context, ln_gamma, ln_beta, w_q, w_kv, w_out, b_out, gate):
        import jax, jax.numpy as jnp
        import numpy as np
        DIM = 256
        NUM_HEADS = 16
        DIM_HEAD = 64
        INNER = NUM_HEADS * DIM_HEAD
        SCALE = DIM_HEAD ** (-0.5)

        def _layernorm(x, gamma, beta, eps=1e-05):
            mu = jnp.mean(x, axis=-1, keepdims=True)
            var = jnp.mean(jnp.square(x - mu), axis=-1, keepdims=True)
            return (x - mu) * jax.lax.rsqrt(var + eps) * gamma + beta
        B, SQ, _ = x.shape
        SK = context.shape[1]
        xn = _layernorm(x, ln_gamma, ln_beta)
        q = (xn @ w_q).reshape(B, SQ, NUM_HEADS, DIM_HEAD)
        kv = context @ w_kv
        k, v = jnp.split(kv, 2, axis=-1)
        k = k.reshape(B, SK, NUM_HEADS, DIM_HEAD)
        v = v.reshape(B, SK, NUM_HEADS, DIM_HEAD)
        scores = jnp.einsum('bqhd,bkhd->bhqk', q * SCALE, k)
        attn = jax.nn.softmax(scores, axis=-1)
        out = jnp.einsum('bhqk,bkhd->bqhd', attn, v).reshape(B, SQ, INNER)
        out = out @ w_out + b_out
        return out * jnp.tanh(gate[0])

    def _L0_ffn_ref(x, gate_w, ew1, ew2, ew3, sw1, sw2, sw3):
        import jax, jax.numpy as jnp
        import numpy as np
        EXPERTS = 8
        TOP_K = 2

        def swiglu(x, w1, w2, w3):
            h = x @ w1
            return h * jax.nn.sigmoid(h) * (x @ w2) @ w3
        B, S, D = x.shape
        gate_out = x @ gate_w
        top_v, top_i = jax.lax.top_k(gate_out, TOP_K)
        masked = jnp.full_like(gate_out, -1e+20)
        bi = jnp.arange(B)[:, None, None]
        si = jnp.arange(S)[None, :, None]
        masked = masked.at[bi, si, top_i].set(top_v)
        probs = jax.nn.softmax(masked, axis=-1)
        chosen = jnp.zeros_like(gate_out, dtype=bool).at[bi, si, top_i].set(True)
        w = jnp.where(chosen, probs, 0.0)

        def one_expert(w1, w2, w3, we):
            return swiglu(x, w1, w2, w3) * we[..., None]
        out = jax.vmap(one_expert, in_axes=(0, 0, 0, 2))(ew1, ew2, ew3, w).sum(0)
        out = out + swiglu(x, sw1, sw2, sw3)
        return out
    x = _layernorm(x + _L0_attn_ref(x, L0_attn_qkv_w, L0_attn_qkv_b, L0_attn_proj_w, L0_attn_proj_b), axis=-1)
    x = _layernorm(x + _L0_xattn_ref(x, ctx_1024, L0_xattn_ln_gamma, L0_xattn_ln_beta, L0_xattn_w_q, L0_xattn_w_kv, L0_xattn_w_out, L0_xattn_b_out, L0_xattn_gate), axis=-1)
    x = _layernorm(x + _L0_ffn_ref(x, L0_ffn_gate_w, L0_ffn_ew1, L0_ffn_ew2, L0_ffn_ew3, L0_ffn_sw1, L0_ffn_sw2, L0_ffn_sw3), axis=-1)
    return x

_drawn_inputs = setup_inputs


def setup_inputs(seed=0):
    import zlib

    import numpy as np

    out = dict(_drawn_inputs(seed))
    spreads = {'L0_xattn_ln_gamma': (1.0, 0.6),
     'L0_xattn_ln_beta': (0.0, 0.8),
     'L0_xattn_b_out': (0.0, 0.1)}
    factors = {'L0_attn_qkv_w': 5.799,
     'L0_attn_qkv_b': 8.0,
     'L0_attn_proj_w': 4.589,
     'L0_attn_proj_b': 2.94,
     'L0_ffn_gate_w': 3.844,
     'L0_ffn_ew1': 3.378,
     'L0_ffn_ew2': 3.339,
     'L0_ffn_ew3': 3.347,
     'L0_ffn_sw1': 3.064,
     'L0_ffn_sw2': 3.031,
     'L0_ffn_sw3': 3.025}
    for name, (base, spread) in spreads.items():
        noise = np.random.default_rng([zlib.crc32(name.encode()), seed]).standard_normal(out[name].shape)
        drawn = base * np.exp(spread * noise) if base else spread * noise
        out[name] = jnp.asarray(drawn.astype(out[name].dtype))
    for name, factor in factors.items():
        out[name] = (out[name] * factor).astype(out[name].dtype)
    return out
```

```python
from contextlib import ExitStack

import numpy as np

import concourse.bass as bass
from concourse import mybir

F32 = mybir.dt.float32
F32R = mybir.dt.float32r
U32 = mybir.dt.uint32
ALU = mybir.AluOpType
ACT = mybir.ActivationFunctionType
X = mybir.AxisListType.X

B, N, D = 8, 112, 256
P = 128
KD = D // P
H, HD = 16, 16
CH, CHD = 16, 64
INNER = CH * CHD
SK, ST = 375, 3
SKT = SK // ST
SKP = SK + 1
PAIRS = CH // 2
EXP = 8
HID = 2 * D
MH = HID // P
TOK = B * N
HALF = TOK // 2
EPS = 1e-5
SELF_SCALE = float(HD) ** -0.5
CROSS_SCALE = float(CHD) ** -0.5

FILLS = ["QA", "QB", "KA", "KB", "S0", "S1", "S2", "S3", "T0", "T1", "O0", "T2", "T3", "O1",
         "C0", "C1", "OT", "PJ", "NT", "Q0", "Q1"]
LAST_READ = {
    "QA": ("qk_stacked_t", 4, 0), "QB": ("qk_stacked_t", 4, 1), "KA": ("qk_stacked_t", 4, 2),
    "KB": ("qk_stacked_t", 4, 3),
    "S0": ("s_shifted", 4, 0), "S1": ("s_shifted", 4, 1), "S2": ("s_shifted", 4, 2), "S3": ("s_shifted", 4, 3),
    "T0": ("pt_lo", 4, 0), "T1": ("pt_lo", 4, 1), "T2": ("pt_lo", 4, 2), "T3": ("pt_lo", 4, 3),
    "O0": ("o_normed", 2, 0), "O1": ("o_normed", 2, 1), "OT": ("ot_lo", 1, 0),
    "C0": ("ctxt_lo", 2, 0), "C1": ("ctxt_lo", 2, 1), "PJ": ("res1", 1, 0),
    "NT": ("xn_affine", 2, 1), "Q0": ("qt_lo", 2, 0), "Q1": ("qt_lo", 2, 1),
}
KV_FILLS = ["K0", "V00", "K1", "V01", "K2", "V02", "K3", "K4", "V10", "K5", "V11", "K6", "V12", "K7"]
V_AT = {0: "V02", 2: "V10", 3: "V11", 4: "V12", 6: "V00", 7: "V01"}


def fill_no(name, b):
    return len(FILLS) * b + FILLS.index(name) + 1


def kv_no(name, b):
    return len(KV_FILLS) * b + KV_FILLS.index(name) + 1


def kv_reads(b, name, kind):
    done = KV_FILLS[:KV_FILLS.index(name) + 1]
    per = sum(f[0] == kind for f in KV_FILLS)
    return per * b + sum(f[0] == kind for f in done)


class Signals:

    def __init__(self, nc, ctx, block):
        self.nc, self.ctx, self.block, self.sems = nc, ctx, block, {}

    def __getitem__(self, name):
        if name not in self.sems:
            self.sems[name] = self.ctx.enter_context(self.nc.semaphore(self.block + "_" + name))
        return self.sems[name]


def later(count):
    return not isinstance(count, int) or count > 0


def product(eng, out, lhs, rhs, start=True, stop=True, **kw):
    (lh, ll), (rh, rl) = lhs, rhs
    eng.matmul(out, ll, rh, start=start, stop=False, **kw)
    eng.matmul(out, lh, rl, start=False, stop=False, **kw)
    return eng.matmul(out, lh, rh, start=False, stop=stop, **kw)


def split_pair(nc, ctx, name, shape):
    return tuple(ctx.enter_context(nc.sbuf_tensor(f"{name}_{part}", shape, F32R)) for part in ("hi", "lo"))


def product_over_width(pe, out, lhs, w, cols):
    for k in range(KD):
        last = product(pe, out, tuple(t[:, k, :] for t in lhs), tuple(t[:, k, cols] for t in w),
                       start=k == 0, stop=k == KD - 1)
    return last


def preparation_block(nc, sg, A, ident, consts, weights, qk_rot, v_all):
    w_k, w_v, w_q, w_o, w_proj = weights
    with ExitStack() as ctx:
        def sb(name, shape, dt=F32):
            return ctx.enter_context(nc.sbuf_tensor(name, shape, dt))

        w_qkv = split_pair(nc, ctx, "w_qkv", [P, KD, 3 * D])
        raw = [sb(f"raw{i}", [P, 2048]) for i in range(2)]
        rope_sb = sb("rope_sb", [N, 2, HD])
        bias_qkv = sb("bias_qkv", [N, 3 * D])
        x_in = sb("x_in", [N, 2, D])
        xt = [split_pair(nc, ctx, f"xt{i}", [P, KD, N]) for i in range(2)]
        qk = sb("qk", [N, 2, 2 * D])
        sin_part = sb("sin_part", [N, 2, 2 * D])
        ps_w = ctx.enter_context(nc.psum_tensor("ps_w", [P, 2, 512], F32))
        ps_x = ctx.enter_context(nc.psum_tensor("ps_x", [P, 2, 512], F32))
        ps_qk = ctx.enter_context(nc.psum_tensor("ps_qk", [P, 2, 512], F32))
        ps_v = ctx.enter_context(nc.psum_tensor("ps_v", [P, 2, 512], F32))
        plain = [(1, w_k, A["w_kv"][:, 0:INNER]), (0, w_v, A["w_kv"][:, INNER:2 * INNER]), (1, w_q, A["w_q"]),
                 (0, w_o, A["w_out"])]
        heads, hw = 2 * H, HD // 2
        block = ctx.enter_context(nc.Block())

        @block.sync
        def _(sp):
            sp.dma_start(raw[0][:, 0:6 * D].rearrange("p (o d) -> p o d", o=6),
                         A["qkv_w"].rearrange("(o p) d -> p o d", p=P)).then_inc(sg["raw0"], 16)
            sp.dma_start(raw[0][:, 6 * D:8 * D].rearrange("p (o d) -> p o d", o=2),
                         A["proj_w"].rearrange("(o p) d -> p o d", p=P)).then_inc(sg["raw0"], 16)
            for b in range(B):
                if later(b - 1):
                    sp.wait_ge(sg["xt_full"], b - 1)
                sp.dma_start(x_in[:, b % 2, :], A["x"][b]).then_inc(sg[f"x_loaded{b % 2}"], 16)
            for i, (stage, _, src) in enumerate(plain):
                if i == 1:
                    sp.wait_ge(sg["w_full"], 4)
                elif i >= 2:
                    sp.wait_ge(sg["w_lo"], i - 1)
                src = src.rearrange("(k p) n -> p k n", p=P)
                sp.dma_start(raw[stage][:, :].rearrange("p (k n) -> p k n", k=src.shape[1]), src)\
                    .then_inc(sg[f"raw{stage}"], 16)

        @block.gpsimd
        def _(pool):
            pool.dma_start(rope_sb[:, :, :], A["rope"]).then_inc(sg["consts"], 16)
            pool.dma_start(bias_qkv[:, :], A["qkv_b"].partition_broadcast(N)).then_inc(sg["consts"], 16)
            pool.memset(ident[:, :], 0.0).then_inc(sg["zeroed"], 1)
            pool.wait_ge(sg["zeroed"], 1)
            pool.affine_select(out=ident[:, :], in_=ident[:, :], compare_op=ALU.not_equal, fill=1.0, base=0,
                               pattern=[[-1, P]], channel_multiplier=1).then_inc(sg["ident"], 1)
            for name in ("proj_b", "b_out", "gate"):
                pool.dma_start(consts[name][:, :], A[name].partition_broadcast(N)).then_inc(sg["consts2"], 16)
            for name in ("gamma", "beta"):
                pool.dma_start(consts[name][:, :], A[name].rearrange("(k p) -> p k", p=P),
                               allow_slow_non_contiguous=True).then_inc(sg["consts2"], 16)
            pool.memset(consts["neg_half"][:, :], -0.5).then_inc(sg["neg_half"], 1)
            pool.wait_ge(sg["consts"], 32)
            with pool.Fori(0, B // 2) as b0:
                for i in range(2):
                    pool.wait_ge(sg["qk_biased"], 2 * b0 + i + 1)
                    t = qk[:, i, :].rearrange("p (h w) -> p h w", w=HD)
                    out = sin_part[:, i, :].rearrange("p (h w) -> p h w", w=HD)
                    for dst, src in ((0, hw), (hw, 0)):
                        sin = rope_sb[:, 1, dst:dst + hw].unsqueeze(1).to_broadcast([N, heads, hw])
                        pool.tensor_tensor(out[:, :, dst:dst + hw], t[:, :, src:src + hw], sin, ALU.mult)\
                            .then_inc(sg["sin_part"], 1)
            pool.wait_ge(sg["consts2"], 5 * 16)

        @block.scalar
        def _(act):
            def hi(dst, src):
                return act.activation(dst, src, ACT.Copy)

            for i in range(4):
                k, half = i % 2, i // 2
                act.wait_ge(sg["w_full"], i + 1)
                if half == 0:
                    hi(w_qkv[0][:, k, 0:512], ps_w[:, k, :]).then_inc(sg["w_hi"], 1)
                else:
                    hi(w_qkv[0][:, k, 512:768], ps_w[:, k, 0:256]).then_inc(sg["w_hi"], 1)
                    hi(w_proj[0][:, k, :], ps_w[:, k, 256:512]).then_inc(sg["w_hi"], 1)
            seen = [32, 0]
            with act.Fori(0, B // 2) as b0:
                for i in range(2):
                    b = 2 * b0 + i
                    act.wait_ge(sg["xt_full"], b + 1)
                    hi(xt[i][0][:, :, :].rearrange("p k n -> p (k n)"), ps_x[:, i, 0:KD * N]).then_inc(sg["xt_hi"], 1)
            for stage, (w, _), _ in plain:
                seen[stage] += 16
                act.wait_ge(sg[f"raw{stage}"], seen[stage])
                hi(w[:, :, :].rearrange("p k n -> p (k n)"), raw[stage][:, :]).then_inc(sg["w_hi"], 1)
            act.wait_ge(sg["consts2"], 5 * 16)
            act.activation(consts["gate"][:, :], consts["gate"][:, :], ACT.Tanh).then_inc(sg["gate_ready"], 1)

        @block.vector
        def _(dve):
            def lo(dst, src, part):
                return dve.tensor_tensor(dst, src, part.bitcast(F32), ALU.subtract)

            for i in range(4):
                k, half = i % 2, i // 2
                if half == 0:
                    dve.wait_ge(sg["w_hi"], i + 1)
                    lo(w_qkv[1][:, k, 0:512], ps_w[:, k, :], w_qkv[0][:, k, 0:512]).then_inc(sg["wt_lo"], 1)
                else:
                    dve.wait_ge(sg["w_hi"], 2 * i)
                    lo(w_qkv[1][:, k, 512:768], ps_w[:, k, 0:256], w_qkv[0][:, k, 512:768]).then_inc(sg["wt_lo"], 1)
                    lo(w_proj[1][:, k, :], ps_w[:, k, 256:512], w_proj[0][:, k, :]).then_inc(sg["wt_lo"], 1)
            dve.wait_ge(sg["consts"], 32)
            with dve.Fori(0, B // 2) as b0:
                for i in range(2):
                    b = 2 * b0 + i
                    dve.wait_ge(sg["xt_hi"], b + 1)
                    lo(xt[i][1][:, :, :].rearrange("p k n -> p (k n)"), ps_x[:, i, 0:KD * N],
                       xt[i][0][:, :, :].rearrange("p k n -> p (k n)")).then_inc(sg["xt_lo"], 1)
                    dve.wait_ge(sg["qk_full"], b + 1)
                    dve.tensor_tensor(qk[:, i, :], ps_qk[0:N, i, :], bias_qkv[:, 0:2 * D], ALU.add)\
                        .then_inc(sg["qk_biased"], 1)
                    dve.wait_ge(sg["v_full"], b + 1)
                    dve.tensor_tensor(v_all[:, b, :], ps_v[0:N, i, 0:D], bias_qkv[:, 2 * D:3 * D], ALU.add)\
                        .then_inc(sg["v_biased"], 1)
                    cos = rope_sb[:, 0, :].unsqueeze(1).to_broadcast([N, heads, HD])
                    dve.wait_ge(sg["sin_part"], 2 * b + 2)
                    dve.tensor_tensor(qk[:, i, :].rearrange("p (h w) -> p h w", w=HD),
                                      qk[:, i, :].rearrange("p (h w) -> p h w", w=HD), cos, ALU.mult)\
                        .then_inc(sg["cos_part"], 1)
                    dve.wait_ge(sg["cos_part"], b + 1)
                    dve.tensor_tensor(qk_rot[:, b, :], qk[:, i, :], sin_part[:, i, :], ALU.add).then_inc(sg["rotated"], 1)
            for i, (stage, (hi_w, lo_w), _) in enumerate(plain):
                dve.wait_ge(sg["w_hi"], 7 + i)
                lo(lo_w[:, :, :].rearrange("p k n -> p (k n)"), raw[stage][:, :],
                   hi_w[:, :, :].rearrange("p k n -> p (k n)")).then_inc(sg["w_lo"], 1)
            dve.wait_ge(sg["gate_ready"], 1)
            dve.tensor_scalar(consts["b_out"][:, :], consts["b_out"][:, :], consts["gate"][:, 0:1], None, ALU.mult)\
                .then_inc(sg["bias_out_gated"], 1)

        @block.tensor
        def _(pe):
            pe.wait_ge(sg["raw0"], 32)
            pe.wait_ge(sg["ident"], 1)
            for i in range(4):
                k, half = i % 2, i // 2
                if later(i - 1):
                    pe.wait_ge(sg["wt_lo"], i - 1)
                for j in range(4):
                    o = 4 * half + j
                    last = pe.transpose(ps_w[:, k, j * P:(j + 1) * P], raw[0][:, o * D + k * P:o * D + (k + 1) * P],
                                        ident[:, :])
                last.then_inc(sg["w_full"], 1)

            def x_transpose(b0, i):
                b = 2 * b0 + i
                pe.wait_ge(sg[f"x_loaded{i}"], 16 * (b0 + 1))
                if later(b - 1):
                    pe.wait_ge(sg["xt_lo"], b - 1)
                for k in range(KD):
                    last = pe.transpose(ps_x[:, i, k * N:(k + 1) * N], x_in[:, i, k * P:(k + 1) * P], ident[0:N, 0:N])
                last.then_inc(sg["xt_full"], 1)

            def project(b, i):
                pe.wait_ge(sg["xt_lo"], b + 1)
                if later(b - 1):
                    pe.wait_ge(sg["qk_biased"], b - 1)
                if later(b - 1):
                    pe.wait_ge(sg["v_biased"], b - 1)
                product_over_width(pe, ps_qk[0:N, i, :], xt[i], w_qkv, slice(0, 512)).then_inc(sg["qk_full"], 1)
                product_over_width(pe, ps_v[0:N, i, 0:D], xt[i], w_qkv, slice(512, 768)).then_inc(sg["v_full"], 1)

            x_transpose(0, 0)
            x_transpose(0, 1)
            pe.wait_ge(sg["wt_lo"], 6)
            project(0, 0)
            project(1, 1)
            with pe.Fori(1, B // 2) as b0:
                for i in range(2):
                    x_transpose(b0, i)
                for i in range(2):
                    project(2 * b0 + i, i)


def attention_block(nc, sg, A, x2_all, ident, consts, weights, qk_rot, v_all):
    w_k, w_v, w_q, w_o, w_proj = weights
    bias_proj, bias_out, gate, gamma, beta, neg_half = (consts[n] for n in ("proj_b", "b_out", "gate", "gamma", "beta",
                                                                           "neg_half"))
    with ExitStack() as ctx:
        def sb(name, shape, dt=F32):
            return ctx.enter_context(nc.sbuf_tensor(name, shape, dt))

        def pair(name, shape):
            return split_pair(nc, ctx, name, shape)


        x_cur = sb("x_cur", [N, D])
        x_res = sb("x_res", [N, D])
        v_self = pair("v_self", [N, B, 2 * HD])
        work = sb("work", [N, 2048])
        qk_t = (sb("q_stacked_t", [P, B, N], F32R), sb("k_stacked_t", [P, B, N], F32R))
        s_max = sb("s_max", [N, 4, 4])
        s_sum = sb("s_sum", [N, 2 * B])
        s_rcp = sb("s_rcp", [N, 2 * B])
        pt = pair("pt", [N, 8, N])
        o_self = sb("o_self", [N, 2 * B, HD])
        o_rows = sb("o_rows", [N, D])
        o_dram = nc.dram_tensor("o_shuffle", (B, 2 * B, N, HD), F32).ap()
        ot = pair("ot", [P, KD, N])
        res = sb("res", [N, D])
        xn = sb("xn", [N, D])
        x1 = sb("x1", [N, D])
        stats = sb("stats", [N, 2, 6])
        mv = sb("mv", [N, 2, 2])
        rstd = sb("rstd", [N, 2])
        xnt_f = sb("xnt_f", [P, KD, N])
        xnt = pair("xnt", [P, KD, N])
        ctx_raw = sb("ctx_raw", [SKT, ST, D])
        ctxt = pair("ctxt", [P, KD, SKP])
        qt = pair("qt", [P, PAIRS, N])
        kt = pair("kt", [P, 2, SKP])
        v = pair("v", [SKT, 2, ST, 512])
        probs = sb("probs", [N, 2, 2, SK])
        c_max = sb("c_max", [N, 2, 2])
        c_neg = sb("c_neg", [N, 2, 2])
        c_sum = sb("c_sum", [N, 2, 2])
        c_rcp = sb("c_rcp", [N, 2, 2])
        cpt = pair("cpt", [SKT, 2, ST, N])
        oct_ = pair("oct", [P, PAIRS, N])
        res2 = sb("res2", [N, D])
        stats2 = sb("stats2", [N, 6])
        mv2 = sb("mv2", [N, 2])
        rstd2 = sb("rstd2", [N, 1])

        ps_s = ctx.enter_context(nc.psum_tensor("ps_s", [P, 2, 512], F32))
        ps_t = ctx.enter_context(nc.psum_tensor("ps_t", [P, 2, 512], F32))
        ps_o = ctx.enter_context(nc.psum_tensor("ps_o", [P, 512], F32))
        ps_kv = ctx.enter_context(nc.psum_tensor("ps_kv", [P, 512], F32))
        ps_a = ctx.enter_context(nc.psum_tensor("ps_a", [P, 2, 512], F32))

        def bank(name):
            return ps_a[:, FILLS.index(name) % 2, :]

        stack = work[:, :].rearrange("p (t b r c w) -> p t b r c w", t=2, b=B, r=2, c=4)
        e_self = work[:, 0:2 * B * N].rearrange("p (s n) -> p s n", s=2 * B)
        block = ctx.enter_context(nc.Block())

        def qk_src(b, i, r):
            return qk_rot[:, :, bass.ds(i * D + (2 * b + r) * HD, HD)].unsqueeze(2).to_broadcast([N, B, 2, HD])

        def iterations(eng, iteration):
            iteration(0, True)
            with eng.Fori(1, B - 1) as b:
                iteration(b, True)
            iteration(B - 1, False)

        @block.sync
        def _(sp):
            def entry(b):
                if later(b):
                    sp.wait_ge(sg["a_full"], fill_no("C1", b - 1))
                sp.dma_start(ctx_raw[:, :, :], A["ctx"][bass.ds(b, 1)].rearrange("a (t p) d -> p (a t) d", p=SKT))\
                    .then_inc(sg["ctx_loaded"], 16)
                if later(b):
                    sp.wait_ge(sg["x_res_ready"], b)
                sp.dma_start(x_cur[:, :], A["x"][bass.ds(b, 1)].rearrange("a n d -> (a n) d")).then_inc(sg["x_loaded"], 16)
                sp.wait_ge(sg["o_normed"], 2 * b + 2)
                sp.dma_start(o_dram[bass.ds(b, 1)].rearrange("a k q w -> q (a k) w"), o_self[:, :, :])\
                    .then_inc(sg["o_stored"], 16)
                sp.wait_ge(sg["o_stored"], 16 * (b + 1))
                if later(b):
                    sp.wait_ge(sg["a_full"], fill_no("OT", b - 1))
                sp.dma_start(o_rows[:, :], o_dram[bass.ds(b, 1)].rearrange("a k (i l) w -> (a k i) (l w)", l=D // HD))\
                    .then_inc(sg["o_rows_loaded"], 16)
            for b in range(B):
                entry(b)

        @block.gpsimd
        def _(pool):
            for t in ctxt:
                pool.memset(t[:, :, SK:SKP].bitcast(F32), 0.0).then_inc(sg["padded"], 1)

            def residual(b):
                pool.wait_ge(sg["x_loaded"], 16 * (b + 1))
                if later(b):
                    pool.wait_ge(sg["res1"], b)
                pool.tensor_tensor(x_res[:, :], x_cur[:, :], bias_proj[:, :], ALU.add).then_inc(sg["x_res_ready"], 1)

            def stack_lo(b):
                pool.wait_ge(sg["qk_hi"], 4 * b + 4)
                for i in range(2):
                    for r in range(2):
                        src = qk_src(b, i, r)
                        hi = stack[:, i, :, r, 0:1, :].to_broadcast([N, B, 2, HD])
                        dst = stack[:, i, :, r, 1:4:2, :] if i == 0 else stack[:, i, :, r, 2:4, :]
                        pool.tensor_tensor(dst.bitcast(F32R), src, hi, ALU.subtract).then_inc(sg["qk_lo"], 1)

            def x1_out(b):
                pool.wait_ge(sg["x1_ready"], b + 1)
                pool.nop(nofuse=True)
                pool.tensor_tensor(x2_all[0:N, b, :], x1[:, :], bias_out[:, :], ALU.add).then_inc(sg["x1_kept"], 1)

            def rsqrt(rs, mean_var, tag, count):
                pool.wait_ge(sg[tag + "_var"], count)
                pool.tensor_tensor(rs, mean_var[:, 1:2], neg_half[:, :], ALU.pow).then_inc(sg[tag + "_rstd"], 1)

            def norms(b):
                rsqrt(rstd[:, 0:1], mv[:, 0, :], "n1", b + 1)
                rsqrt(rstd[:, 1:2], mv[:, 1, :], "n2", b + 1)
                x1_out(b)

            def x2_norm(b):
                rsqrt(rstd2[:, :], mv2[:, :], "n3", b + 1)

            def normalise(b, s):
                pool.wait_ge(sg["c_rcp_ready"], PAIRS * b + s + 1)
                p = probs[:, s % 2]
                r = c_rcp[:, s % 2].unsqueeze(2).to_broadcast([N, 2, SK])
                pool.tensor_tensor(p, p, r, ALU.mult).then_inc(sg["p_normed"], 1)

            residual(0)
            stack_lo(0)
            norms(0)

            def iteration(b, more):
                for s in range(PAIRS):
                    if more and s == 0:
                        residual(b + 1)
                    normalise(b, s)
                    if more:
                        if s == 0:
                            stack_lo(b + 1)
                        if s == 6:
                            norms(b + 1)
                    if s == 2 and later(b):
                        x2_norm(b - 1)
            iterations(pool, iteration)
            x2_norm(B - 1)

        @block.scalar
        def _(act):
            def hi(dst, src):
                return act.activation(dst, src, ACT.Copy)

            def v_hi(b):
                if later(b):
                    act.wait_ge(sg["a_full"], fill_no("O1", b - 1))
                hi(v_self[0][:, :, :], v_all[:, :, bass.ds(2 * HD * b, 2 * HD)]).then_inc(sg["v_self_hi"], 1)

            def stack_hi(b):
                if later(b):
                    act.wait_ge(sg["a_full"], fill_no("T3", b - 1))
                for i in range(2):
                    for r in range(2):
                        dst = stack[:, i, :, r, 0:4:2, :] if i == 0 else stack[:, i, :, r, 0:2, :]
                        hi(dst.bitcast(F32R), qk_src(b, i, r)).then_inc(sg["qk_hi"], 1)

            def stacked_t(b):
                if later(b):
                    act.wait_ge(sg["a_full"], fill_no("S3", b - 1))
                for i, f in enumerate(("QA", "QB", "KA", "KB")):
                    act.wait_ge(sg["a_full"], fill_no(f, b))
                    dst = qk_t[i // 2][:, 4 * (i % 2):4 * (i % 2) + 4, :]
                    hi(dst.rearrange("p a n -> p (a n)"), bank(f)[:, 0:4 * N]).then_inc(sg["qk_stacked_t"], 1)

            def self_exp(b):
                for i in range(2):
                    act.wait_ge(sg["s_shifted"], 4 * b + 2 * i + 2)
                    e = e_self[:, 8 * i:8 * i + 8, :]
                    act.activation(e, e, ACT.Exp, scale=SELF_SCALE).then_inc(sg["e_ready"], 1)

            def self_pt(b, i):
                act.wait_ge(sg["a_full"], fill_no(f"T{i}", b))
                if i >= 2:
                    act.wait_ge(sg["a_full"], fill_no("O0", b))
                elif later(b):
                    act.wait_ge(sg["a_full"], fill_no("O1", b - 1))
                dst = pt[0][:, 4 * (i % 2):4 * (i % 2) + 4, :]
                hi(dst.rearrange("p a n -> p (a n)"), bank(f"T{i}")[0:N, 0:4 * N]).then_inc(sg["pt_hi"], 1)

            def ot_hi(b):
                act.wait_ge(sg["a_full"], fill_no("OT", b))
                hi(ot[0][:, :, :].rearrange("p k n -> p (k n)"), bank("OT")[:, 0:KD * N]).then_inc(sg["ot_hi"], 1)

            def ctx_hi(b):
                act.wait_ge(sg["padded"], 2)
                for k in range(KD):
                    act.wait_ge(sg["a_full"], fill_no(f"C{k}", b))
                    hi(ctxt[0][:, k, 0:SK], bank(f"C{k}")[:, 0:SK]).then_inc(sg["ctxt_hi"], 1)

            def xn_affine(b):
                act.wait_ge(sg["a_full"], fill_no("NT", b))
                if later(b):
                    act.wait_ge(sg["xnt_lo_ready"], b)
                for k in range(KD):
                    act.activation(xnt_f[:, k, :], bank("NT")[:, k * N:(k + 1) * N], ACT.Identity,
                                   bias=beta[:, k:k + 1], scale=gamma[:, k:k + 1]).then_inc(sg["xn_affine"], 1)

            def q_hi(b):
                for i in range(2):
                    act.wait_ge(sg["a_full"], fill_no(f"Q{i}", b))
                    if later(PAIRS * b):
                        act.wait_ge(sg["s_full"], PAIRS * b)
                    hi(qt[0][:, 4 * i:4 * i + 4, :].rearrange("p a n -> p (a n)"), bank(f"Q{i}")[:, 0:4 * N]).then_inc(sg["qt_hi"], 1)

            def k_hi(b, p):
                act.wait_ge(sg["kv_full"], kv_no(f"K{p}", b))
                if later(PAIRS * b + p - 1):
                    act.wait_ge(sg["s_full"], PAIRS * b + p - 1)
                hi(kt[0][:, p % 2, :], ps_kv[:, 0:SKP]).then_inc(sg["kt_hi"], 1)

            def v_hi_cross(b, f):
                q, t = int(f[1]), int(f[2])
                act.wait_ge(sg["kv_full"], kv_no(f, b))
                if later(PAIRS * (b - 1) + 4 * q + 4):
                    act.wait_ge(sg["pv_full"], PAIRS * (b - 1) + 4 * q + 4)
                hi(v[0][:, q, t, :], ps_kv[0:SKT, :]).then_inc(sg["v_hi"], 1)

            def exps(b, s):
                act.wait_ge(sg["c_neg_ready"], PAIRS * b + s + 1)
                if later(PAIRS * b + s - 1):
                    act.wait_ge(sg["t_full"], PAIRS * b + s - 1)
                for h in range(2):
                    act.activation(probs[:, s % 2, h, :], ps_s[0:N, h, 0:SK], ACT.Exp, bias=c_neg[:, s % 2, h:h + 1],
                                   scale=CROSS_SCALE, accum_out=c_sum[:, s % 2, h:h + 1]).then_inc(sg["c_exp"], 1)

            def cpt_hi(b, s):
                act.wait_ge(sg["t_full"], PAIRS * b + s + 1)
                if later(PAIRS * b + s):
                    act.wait_ge(sg["pv_full"], PAIRS * b + s)
                hi(cpt[0][:, :, :, :].rearrange("p h t n -> p h (t n)"), ps_t[0:SKT, :, 0:ST * N]).then_inc(sg["cpt_hi"], 1)

            def o_hi(b, s):
                act.wait_ge(sg["pv_full"], PAIRS * b + s + 1)
                if later(b):
                    act.wait_ge(sg["wo_full"], b)
                for h in range(2):
                    r = slice(64 * h, 64 * h + 64)
                    hi(oct_[0][r, s, :], ps_o[r, h * N:(h + 1) * N]).then_inc(sg["oct_hi"], 1)

            v_hi(0)
            stack_hi(0)
            stacked_t(0)
            self_exp(0)
            for i in range(4):
                self_pt(0, i)
            ctx_hi(0)
            ot_hi(0)
            k_hi(0, 0)
            v_hi_cross(0, "V00")
            xn_affine(0)
            k_hi(0, 1)
            v_hi_cross(0, "V01")
            q_hi(0)

            def iteration(b, more):
                for s in range(PAIRS):
                    exps(b, s)
                    if s + 2 < PAIRS:
                        k_hi(b, s + 2)
                    elif more:
                        if s == 7:
                            xn_affine(b + 1)
                        k_hi(b + 1, s + 2 - PAIRS)
                    if more:
                        if s == 0:
                            v_hi(b + 1)
                            stack_hi(b + 1)
                        if s == 1:
                            stacked_t(b + 1)
                        if s == 3:
                            self_exp(b + 1)
                            for i in range(4):
                                self_pt(b + 1, i)
                        if s == 5:
                            ctx_hi(b + 1)
                            ot_hi(b + 1)
                        if s == 7:
                            q_hi(b + 1)
                    if s in V_AT and (s < 6 or more):
                        v_hi_cross(b if s < 6 else b + 1, V_AT[s])
                    if s >= 2:
                        o_hi(b, s - 2)
                    elif later(b):
                        o_hi(b - 1, s + 6)
                    if s >= 1:
                        cpt_hi(b, s - 1)
                    elif later(b):
                        cpt_hi(b - 1, 7)
            iterations(act, iteration)
            o_hi(B - 1, 6)
            cpt_hi(B - 1, 7)
            o_hi(B - 1, 7)

        @block.vector
        def _(dve):
            def lo(dst, src, part):
                return dve.tensor_tensor(dst, src, part.bitcast(F32), ALU.subtract)

            def norm(src, dst, st, mean_var, rs, tag, count):
                dve.bn_stats(st, src).then_inc(sg[tag + "_stats"], 1)
                dve.wait_ge(sg[tag + "_stats"], count)
                dve.nop(nofuse=True)
                dve.bn_aggr(mean_var, st).then_inc(sg[tag + "_aggr"], 1)
                dve.wait_ge(sg[tag + "_aggr"], count)
                dve.tensor_scalar(mean_var[:, 1:2], mean_var[:, 1:2], EPS, None, ALU.add).then_inc(sg[tag + "_var"], 1)
                dve.wait_ge(sg[tag + "_rstd"], count)
                return dve.tensor_scalar(dst, src, mean_var[:, 0:1], rs, ALU.subtract, ALU.mult)

            def v_split(b):
                dve.wait_ge(sg["v_self_hi"], b + 1)
                lo(v_self[1][:, :, :], v_all[:, :, bass.ds(2 * HD * b, 2 * HD)], v_self[0][:, :, :]).then_inc(sg["v_self_lo"], 1)

            def self_max(b):
                for f in range(4):
                    src = bank(f"S{f}")[0:N, 0:4 * N].rearrange("p (a n) -> p a n", a=4)
                    dve.wait_ge(sg["a_full"], fill_no(f"S{f}", b))
                    dve.reduce_max(s_max[:, f, :], src, X).then_inc(sg["s_max_ready"], 1)
                    dve.wait_ge(sg["s_max_ready"], 4 * b + f + 1)
                    dve.tensor_tensor(e_self[:, 4 * f:4 * f + 4, :], src,
                                      s_max[:, f, :].unsqueeze(2).to_broadcast([N, 4, N]), ALU.subtract)\
                        .then_inc(sg["s_shifted"], 1)

            def self_sums(b):
                for i in range(2):
                    dve.wait_ge(sg["e_ready"], 2 * b + i + 1)
                    dve.reduce_sum(s_sum[:, 8 * i:8 * i + 8], e_self[:, 8 * i:8 * i + 8, :], X).then_inc(sg["s_sum_ready"], 1)
                dve.wait_ge(sg["s_sum_ready"], 2 * b + 2)
                dve.reciprocal(s_rcp[:, :], s_sum[:, :]).then_inc(sg["s_rcp_ready"], 1)

            def self_pt(b, i):
                dve.wait_ge(sg["pt_hi"], 4 * b + i + 1)
                dst = slice(4 * (i % 2), 4 * (i % 2) + 4)
                lo(pt[1][:, dst, :].rearrange("p a n -> p (a n)"), bank(f"T{i}")[0:N, 0:4 * N],
                   pt[0][:, dst, :].rearrange("p a n -> p (a n)")).then_inc(sg["pt_lo"], 1)

            def o_norm(b, i):
                dve.wait_ge(sg["a_full"], fill_no(f"O{i}", b))
                dve.wait_ge(sg["s_rcp_ready"], b + 1)
                if later(16 * b):
                    dve.wait_ge(sg["o_stored"], 16 * b)
                out = o_self[:, :, :].rearrange("p (r b) w -> p r b w", r=2)[:, :, 4 * i:4 * i + 4, :]
                rcp = s_rcp[:, 8 * i:8 * i + 8].rearrange("p (r b) -> p r b", r=2).unsqueeze(3)
                dve.tensor_tensor(out, bank(f"O{i}")[0:N, 0:128].rearrange("p (r b w) -> p r b w", r=2, w=HD),
                                  rcp.to_broadcast([N, 2, 4, HD]), ALU.mult).then_inc(sg["o_normed"], 1)

            def ot_lo(b):
                dve.wait_ge(sg["ot_hi"], b + 1)
                lo(ot[1][:, :, :].rearrange("p k n -> p (k n)"), bank("OT")[:, 0:KD * N],
                   ot[0][:, :, :].rearrange("p k n -> p (k n)")).then_inc(sg["ot_lo"], 1)

            def ctx_lo(b):
                dve.wait_ge(sg["padded"], 2)
                for k in range(KD):
                    dve.wait_ge(sg["ctxt_hi"], 2 * b + k + 1)
                    lo(ctxt[1][:, k, 0:SK], bank(f"C{k}")[:, 0:SK], ctxt[0][:, k, 0:SK]).then_inc(sg["ctxt_lo"], 1)

            def norms(b):
                dve.wait_ge(sg["a_full"], fill_no("PJ", b))
                dve.wait_ge(sg["x_res_ready"], b + 1)
                dve.tensor_tensor(res[:, :], bank("PJ")[0:N, 0:D], x_res[:, :], ALU.add).then_inc(sg["res1"], 1)
                dve.wait_ge(sg["res1"], b + 1)
                if later(b):
                    dve.wait_ge(sg["x1_kept"], b)
                norm(res[:, :], x1[:, :], stats[:, 0, :], mv[:, 0, :], rstd[:, 0:1], "n1", b + 1).then_inc(sg["x1_ready"], 1)
                dve.wait_ge(sg["x1_ready"], b + 1)
                if later(b):
                    dve.wait_ge(sg["a_full"], fill_no("NT", b - 1))
                norm(x1[:, :], xn[:, :], stats[:, 1, :], mv[:, 1, :], rstd[:, 1:2], "n2", b + 1).then_inc(sg["xn_ready"], 1)

            def xnt_split(b):
                dve.wait_ge(sg["xn_affine"], 2 * b + 2)
                if later(b):
                    dve.wait_ge(sg["a_full"], fill_no("Q1", b - 1))
                dve.tensor_copy(xnt[0][:, :, :], xnt_f[:, :, :]).then_inc(sg["xnt_hi_ready"], 1)
                dve.wait_ge(sg["xnt_hi_ready"], b + 1)
                lo(xnt[1][:, :, :], xnt_f[:, :, :], xnt[0][:, :, :]).then_inc(sg["xnt_lo_ready"], 1)

            def q_lo(b):
                for i in range(2):
                    dve.wait_ge(sg["qt_hi"], 2 * b + i + 1)
                    sl = slice(4 * i, 4 * i + 4)
                    lo(qt[1][:, sl, :].rearrange("p a n -> p (a n)"), bank(f"Q{i}")[:, 0:4 * N],
                       qt[0][:, sl, :].rearrange("p a n -> p (a n)")).then_inc(sg["qt_lo"], 1)

            def k_lo(b, p):
                dve.wait_ge(sg["kt_hi"], PAIRS * b + p + 1)
                lo(kt[1][:, p % 2, :], ps_kv[:, 0:SKP], kt[0][:, p % 2, :]).then_inc(sg["kt_lo"], 1)

            def v_lo_cross(b, f):
                q, t = int(f[1]), int(f[2])
                dve.wait_ge(sg["v_hi"], kv_reads(b, f, "V"))
                lo(v[1][:, q, t, :], ps_kv[0:SKT, :], v[0][:, q, t, :]).then_inc(sg["v_lo"], 1)

            def maxima(b, s):
                dve.wait_ge(sg["s_full"], PAIRS * b + s + 1)
                dve.reduce_max(c_max[:, s % 2, :], ps_s[0:N, :, 0:SK], X).then_inc(sg["c_max_ready"], 1)
                dve.wait_ge(sg["c_max_ready"], PAIRS * b + s + 1)
                dve.tensor_scalar(c_neg[:, s % 2, :], c_max[:, s % 2, :], -CROSS_SCALE, None, ALU.mult)\
                    .then_inc(sg["c_neg_ready"], 1)

            def rcp(b, s):
                dve.wait_ge(sg["c_exp"], 2 * (PAIRS * b + s) + 2)
                if later(PAIRS * b + s - 1):
                    dve.wait_ge(sg["p_normed"], PAIRS * b + s - 1)
                dve.reciprocal(c_rcp[:, s % 2, :], c_sum[:, s % 2, :]).then_inc(sg["c_rcp_ready"], 1)

            def cpt_lo(b, s):
                dve.wait_ge(sg["cpt_hi"], PAIRS * b + s + 1)
                dve.tensor_tensor(cpt[1][:, :, :, :].rearrange("p h t n -> p h (t n)"), ps_t[0:SKT, :, 0:ST * N],
                                  cpt[0][:, :, :, :].rearrange("p h t n -> p h (t n)").bitcast(F32), ALU.subtract)\
                    .then_inc(sg["cpt_lo"], 1)

            def o_lo(b, s):
                for h in range(2):
                    dve.wait_ge(sg["oct_hi"], 2 * (PAIRS * b + s) + h + 1)
                    r = slice(64 * h, 64 * h + 64)
                    lo(oct_[1][r, s, :], ps_o[r, h * N:(h + 1) * N], oct_[0][r, s, :]).then_inc(sg["oct_lo"], 1)

            def x2_norm(b):
                dve.wait_ge(sg["wo_full"], b + 1)
                dve.wait_ge(sg["x1_kept"], b + 1)
                dve.scalar_tensor_tensor(res2[:, :], ps_o[0:N, 0:D], gate[:, 0:1], x2_all[0:N, b, :],
                                         op0=ALU.mult, op1=ALU.add).then_inc(sg["res2"], 1)
                dve.wait_ge(sg["res2"], b + 1)
                norm(res2[:, :], x2_all[0:N, b, :], stats2[:, :], mv2[:, :], rstd2[:, :], "n3", b + 1).then_inc(sg["x2_ready"], 1)

            v_split(0)
            self_max(0)
            self_sums(0)
            self_pt(0, 0)
            self_pt(0, 1)
            o_norm(0, 0)
            self_pt(0, 2)
            self_pt(0, 3)
            o_norm(0, 1)
            ctx_lo(0)
            ot_lo(0)
            k_lo(0, 0)
            v_lo_cross(0, "V00")
            norms(0)
            xnt_split(0)
            k_lo(0, 1)
            v_lo_cross(0, "V01")
            q_lo(0)

            def iteration(b, more):
                for s in range(PAIRS):
                    maxima(b, s)
                    if s + 2 < PAIRS:
                        k_lo(b, s + 2)
                    elif more:
                        if s == 7:
                            xnt_split(b + 1)
                        k_lo(b + 1, s + 2 - PAIRS)
                    rcp(b, s)
                    if more:
                        if s == 0:
                            v_split(b + 1)
                        if s == 2:
                            self_max(b + 1)
                        if s == 3:
                            self_sums(b + 1)
                            self_pt(b + 1, 0)
                            self_pt(b + 1, 1)
                            o_norm(b + 1, 0)
                            self_pt(b + 1, 2)
                            self_pt(b + 1, 3)
                            o_norm(b + 1, 1)
                        if s == 5:
                            ctx_lo(b + 1)
                            ot_lo(b + 1)
                        if s == 6:
                            norms(b + 1)
                        if s == 7:
                            q_lo(b + 1)
                    if s in V_AT and (s < 6 or more):
                        v_lo_cross(b if s < 6 else b + 1, V_AT[s])
                    if s == 2 and later(b):
                        x2_norm(b - 1)
                    if s >= 2:
                        o_lo(b, s - 2)
                    elif later(b):
                        o_lo(b - 1, s + 6)
                    if s >= 1:
                        cpt_lo(b, s - 1)
                    elif later(b):
                        cpt_lo(b - 1, 7)
            iterations(dve, iteration)
            o_lo(B - 1, 6)
            cpt_lo(B - 1, 7)
            o_lo(B - 1, 7)
            x2_norm(B - 1)
            dve.wait_ge(sg["x2_ready"], B)

        @block.tensor
        def _(pe):
            def free(name, b):
                i = FILLS.index(name)
                if i >= 2:
                    signal, per, which = LAST_READ[FILLS[i - 2]]
                    pe.wait_ge(sg[signal], per * b + which + 1)
                else:
                    last = [f for j, f in enumerate(FILLS) if j % 2 == i][-1]
                    signal, per, which = LAST_READ[last]
                    if later(b):
                        pe.wait_ge(sg[signal], per * (b - 1) + which + 1)

            def stacked_transpose(b):
                for i, f in enumerate(("QA", "QB", "KA", "KB")):
                    pe.wait_ge(sg["qk_lo"], 4 * b + 2 * (i // 2) + 2)
                    free(f, b)
                    for j in range(4):
                        c = (i // 2) * 1024 + (4 * (i % 2) + j) * P
                        last = pe.transpose(bank(f)[:, j * N:(j + 1) * N], work[0:N, c:c + P], ident[0:N, 0:N])
                    last.then_inc(sg["a_full"], 1)

            def self_scores(b):
                for f in range(4):
                    pe.wait_ge(sg["qk_stacked_t"], 4 * b + 4)
                    free(f"S{f}", b)
                    r = slice(64 * (f % 2), 64 * (f % 2) + 64)
                    for j in range(4):
                        pr = 4 * (f // 2) + j
                        last = pe.matmul(bank(f"S{f}")[0:N, j * N:(j + 1) * N], qk_t[0][r, pr, :], qk_t[1][r, pr, :],
                                         start=True, stop=True)
                    last.then_inc(sg["a_full"], 1)

            def self_pt(b, i):
                pe.wait_ge(sg["e_ready"], 2 * b + i // 2 + 1)
                free(f"T{i}", b)
                for j in range(4):
                    last = pe.transpose(bank(f"T{i}")[0:N, j * N:(j + 1) * N], e_self[:, 4 * i + j, :], ident[0:N, 0:N])
                last.then_inc(sg["a_full"], 1)

            def self_out(b, i):
                pe.wait_ge(sg["pt_lo"], 4 * b + 2 * i + 2)
                pe.wait_ge(sg["v_self_lo"], b + 1)
                free(f"O{i}", b)
                for j in range(8):
                    bb, r = 4 * i + j % 4, j // 4
                    last = product(pe, bank(f"O{i}")[0:N, j * HD:(j + 1) * HD], tuple(t[:, j, :] for t in pt),
                                   tuple(t[:, bb, r * HD:(r + 1) * HD] for t in v_self))
                last.then_inc(sg["a_full"], 1)

            def o_transpose(b):
                pe.wait_ge(sg["o_rows_loaded"], 16 * (b + 1))
                free("OT", b)
                for k in range(KD):
                    last = pe.transpose(bank("OT")[:, k * N:(k + 1) * N], o_rows[:, k * P:(k + 1) * P], ident[0:N, 0:N])
                last.then_inc(sg["a_full"], 1)

            def ctx_transpose(b):
                pe.wait_ge(sg["ctx_loaded"], 16 * (b + 1))
                for k in range(KD):
                    free(f"C{k}", b)
                    for t in range(ST):
                        last = pe.transpose(bank(f"C{k}")[:, t * SKT:(t + 1) * SKT], ctx_raw[:, t, k * P:(k + 1) * P],
                                            ident[0:SKT, 0:SKT])
                    last.then_inc(sg["a_full"], 1)

            def out_project(b):
                pe.wait_ge(sg["ot_lo"], b + 1)
                free("PJ", b)
                product_over_width(pe, bank("PJ")[0:N, 0:D], ot, w_proj, slice(0, D)).then_inc(sg["a_full"], 1)

            def xn_transpose(b):
                pe.wait_ge(sg["xn_ready"], b + 1)
                free("NT", b)
                for k in range(KD):
                    last = pe.transpose(bank("NT")[:, k * N:(k + 1) * N], xn[:, k * P:(k + 1) * P], ident[0:N, 0:N])
                last.then_inc(sg["a_full"], 1)

            def q_project(b):
                pe.wait_ge(sg["xnt_lo_ready"], b + 1)
                for i in range(2):
                    free(f"Q{i}", b)
                    for j in range(4):
                        m = slice((4 * i + j) * P, (4 * i + j + 1) * P)
                        for k in range(KD):
                            last = product(pe, bank(f"Q{i}")[:, j * N:(j + 1) * N], tuple(t[:, k, m] for t in w_q),
                                           tuple(t[:, k, :] for t in xnt), start=k == 0, stop=k == KD - 1)
                    last.then_inc(sg["a_full"], 1)

            def kv_free(f, b):
                i = KV_FILLS.index(f)
                prev, pb = (KV_FILLS[i - 1], b) if i else (KV_FILLS[-1], b - 1)
                if isinstance(pb, int) and pb < 0:
                    return
                pe.wait_ge(sg["kt_lo" if prev[0] == "K" else "v_lo"], kv_reads(pb, prev, prev[0]))

            def k_project(b, p):
                pe.wait_ge(sg["ctxt_lo"], 2 * b + 2)
                kv_free(f"K{p}", b)
                m = slice(p * P, (p + 1) * P)
                for k in range(KD):
                    last = product(pe, ps_kv[:, 0:SKP], tuple(t[:, k, m] for t in w_k), tuple(t[:, k, :] for t in ctxt),
                                   start=k == 0, stop=k == KD - 1)
                last.then_inc(sg["kv_full"], 1)

            def v_project(b, f):
                q, t = int(f[1]), int(f[2])
                kv_free(f, b)
                rows = slice(t * SKT, (t + 1) * SKT)
                for k in range(KD):
                    last = product(pe, ps_kv[0:SKT, :], tuple(c[:, k, rows] for c in ctxt),
                                   tuple(w[:, k, 512 * q:512 * q + 512] for w in w_v), start=k == 0, stop=k == KD - 1)
                last.then_inc(sg["kv_full"], 1)

            def scores(b, s):
                pe.wait_ge(sg["qt_lo"], 2 * b + 2)
                pe.wait_ge(sg["kt_lo"], PAIRS * b + s + 1)
                if later(2 * (PAIRS * b + s)):
                    pe.wait_ge(sg["c_exp"], 2 * (PAIRS * b + s))
                for h in range(2):
                    r = slice(64 * h, 64 * h + 64)
                    last = product(pe, ps_s[0:N, h, 0:SKP], tuple(t[r, s, :] for t in qt),
                                   tuple(t[r, s % 2, :] for t in kt))
                last.then_inc(sg["s_full"], 1)

            def p_transpose(b, s):
                pe.wait_ge(sg["p_normed"], PAIRS * b + s + 1)
                if later(PAIRS * b + s):
                    pe.wait_ge(sg["cpt_lo"], PAIRS * b + s)
                for h in range(2):
                    for t in range(ST):
                        last = pe.transpose(ps_t[0:SKT, h, t * N:(t + 1) * N],
                                            probs[:, s % 2, h, t * SKT:(t + 1) * SKT], ident[0:N, 0:N])
                last.then_inc(sg["t_full"], 1)

            def pv(b, s):
                pe.wait_ge(sg["cpt_lo"], PAIRS * b + s + 1)
                pe.wait_ge(sg["v_lo"], kv_reads(b, "V02" if s < 4 else "V12", "V"))
                if s:
                    pe.wait_ge(sg["oct_lo"], 2 * (PAIRS * b + s))
                else:
                    if later(b):
                        pe.wait_ge(sg["res2"], b)
                c = slice((s % 4) * P, (s % 4 + 1) * P)
                for t in range(ST):
                    last = product(pe, ps_o[:, 0:2 * N], tuple(w[:, s // 4, t, c] for w in v),
                                   tuple(w[:, :, t, :] for w in cpt), start=t == 0, stop=t == ST - 1)
                last.then_inc(sg["pv_full"], 1)

            def cross_out(b):
                pe.wait_ge(sg["oct_lo"], 2 * PAIRS * (b + 1))
                for k in range(PAIRS):
                    last = product(pe, ps_o[0:N, 0:D], tuple(t[:, k, :] for t in oct_), tuple(t[:, k, :] for t in w_o),
                                   start=k == 0, stop=k == PAIRS - 1)
                last.then_inc(sg["wo_full"], 1)

            stacked_transpose(0)
            self_scores(0)
            self_pt(0, 0)
            self_pt(0, 1)
            self_out(0, 0)
            self_pt(0, 2)
            self_pt(0, 3)
            self_out(0, 1)
            ctx_transpose(0)
            o_transpose(0)
            out_project(0)
            k_project(0, 0)
            v_project(0, "V00")
            xn_transpose(0)
            k_project(0, 1)
            v_project(0, "V01")
            q_project(0)

            def iteration(b, more):
                for s in range(PAIRS):
                    scores(b, s)
                    if more and s == 7:
                        xn_transpose(b + 1)
                    if s + 2 < PAIRS:
                        k_project(b, s + 2)
                    elif more:
                        k_project(b + 1, s + 2 - PAIRS)
                    if more:
                        if s == 1:
                            stacked_transpose(b + 1)
                        if s == 2:
                            self_scores(b + 1)
                        if s == 3:
                            self_pt(b + 1, 0)
                            self_pt(b + 1, 1)
                            self_out(b + 1, 0)
                            self_pt(b + 1, 2)
                            self_pt(b + 1, 3)
                            self_out(b + 1, 1)
                        if s == 5:
                            ctx_transpose(b + 1)
                            o_transpose(b + 1)
                        if s == 6:
                            out_project(b + 1)
                        if s == 7:
                            q_project(b + 1)
                    if s in V_AT and (s < 6 or more):
                        v_project(b if s < 6 else b + 1, V_AT[s])
                    if s == 2 and later(b):
                        cross_out(b - 1)
                    if s >= 2:
                        pv(b, s - 2)
                    elif later(b):
                        pv(b - 1, s + 6)
                    if s >= 1:
                        p_transpose(b, s - 1)
                    elif later(b):
                        p_transpose(b - 1, 7)
            iterations(pe, iteration)
            pv(B - 1, 6)
            p_transpose(B - 1, 7)
            pv(B - 1, 7)
            cross_out(B - 1)


def ffn_block(nc, sg, A, x2_all, ident, out):
    UNITS = 2 * MH
    with ExitStack() as ctx:
        def sb(name, shape, dt=F32):
            return ctx.enter_context(nc.sbuf_tensor(name, shape, dt))

        def pair(name, shape):
            return split_pair(nc, ctx, name, shape)


        raw = sb("ffn_raw", [P, MH, 6, P])
        w = pair("ffn_w", [P, MH, 6, P])
        x2t = pair("x2t", [P, KD, TOK])
        gw_raw = sb("gw_raw", [P, KD, EXP])
        gw = pair("gw", [P, KD, EXP])
        logits = sb("logits", [N, B, EXP])
        top = sb("top", [N, B, 8])
        top_i = sb("top_i", [N, B, 8], U32)
        top_f = sb("top_f", [N, B, 2])
        gap = sb("gap", [N, B])
        gap_e = sb("gap_e", [N, B])
        w_top = sb("w_top", [N, 2, B])
        eid = sb("eid", [N, EXP])
        pick = sb("pick", [N, 2, B, EXP])
        w_tok = sb("w_tok", [N, B, EXP])
        w_bc = sb("w_bc", [P, EXP, TOK])
        s_act = sb("s_act", [P, 2, HALF])
        g = sb("g", [P, 2, HALF])
        gs = pair("gs", [P, 2, HALF])
        y_sb = sb("y_sb", [P, KD, TOK])
        res = sb("ffn_res", [N, B, D])
        stats = sb("ffn_stats", [N, B, 6])
        mv = sb("ffn_mv", [N, B, 2])
        rstd = sb("ffn_rstd", [N, B])
        var = sb("ffn_var", [N, B])
        neg_half = sb("ffn_neg_half", [N, B])
        y_out = sb("y_out", [N, B, D])

        ps_y = ctx.enter_context(nc.psum_tensor("ps_y", [P, 4, 512], F32))
        ps_h = ctx.enter_context(nc.psum_tensor("ps_h", [P, 4, 512], F32))
        block = ctx.enter_context(nc.Block())

        def half(i):
            return slice(i * HALF, (i + 1) * HALF)

        @block.sync
        def _(sp):
            def load(w1, w2, w3):
                for i, src in ((0, w1), (2, w2)):
                    for k in range(KD):
                        sp.dma_start(raw[:, :, i + k, :], src[k * P:(k + 1) * P, :].rearrange("p (m c) -> p m c", m=MH))\
                            .then_inc(sg["raw_loaded"], 16)
                sp.dma_start(raw[:, :, 4:6, :].rearrange("p m o c -> p m (o c)"),
                             w3.rearrange("(m p) d -> p m d", p=P)).then_inc(sg["raw_loaded"], 16)

            sp.dma_start(gw_raw[:, :, :], A["gate_w"].rearrange("(k p) e -> p k e", p=P)).then_inc(sg["gw_loaded"], 16)
            load(A["sw1"], A["sw2"], A["sw3"])

            def expert_load(e):
                sp.wait_ge(sg["w_lo"], MH * e)
                load(*(A[n][bass.ds(e - 1, 1)].rearrange("a d h -> (a d) h") for n in ("ew1", "ew2", "ew3")))
            with sp.Fori(1, EXP + 1) as e:
                expert_load(e)
            for b in range(B):
                sp.wait_ge(sg["y_ready"], b + 1)
                sp.dma_start(out[b], y_out[:, b, :]).then_inc(sg["stored"], 16)
            sp.wait_ge(sg["stored"], 16 * B)

        def split_at(j):
            return {0: (0, 2), 2: (0, 3), 4: (1, 0), 6: (1, 1)}.get(j)

        def unit_no(e, j):
            return UNITS * e + j

        def w_split_free(eng, e, m):
            eng.wait_ge(sg["down_done"], unit_no(e - 1, 2 * m + 1) + 1)

        @block.gpsimd
        def _(pool):
            pool.iota(top_i[:, 0, :], [[1, EXP]], base=0, channel_multiplier=0).then_inc(sg["iota"], 1)
            pool.wait_ge(sg["iota"], 1)
            pool.memset(neg_half[:, :], -0.5).then_inc(sg["iota"], 1)
            pool.wait_ge(sg["iota"], 2)
            pool.tensor_copy(eid[:, :], top_i[:, 0, :]).then_inc(sg["eid_ready"], 1)

            def unit(e, j):
                u = unit_no(e, j)
                if later(e):
                    pool.wait_ge(sg["g_ready"], u + 1)
                    pool.wait_ge(sg["w_bc_ready"], 2 * EXP)
                    pool.nop(nofuse=True)
                    pool.tensor_tensor(g[:, j % 2, :], g[:, j % 2, :], w_bc[:, e - 1, half(j % 2)], ALU.mult)\
                        .then_inc(sg["g_weighted"], 1)
                pool.wait_ge(sg["g_hi"], u + 1)
                pool.tensor_tensor(gs[1][:, j % 2, :], g[:, j % 2, :], gs[0][:, j % 2, :].bitcast(F32), ALU.subtract)\
                    .then_inc(sg["g_lo"], 1)

            def expert(e):
                for j in range(UNITS):
                    unit(e, j)
            expert(0)
            with pool.Fori(1, EXP + 1) as e:
                expert(e)
            pool.wait_ge(sg["y_var"], 1)
            pool.tensor_tensor(rstd[:, :], var[:, :], neg_half[:, :], ALU.pow).then_inc(sg["y_rstd"], 1)

        @block.scalar
        def _(act):
            def hi(dst, src):
                return act.activation(dst, src, ACT.Copy)

            for i in range(4):
                k, hf = i // 2, i % 2
                act.wait_ge(sg["x2t_full"], i + 1)
                hi(x2t[0][:, k, half(hf)], ps_h[:, i, 0:HALF]).then_inc(sg["x2t_hi"], 1)
            act.wait_ge(sg["gw_loaded"], 16)
            hi(gw[0][:, :, :], gw_raw[:, :, :]).then_inc(sg["gw_hi"], 1)
            act.wait_ge(sg["raw_loaded"], 80)
            for m in range(MH):
                hi(w[0][:, m], raw[:, m]).then_inc(sg["w_hi"], 1)
            act.wait_ge(sg["gap_ready"], 1)
            act.activation(gap_e[:, :], gap[:, :], ACT.Exp).then_inc(sg["gap_exp"], 1)

            def unit(e, j, more):
                u = unit_no(e, j)
                act.wait_ge(sg["h_full"], u + 1)
                if later(u - 1):
                    act.wait_ge(sg["g_ready"], u - 1)
                act.activation(s_act[:, j % 2, :], ps_h[:, 2 * (j % 2), 0:HALF], ACT.Silu).then_inc(sg["silu"], 1)
                sp = split_at(j)
                if sp and (sp[0] == 0 or more) and (sp[0] == 1 or later(e)):
                    en, m = e + sp[0], sp[1]
                    act.wait_ge(sg["raw_loaded"], 80 * (en + 1))
                    w_split_free(act, en, m)
                    hi(w[0][:, m], raw[:, m]).then_inc(sg["w_hi"], 1)
                if later(e):
                    act.wait_ge(sg["g_weighted"], unit_no(e - 1, j) + 1)
                else:
                    act.wait_ge(sg["g_ready"], u + 1)
                if later(u - 1):
                    act.wait_ge(sg["down_done"], u - 1)
                hi(gs[0][:, j % 2, :], g[:, j % 2, :]).then_inc(sg["g_hi"], 1)

            def expert(e, more=True):
                for j in range(UNITS):
                    unit(e, j, more)
            expert(0)
            for f in range(EXP * 2):
                act.wait_ge(sg["wt_full"], f + 1)
                act.activation(w_bc[:, f // 2, half(f % 2)], ps_h[:, f % 4, 0:HALF], ACT.Copy).then_inc(sg["w_bc_ready"], 1)
            with act.Fori(1, EXP) as e:
                expert(e)
            expert(EXP, False)
            for i in range(4):
                act.wait_ge(sg["y_done"], 1)
                act.activation(y_sb[:, i // 2, half(i % 2)], ps_y[:, i, 0:HALF], ACT.Copy).then_inc(sg["y_copied"], 1)

        @block.vector
        def _(dve):
            def lo(dst, src, part):
                return dve.tensor_tensor(dst, src, part.bitcast(F32), ALU.subtract)

            for i in range(4):
                k, hf = i // 2, i % 2
                dve.wait_ge(sg["x2t_hi"], i + 1)
                lo(x2t[1][:, k, half(hf)], ps_h[:, i, 0:HALF], x2t[0][:, k, half(hf)]).then_inc(sg["x2t_lo"], 1)
            dve.wait_ge(sg["gw_hi"], 1)
            lo(gw[1][:, :, :], gw_raw[:, :, :], gw[0][:, :, :]).then_inc(sg["gw_lo"], 1)
            for m in range(MH):
                dve.wait_ge(sg["w_hi"], m + 1)
                lo(w[1][:, m], raw[:, m], w[0][:, m]).then_inc(sg["w_lo"], 1)

            dve.wait_ge(sg["eid_ready"], 1)
            dve.wait_ge(sg["logits_full"], 1)
            dve.tensor_copy(logits[:, :, :].rearrange("p b e -> p (b e)"), ps_y[0:N, 0, 0:B * EXP]).then_inc(sg["gating"], 1)
            dve.wait_ge(sg["gating"], 1)
            for b in range(B):
                dve.max(top[:, b, :], logits[:, b, :]).then_inc(sg["top_ready"], 1)
                dve.wait_ge(sg["top_ready"], b + 1)
                dve.max_index(top_i[:, b, :], top[:, b, :], logits[:, b, :]).then_inc(sg["gating"], 1)
            dve.wait_ge(sg["gating"], 1 + B)
            dve.tensor_copy(top_f[:, :, :], top_i[:, :, 0:2]).then_inc(sg["gating"], 1)
            dve.tensor_tensor(gap[:, :], top[:, :, 1], top[:, :, 0], ALU.subtract).then_inc(sg["gap_ready"], 1)
            dve.wait_ge(sg["gap_exp"], 1)
            dve.tensor_scalar(w_top[:, 0, :], gap_e[:, :], 1.0, None, ALU.add).then_inc(sg["gating"], 1)
            dve.wait_ge(sg["gating"], 3 + B)
            dve.reciprocal(w_top[:, 0, :], w_top[:, 0, :]).then_inc(sg["gating"], 1)
            dve.wait_ge(sg["gating"], 4 + B)
            dve.tensor_tensor(w_top[:, 1, :], w_top[:, 0, :], gap_e[:, :], ALU.mult).then_inc(sg["gating"], 1)
            for c in range(2):
                dve.tensor_tensor(pick[:, c], eid[:, :].unsqueeze(1).to_broadcast([N, B, EXP]),
                                  top_f[:, :, c].unsqueeze(2).to_broadcast([N, B, EXP]), ALU.is_equal)\
                    .then_inc(sg["gating"], 1)
            dve.wait_ge(sg["gating"], 7 + B)
            for c in range(2):
                dve.tensor_tensor(pick[:, c], pick[:, c], w_top[:, c, :].unsqueeze(2).to_broadcast([N, B, EXP]), ALU.mult)\
                    .then_inc(sg["gating"], 1)
            dve.wait_ge(sg["gating"], 9 + B)
            dve.tensor_tensor(w_tok[:, :, :], pick[:, 0], pick[:, 1], ALU.add).then_inc(sg["w_tok_ready"], 1)

            def unit(e, j, more):
                u = unit_no(e, j)
                dve.wait_ge(sg["silu"], u + 1)
                if later(u - 1):
                    dve.wait_ge(sg["g_lo"], u - 1)
                dve.tensor_tensor(g[:, j % 2, :], s_act[:, j % 2, :], ps_h[:, 2 * (j % 2) + 1, 0:HALF], ALU.mult)\
                    .then_inc(sg["g_ready"], 1)
                sp = split_at(j)
                if sp and (sp[0] == 0 or more) and (sp[0] == 1 or later(e)):
                    en, m = e + sp[0], sp[1]
                    dve.wait_ge(sg["w_hi"], MH * en + m + 1)
                    lo(w[1][:, m], raw[:, m], w[0][:, m]).then_inc(sg["w_lo"], 1)

            def expert(e, more=True):
                for j in range(UNITS):
                    unit(e, j, more)
            expert(0)
            with dve.Fori(1, EXP) as e:
                expert(e)
            expert(EXP, False)

            for b in range(B):
                dve.wait_ge(sg["yt_full"], b + 1)
                dve.tensor_tensor(res[:, b, :], ps_h[0:N, b % 4, 0:D], x2_all[0:N, b, :], ALU.add).then_inc(sg["y_res"], 1)
                dve.wait_ge(sg["y_res"], b + 1)
                dve.bn_stats(stats[:, b, :], res[:, b, :]).then_inc(sg["y_stats"], 1)
            for b in range(B):
                dve.wait_ge(sg["y_stats"], b + 1)
                dve.bn_aggr(mv[:, b, :], stats[:, b, :]).then_inc(sg["y_aggr"], 1)
            dve.wait_ge(sg["y_aggr"], B)
            dve.tensor_scalar(var[:, :], mv[:, :, 1], EPS, None, ALU.add).then_inc(sg["y_var"], 1)
            dve.wait_ge(sg["y_rstd"], 1)
            for b in range(B):
                dve.tensor_scalar(y_out[:, b, :], res[:, b, :], mv[:, b, 0:1], rstd[:, b:b + 1], ALU.subtract, ALU.mult)\
                    .then_inc(sg["y_ready"], 1)

        @block.tensor
        def _(pe):
            for i in range(4):
                k, hf = i // 2, i % 2
                for j in range(4):
                    last = pe.transpose(ps_h[:, i, j * N:(j + 1) * N], x2_all[0:N, 4 * hf + j, k * P:(k + 1) * P],
                                        ident[0:N, 0:N])
                last.then_inc(sg["x2t_full"], 1)
            pe.wait_ge(sg["x2t_lo"], 4)
            pe.wait_ge(sg["gw_lo"], 1)
            for b in range(B):
                t = slice(b * N, (b + 1) * N)
                for k in range(KD):
                    last = product(pe, ps_y[0:N, 0, b * EXP:(b + 1) * EXP], tuple(c[:, k, t] for c in x2t),
                                   tuple(c[:, k, :] for c in gw), start=k == 0, stop=k == KD - 1)
            last.then_inc(sg["logits_full"], 1)

            def up(e, j):
                u, m = unit_no(e, j), j // 2
                pe.wait_ge(sg["w_lo"], MH * e + m + 1)
                if later(u - 1):
                    pe.wait_ge(sg["g_ready"], u - 1)
                for i in range(2):
                    for k in range(KD):
                        last = product(pe, ps_h[:, 2 * (j % 2) + i, 0:HALF], tuple(c[:, m, 2 * i + k, :] for c in w),
                                       tuple(c[:, k, half(j % 2)] for c in x2t), start=k == 0, stop=k == KD - 1)
                last.then_inc(sg["h_full"], 1)

            def down(e, j, first=False, final=False):
                u, m = unit_no(e, j), j // 2
                pe.wait_ge(sg["g_lo"], u + 1)
                if first:
                    pe.wait_ge(sg["gating"], 1)
                for o in range(2):
                    last = product(pe, ps_y[:, 2 * o + j % 2, 0:HALF], tuple(c[:, m, 4 + o, :] for c in w),
                                   tuple(c[:, j % 2, :] for c in gs), start=first, stop=final, skip_group_check=True)
                last.then_inc(sg["down_done"], 1)

            def expert(e):
                for j in range(UNITS):
                    up(e, j)
                    if j >= 2:
                        down(e, j - 2, first=isinstance(e, int) and e == 0 and j < 4)
                    elif later(e - 1):
                        down(e - 1, j + UNITS - 2)

            expert(0)
            down(0, UNITS - 2)
            down(0, UNITS - 1)
            pe.wait_ge(sg["w_tok_ready"], 1)
            pe.wait_ge(sg["g_ready"], UNITS)
            for f in range(EXP * 2):
                if later(f - 3):
                    pe.wait_ge(sg["w_bc_ready"], f - 3)
                for i in range(4):
                    b = 4 * (f % 2) + i
                    last = pe.transpose(ps_h[:, f % 4, i * N:(i + 1) * N],
                                        w_tok[:, b, f // 2:f // 2 + 1].to_broadcast([N, P]), ident[0:N, 0:N])
                last.then_inc(sg["wt_full"], 1)
            pe.wait_ge(sg["w_bc_ready"], 2 * EXP)
            expert(1)
            with pe.Fori(2, EXP + 1) as e:
                expert(e)
            for j in (UNITS - 2, UNITS - 1):
                down(EXP, j, final=True)
            pe.wait_ge(sg["down_done"], UNITS * (EXP + 1))
            pe.transpose(ps_h[0:N, 3, 0:N], ident[0:N, 0:N], ident[0:N, 0:N]).then_inc(sg["y_done"], 1)
            pe.wait_ge(sg["y_copied"], 4)
            for b in range(B):
                if later(b - 3):
                    pe.wait_ge(sg["y_res"], b - 3)
                for k in range(KD):
                    last = pe.transpose(ps_h[0:N, b % 4, k * P:(k + 1) * P], y_sb[:, k, b * N:(b + 1) * N], ident[:, :])
                last.then_inc(sg["yt_full"], 1)


def decoder_layer(nc, A, out):
    with ExitStack() as outer:
        x2_all = outer.enter_context(nc.sbuf_tensor("x2_all", [P, B, D], F32))
        ident = outer.enter_context(nc.sbuf_tensor("ident", [P, P], F32))
        signals = [Signals(nc, outer, block) for block in ("prep", "attn", "ffn")]
        with ExitStack() as ctx:
            consts = {n: ctx.enter_context(nc.sbuf_tensor("const_" + n, shape, F32)) for n, shape in
                      (("proj_b", [N, D]), ("b_out", [N, D]), ("gate", [N, 1]), ("neg_half", [N, 1]),
                       ("gamma", [P, KD]), ("beta", [P, KD]))}
            weights = [split_pair(nc, ctx, name, shape) for name, shape in
                       (("w_k", [P, KD, INNER]), ("w_v", [P, KD, INNER]), ("w_q", [P, KD, INNER]),
                        ("w_o", [P, PAIRS, D]), ("w_proj", [P, KD, D]))]
            qk_rot = ctx.enter_context(nc.sbuf_tensor("qk_rot", [N, B, 2 * D], F32))
            v_all = ctx.enter_context(nc.sbuf_tensor("v_all", [N, B, D], F32))
            preparation_block(nc, signals[0], A, ident, consts, weights, qk_rot, v_all)
            attention_block(nc, signals[1], A, x2_all, ident, consts, weights, qk_rot, v_all)
        ffn_block(nc, signals[2], A, x2_all, ident, out)


def rope_table():
    inv = (np.float32(1.0) / np.float32(10000.0) ** (np.arange(0, HD, 2, dtype=np.float32) / np.float32(HD))).astype(np.float32)
    f = np.arange(N, dtype=np.float32)[:, None] * inv[None, :]
    cos, sin = np.cos(f), np.sin(f)
    return np.stack([np.concatenate([cos, cos], 1), np.concatenate([-sin, sin], 1)], 1).astype(np.float32)


_INS = {"x": "x", "ctx_1024": "ctx", "L0_attn_qkv_w": "qkv_w", "L0_attn_qkv_b": "qkv_b", "L0_attn_proj_w": "proj_w",
        "L0_attn_proj_b": "proj_b", "L0_xattn_ln_gamma": "gamma", "L0_xattn_ln_beta": "beta", "L0_xattn_w_q": "w_q",
        "L0_xattn_w_kv": "w_kv", "L0_xattn_w_out": "w_out", "L0_xattn_b_out": "b_out", "L0_xattn_gate": "gate",
        "L0_ffn_gate_w": "gate_w", "L0_ffn_ew1": "ew1", "L0_ffn_ew2": "ew2", "L0_ffn_ew3": "ew3",
        "L0_ffn_sw1": "sw1", "L0_ffn_sw2": "sw2", "L0_ffn_sw3": "sw3"}


def kernel(**inputs):
    import concourse.bacc as _bacc
    from concourse import mybir as _mybir
    from concourse.bass_utils import run_bass_kernel_spmd as _run

    nc = _bacc.Bacc("TRN2", target_bir_lowering=False, num_devices=1)
    arrays, args = {}, {}
    for name, short in _INS.items():
        a = np.ascontiguousarray(inputs[name])
        arrays[f"in_{name}_dram"] = a
        args[short] = nc.dram_tensor(f"in_{name}_dram", a.shape, _mybir.dt.from_np(a.dtype), kind="ExternalInput").ap()
    table = rope_table()
    arrays["in_rope_dram"] = table
    args["rope"] = nc.dram_tensor("in_rope_dram", table.shape, _mybir.dt.from_np(table.dtype), kind="ExternalInput").ap()
    out = nc.dram_tensor("out_0_dram", (B, N, D), _mybir.dt.from_np(np.dtype("float32")), kind="ExternalOutput").ap()
    decoder_layer(nc, args, out)
    r = _run(nc, [arrays], core_ids=[0])
    return r.results[0]["out_0_dram"]
```

```python
from contextlib import ExitStack

import numpy as np

import concourse.bass as bass
from concourse import mybir

F32 = mybir.dt.float32
F32R = mybir.dt.float32r
U32 = mybir.dt.uint32
ALU = mybir.AluOpType
ACT = mybir.ActivationFunctionType
X = mybir.AxisListType.X

B, N, D = 8, 112, 256
P = 128
KD = D // P
H, HD = 16, 16
CH, CHD = 16, 64
INNER = CH * CHD
SK, ST = 375, 3
SKT = SK // ST
SKP = SK + 1
PAIRS = CH // 2
EXP = 8
HID = 2 * D
MH = HID // P
TOK = B * N
HALF = TOK // 2
VS = HD + 2
VW = VS + HD
EPS = 1e-5
SELF_SCALE = float(HD) ** -0.5
CROSS_SCALE = float(CHD) ** -0.5

FILLS = ["QA", "QB", "KA", "KB", "S0", "S1", "S2", "S3", "T0", "T1", "O0", "T2", "T3", "O1",
         "OT", "PJ", "NT", "R0", "R1", "Q0", "Q1"]
LAST_READ = {
    "QA": ("qk_stacked_t", 4, 0), "QB": ("qk_stacked_t", 4, 1), "KA": ("qk_stacked_t", 4, 2),
    "KB": ("qk_stacked_t", 4, 3),
    "S0": ("s_shifted", 4, 0), "S1": ("s_shifted", 4, 1), "S2": ("s_shifted", 4, 2), "S3": ("s_shifted", 4, 3),
    "T0": ("pt_lo", 4, 0), "T1": ("pt_lo", 4, 1), "T2": ("pt_lo", 4, 2), "T3": ("pt_lo", 4, 3),
    "O0": ("o_summed", 2, 0), "O1": ("o_summed", 2, 1), "OT": ("ot_lo", 1, 0),
    "PJ": ("res1", 1, 0),
    "NT": ("xn_affine", 2, 1), "R0": ("q_rows", 2, 0), "R1": ("q_rows", 2, 1), "Q0": ("qt_lo", 2, 0), "Q1": ("qt_lo", 2, 1),
}
V_FILLS = ["V00", "V01", "V02", "V10", "V11", "V12"]
FILL_AT = {(0, 3): ["QA"], (0, 4): ["QB"], (1, 0): ["KA"], (1, 1): ["KB"], (1, 3): ["S0"], (1, 4): ["S1"],
           (2, 0): ["S2"], (2, 1): ["S3"], (2, 3): ["T0"], (2, 4): ["T1"], (3, 1): ["O0", "T2"],
           (3, 2): ["T3"], (3, 4): ["O1"], (5, 0): ["OT"], (5, 1): ["C0"], (5, 2): ["C1"], (5, 3): ["PJ"],
           (6, 2): ["NT"], (6, 4): ["R0"], (7, 0): ["R1"], (7, 1): ["Q0"], (7, 2): ["Q1"]}
V_AT = {0: "V02", 2: "V10", 3: "V11", 4: "V12", 6: "V00", 7: "V01"}


def fill_no(name, b):
    return len(FILLS) * b + FILLS.index(name) + 1


def v_no(name, b):
    return len(V_FILLS) * b + V_FILLS.index(name) + 1


def v_before_output(b):
    return v_no("V02", b + 1) if not isinstance(b, int) or b + 1 < B else v_no("V12", b)


class Signals:

    def __init__(self, nc, ctx, block):
        self.nc, self.ctx, self.block, self.sems = nc, ctx, block, {}

    def __getitem__(self, name):
        if name not in self.sems:
            self.sems[name] = self.ctx.enter_context(self.nc.semaphore(self.block + "_" + name))
        return self.sems[name]


def later(count):
    return not isinstance(count, int) or count > 0


def product(eng, out, lhs, rhs, start=True, stop=True, **kw):
    (lh, ll), (rh, rl) = lhs, rhs
    eng.matmul(out, ll, rh, start=start, stop=False, **kw)
    eng.matmul(out, lh, rl, start=False, stop=False, **kw)
    return eng.matmul(out, lh, rh, start=False, stop=stop, **kw)


def split_pair(nc, ctx, name, shape):
    return tuple(ctx.enter_context(nc.sbuf_tensor(f"{name}_{part}", shape, F32R)) for part in ("hi", "lo"))


def product_over_width(pe, out, lhs, w, cols):
    for k in range(KD):
        last = product(pe, out, tuple(t[:, k, :] for t in lhs), tuple(t[:, k, cols] for t in w),
                       start=k == 0, stop=k == KD - 1)
    return last


def preparation_block(nc, sg, A, ident, consts, weights, qk_rot, v_all):
    w_k, w_v, w_q, w_o, w_proj = weights
    with ExitStack() as ctx:
        def sb(name, shape, dt=F32):
            return ctx.enter_context(nc.sbuf_tensor(name, shape, dt))

        w_qkv = split_pair(nc, ctx, "w_qkv", [P, KD, 3 * D])
        raw = sb("raw", [P, 8, D])
        rope_sb = sb("rope_sb", [N, 2, HD])
        bias_qkv = sb("bias_qkv", [N, 3 * D])
        x_in = sb("x_in", [N, 2, D])
        xt = [split_pair(nc, ctx, f"xt{i}", [P, KD, N]) for i in range(2)]
        qk = sb("qk", [N, 2, 2 * D])
        sin_part = sb("sin_part", [N, 2, 2 * D])
        ps_w = ctx.enter_context(nc.psum_tensor("ps_w", [P, 2, 512], F32))
        ps_x = ctx.enter_context(nc.psum_tensor("ps_x", [P, 2, 512], F32))
        ps_qk = ctx.enter_context(nc.psum_tensor("ps_qk", [P, 2, 512], F32))
        ps_v = ctx.enter_context(nc.psum_tensor("ps_v", [P, 2, 512], F32))
        plain = [(w_o, A["w_out"]), (w_k, A["w_kv"][:, 0:INNER]), (w_v, A["w_kv"][:, INNER:2 * INNER]), (w_q, A["w_q"])]
        plain_raw = [sb(f"plain_raw{i}", [P, 2048]) for i in range(4)]
        heads, hw = 2 * H, HD // 2
        block = ctx.enter_context(nc.Block())

        @block.sync
        def _(sp):
            sp.dma_start(raw[:, 0:6, :], A["qkv_w"].rearrange("(o p) d -> p o d", p=P)).then_inc(sg["raw0"], 16)
            for b in range(B):
                if later(b - 1):
                    sp.wait_ge(sg["xt_full"], b - 1)
                sp.dma_start(x_in[:, b % 2, :], A["x"][b]).then_inc(sg[f"x_loaded{b % 2}"], 16)
                if 2 <= b < 6:
                    i = b - 2
                    src = plain[i][1].rearrange("(k p) n -> p k n", p=P)
                    sp.dma_start(plain_raw[i][:, :].rearrange("p (k n) -> p k n", k=src.shape[1]), src)\
                        .then_inc(sg[f"plain{i}"], 16)
            sp.dma_start(raw[:, 6:8, :], A["proj_w"].rearrange("(o p) d -> p o d", p=P)).then_inc(sg["raw1"], 16)

        @block.gpsimd
        def _(pool):
            def plain_lo(i):
                (hi_w, lo_w), _ = plain[i]
                pool.wait_ge(sg["plain_hi"], i + 1)
                return pool.tensor_tensor(lo_w[:, :, :].rearrange("p k n -> p (k n)"), plain_raw[i][:, :],
                                          hi_w[:, :, :].rearrange("p k n -> p (k n)").bitcast(F32), ALU.subtract)

            pool.dma_start(rope_sb[:, :, :], A["rope"]).then_inc(sg["consts"], 16)
            pool.dma_start(bias_qkv[:, :], A["qkv_b"].partition_broadcast(N)).then_inc(sg["consts"], 16)
            pool.memset(ident[:, :], 0.0).then_inc(sg["zeroed"], 1)
            pool.wait_ge(sg["zeroed"], 1)
            pool.affine_select(out=ident[:, :], in_=ident[:, :], compare_op=ALU.not_equal, fill=1.0, base=0,
                               pattern=[[-1, P]], channel_multiplier=1).then_inc(sg["ident"], 1)
            for name in ("proj_b", "b_out", "gate"):
                pool.dma_start(consts[name][:, :], A[name].partition_broadcast(N)).then_inc(sg["consts2"], 16)
            for name in ("gamma", "beta"):
                pool.dma_start(consts[name][:, :], A[name].rearrange("(k p) -> p k", p=P),
                               allow_slow_non_contiguous=True).then_inc(sg["consts2"], 16)
            pool.memset(consts["neg_half"][:, :], -0.5).then_inc(sg["neg_half"], 1)
            pool.wait_ge(sg["consts"], 32)
            with pool.Fori(0, B // 2) as b0:
                for i in range(2):
                    pool.wait_ge(sg["qk_biased"], 2 * b0 + i + 1)
                    t = qk[:, i, :].rearrange("p (h w) -> p h w", w=HD)
                    out = sin_part[:, i, :].rearrange("p (h w) -> p h w", w=HD)
                    for dst, src in ((0, hw), (hw, 0)):
                        sin = rope_sb[:, 1, dst:dst + hw].unsqueeze(1).to_broadcast([N, heads, hw])
                        pool.tensor_tensor(out[:, :, dst:dst + hw], t[:, :, src:src + hw], sin, ALU.mult)\
                            .then_inc(sg["sin_part"], 1)
            plain_lo(0).then_inc(sg["plain_lo"], 1)
            pool.wait_ge(sg["consts2"], 5 * 16)

        @block.scalar
        def _(act):
            def hi(dst, src):
                return act.activation(dst, src, ACT.Copy)

            def xt_hi(b, i):
                act.wait_ge(sg["xt_full"], b + 1)
                if later(b - 1):
                    act.wait_ge(sg["v_full"], b - 1)
                hi(xt[i][0][:, :, :].rearrange("p k n -> p (k n)"), ps_x[:, i, 0:KD * N]).then_inc(sg["xt_hi"], 1)

            for i in range(4):
                k, half = i % 2, i // 2
                act.wait_ge(sg["w_full"], i + 1)
                if half == 0:
                    hi(w_qkv[0][:, k, 0:512], ps_w[:, k, :]).then_inc(sg["w_hi"], 1)
                else:
                    hi(w_qkv[0][:, k, 512:768], ps_w[:, k, 0:256]).then_inc(sg["w_hi"], 1)
            xt_hi(0, 0)
            xt_hi(1, 1)
            with act.Fori(1, B // 2) as b0:
                for i in range(2):
                    xt_hi(2 * b0 + i, i)
            for i, ((w, _), _) in enumerate(plain):
                act.wait_ge(sg[f"plain{i}"], 16)
                hi(w[:, :, :].rearrange("p k n -> p (k n)"), plain_raw[i][:, :]).then_inc(sg["plain_hi"], 1)
            for k in range(KD):
                act.wait_ge(sg["w_full"], 5 + k)
                hi(w_proj[0][:, k, :], ps_w[:, k, 256:512]).then_inc(sg["w_hi"], 1)
            act.wait_ge(sg["consts2"], 5 * 16)
            act.activation(consts["gate"][:, :], consts["gate"][:, :], ACT.Tanh).then_inc(sg["gate_ready"], 1)

        @block.vector
        def _(dve):
            def lo(dst, src, part):
                return dve.tensor_tensor(dst, src, part.bitcast(F32), ALU.subtract)

            for i in range(4):
                k, half = i % 2, i // 2
                cols = slice(512 * half, 512 * half + 512 // (1 + half))
                dve.wait_ge(sg["w_hi"], i + 1)
                lo(w_qkv[1][:, k, cols], ps_w[:, k, 0:512 // (1 + half)], w_qkv[0][:, k, cols]).then_inc(sg["wt_lo"], 1)

            def xt_lo(b, i):
                dve.wait_ge(sg["xt_hi"], b + 1)
                lo(xt[i][1][:, :, :].rearrange("p k n -> p (k n)"), ps_x[:, i, 0:KD * N],
                   xt[i][0][:, :, :].rearrange("p k n -> p (k n)")).then_inc(sg["xt_lo"], 1)

            def add_bias(b, i):
                dve.wait_ge(sg["qk_full"], b + 1)
                dve.tensor_tensor(qk[:, i, :], ps_qk[0:N, i, :], bias_qkv[:, 0:2 * D], ALU.add)\
                    .then_inc(sg["qk_biased"], 1)
                dve.wait_ge(sg["v_full"], b + 1)
                dve.tensor_tensor(v_all[:, b, :], ps_v[0:N, i, 0:D], bias_qkv[:, 2 * D:3 * D], ALU.add)\
                    .then_inc(sg["v_biased"], 1)

            def rotate(b, i):
                cos = rope_sb[:, 0, :].unsqueeze(1).to_broadcast([N, heads, HD])
                dve.wait_ge(sg["sin_part"], 2 * b + 2)
                dve.tensor_tensor(qk[:, i, :].rearrange("p (h w) -> p h w", w=HD),
                                  qk[:, i, :].rearrange("p (h w) -> p h w", w=HD), cos, ALU.mult)\
                    .then_inc(sg["cos_part"], 1)
                dve.wait_ge(sg["cos_part"], b + 1)
                dve.tensor_tensor(qk_rot[:, b, :], qk[:, i, :], sin_part[:, i, :], ALU.add).then_inc(sg["rotated"], 1)

            xt_lo(0, 0)
            xt_lo(1, 1)
            dve.wait_ge(sg["consts"], 32)
            with dve.Fori(0, B // 2 - 1) as b0:
                for i in range(2):
                    add_bias(2 * b0 + i, i)
                for i in range(2):
                    xt_lo(2 * b0 + 2 + i, i)
                for i in range(2):
                    rotate(2 * b0 + i, i)
                dve.wait_ge(sg["rotated"], 2 * b0 + 2)
            for i in range(2):
                add_bias(B - 2 + i, i)
            for i in range(2):
                rotate(B - 2 + i, i)
            for i in range(1, 4):
                (hi_w, lo_w), _ = plain[i]
                dve.wait_ge(sg["plain_hi"], i + 1)
                lo(lo_w[:, :, :].rearrange("p k n -> p (k n)"), plain_raw[i][:, :],
                   hi_w[:, :, :].rearrange("p k n -> p (k n)")).then_inc(sg["plain_lo"], 1)
            for k in range(KD):
                dve.wait_ge(sg["w_hi"], 5 + k)
                lo(w_proj[1][:, k, :], ps_w[:, k, 256:512], w_proj[0][:, k, :]).then_inc(sg["wt_lo"], 1)
            dve.wait_ge(sg["gate_ready"], 1)
            dve.tensor_scalar(consts["b_out"][:, :], consts["b_out"][:, :], consts["gate"][:, 0:1], None, ALU.mult)\
                .then_inc(sg["bias_out_gated"], 1)

        @block.tensor
        def _(pe):
            pe.wait_ge(sg["raw0"], 16)
            pe.wait_ge(sg["ident"], 1)
            for i in range(4):
                k, half = i % 2, i // 2
                if later(i - 1):
                    pe.wait_ge(sg["wt_lo"], i - 1)
                for j in range(4 if half == 0 else 2):
                    last = pe.transpose(ps_w[:, k, j * P:(j + 1) * P], raw[:, 4 * half + j, k * P:(k + 1) * P], ident[:, :])
                last.then_inc(sg["w_full"], 1)

            def x_transpose(b0, i):
                b = 2 * b0 + i
                pe.wait_ge(sg[f"x_loaded{i}"], 16 * (b0 + 1))
                if later(b - 1):
                    pe.wait_ge(sg["xt_lo"], b - 1)
                for k in range(KD):
                    last = pe.transpose(ps_x[:, i, k * N:(k + 1) * N], x_in[:, i, k * P:(k + 1) * P], ident[0:N, 0:N])
                last.then_inc(sg["xt_full"], 1)

            def project(b, i):
                pe.wait_ge(sg["xt_lo"], b + 1)
                if later(b - 1):
                    pe.wait_ge(sg["qk_biased"], b - 1)
                if later(b - 1):
                    pe.wait_ge(sg["v_biased"], b - 1)
                product_over_width(pe, ps_qk[0:N, i, :], xt[i], w_qkv, slice(0, 512)).then_inc(sg["qk_full"], 1)
                product_over_width(pe, ps_v[0:N, i, 0:D], xt[i], w_qkv, slice(512, 768)).then_inc(sg["v_full"], 1)

            for i in range(2):
                x_transpose(0, i)
            pe.wait_ge(sg["wt_lo"], 4)
            for i in range(2):
                x_transpose(1, i)
            for i in range(2):
                project(i, i)
            with pe.Fori(1, B // 2 - 1) as b0:
                for i in range(2):
                    x_transpose(b0 + 1, i)
                for i in range(2):
                    project(2 * b0 + i, i)
            for i in range(2):
                project(B - 2 + i, i)
            pe.wait_ge(sg["raw1"], 16)
            for k in range(KD):
                for j in range(2):
                    last = pe.transpose(ps_w[:, k, 256 + j * P:256 + (j + 1) * P], raw[:, 6 + j, k * P:(k + 1) * P], ident[:, :])
                last.then_inc(sg["w_full"], 1)



def attention_block(nc, sg, A, x2_all, ident, consts, weights, qk_rot, v_all):
    w_k, w_v, w_q, w_o, w_proj = weights
    bias_proj, bias_out, gate, gamma, beta, neg_half = (consts[n] for n in ("proj_b", "b_out", "gate", "gamma", "beta",
                                                                           "neg_half"))
    with ExitStack() as ctx:
        def sb(name, shape, dt=F32):
            return ctx.enter_context(nc.sbuf_tensor(name, shape, dt))

        def pair(name, shape):
            return split_pair(nc, ctx, name, shape)


        x_cur = sb("x_cur", [N, D])
        x_res = sb("x_res", [N, D])
        v_self = sb("v_self", [N, B, 2, VW], F32R)
        work = sb("work", [N, 2048])
        qk_t = (sb("q_stacked_t", [P, B, N], F32R), sb("k_stacked_t", [P, B, N], F32R))
        s_max = sb("s_max", [N, 4, 4])
        o_sum = sb("o_sum", [N, 2, 4, HD])
        s_rcp = sb("s_rcp", [N, 2, 4])
        pt = pair("pt", [N, 8, N])
        o_self = sb("o_self", [N, 2 * B, HD])
        o_rows = sb("o_rows", [N, D])
        o_dram = nc.dram_tensor("o_shuffle", (B, 2 * B, N, HD), F32).ap()
        ot = pair("ot", [P, KD, N])
        res = sb("res", [N, D])
        xn = sb("xn", [N, D])
        x1 = sb("x1", [N, D])
        stats = sb("stats", [N, 2, 6])
        mv = sb("mv", [N, 2, 2])
        rstd = sb("rstd", [N, 2])
        xnt_f = sb("xnt_f", [P, KD, N])
        xnt = pair("xnt", [P, KD, N])
        ctx_raw = sb("ctx_raw", [SKT, ST, D])
        ctxt = pair("ctxt", [P, KD, SKP])
        qt = pair("qt", [P, PAIRS, N])
        kt = pair("kt", [P, 2, SKP])
        v = pair("v", [SKT, 2, ST, 512])
        probs = sb("probs", [N, 2, 2, SK])
        c_max = sb("c_max", [N, 2, 2])
        c_neg = sb("c_neg", [N, 2, 2])
        c_sum = sb("c_sum", [N, 2, 2])
        c_rcp = sb("c_rcp", [N, 2, 2])
        cpt = pair("cpt", [SKT, 2, ST, N])
        oct_ = pair("oct", [P, PAIRS, N])
        res2 = sb("res2", [N, D])
        stats2 = sb("stats2", [N, 6])
        mv2 = sb("mv2", [N, 2])
        rstd2 = sb("rstd2", [N, 1])

        ps_s = ctx.enter_context(nc.psum_tensor("ps_s", [P, 2, 512], F32))
        ps_t = ctx.enter_context(nc.psum_tensor("ps_t", [P, 2, 512], F32))
        ps_o = ctx.enter_context(nc.psum_tensor("ps_o", [P, 512], F32))
        ps_v = ctx.enter_context(nc.psum_tensor("ps_vx", [P, 512], F32))
        ps_a = ctx.enter_context(nc.psum_tensor("ps_a", [P, 2, 512], F32))

        def bank(name):
            if name[0] == "C":
                return ps_a[:, FILLS.index({"C0": "PJ", "C1": "NT"}[name]) % 2, :]
            return ps_a[:, FILLS.index(name) % 2, :]

        def ctx_bank(b, k):
            return bank(f"C{k}") if later(b) else ps_s[:, k, :]

        stack = work[:, :].rearrange("p (t b r c w) -> p t b r c w", t=2, b=B, r=2, c=4)
        e_self = work[:, 0:2 * B * N].rearrange("p (s n) -> p s n", s=2 * B)
        q_rows = work[:, 0:1024].rearrange("p (i n) -> p i n", i=2)
        block = ctx.enter_context(nc.Block())

        def qk_src(b, i, r):
            return qk_rot[:, :, bass.ds(i * D + (2 * b + r) * HD, HD)].unsqueeze(2).to_broadcast([N, B, 2, HD])

        def v_heads(b):
            return v_all[:, :, bass.ds(2 * HD * b, 2 * HD)].rearrange("p b (r w) -> p b r w", r=2)

        def iterations(eng, iteration):
            iteration(0, True)
            with eng.Fori(1, B - 1) as b:
                iteration(b, True)
            iteration(B - 1, False)

        @block.sync
        def _(sp):
            def entry(b):
                if later(b):
                    sp.wait_ge(sg["c_full"], 2 * b)
                sp.dma_start(ctx_raw[:, :, :], A["ctx"][bass.ds(b, 1)].rearrange("a (t p) d -> p (a t) d", p=SKT))\
                    .then_inc(sg["ctx_loaded"], 16)
                if later(b):
                    sp.wait_ge(sg["x_res_ready"], b)
                sp.dma_start(x_cur[:, :], A["x"][bass.ds(b, 1)].rearrange("a n d -> (a n) d")).then_inc(sg["x_loaded"], 16)
                sp.wait_ge(sg["o_normed"], 2 * b + 2)
                sp.dma_start(o_dram[bass.ds(b, 1)].rearrange("a k q w -> q (a k) w"), o_self[:, :, :])\
                    .then_inc(sg["o_stored"], 16)
                sp.wait_ge(sg["o_stored"], 16 * (b + 1))
                if later(b):
                    sp.wait_ge(sg["a_full"], fill_no("OT", b - 1))
                sp.dma_start(o_rows[:, :], o_dram[bass.ds(b, 1)].rearrange("a k (i l) w -> (a k i) (l w)", l=D // HD))\
                    .then_inc(sg["o_rows_loaded"], 16)
            for b in range(B):
                entry(b)

        @block.gpsimd
        def _(pool):
            for i, value in ((HD, 1.0), (HD + 1, 0.0)):
                pool.memset(v_self[:, :, :, i:i + 1].bitcast(F32), value).then_inc(sg["v_ones"], 1)
            for t in ctxt:
                pool.memset(t[:, :, SK:SKP].bitcast(F32), 0.0).then_inc(sg["padded"], 1)

            def residual(b):
                pool.wait_ge(sg["x_loaded"], 16 * (b + 1))
                if later(b):
                    pool.wait_ge(sg["res1"], b)
                pool.tensor_tensor(x_res[:, :], x_cur[:, :], bias_proj[:, :], ALU.add).then_inc(sg["x_res_ready"], 1)

            def stack_lo(b, i, r):
                pool.wait_ge(sg["qk_hi"], 4 * b + 2 * i + r + 1)
                src = qk_src(b, i, r)
                hi = stack[:, i, :, r, 0:1, :].to_broadcast([N, B, 2, HD])
                dst = stack[:, i, :, r, 1:4:2, :] if i == 0 else stack[:, i, :, r, 2:4, :]
                pool.tensor_tensor(dst.bitcast(F32R), src, hi, ALU.subtract).then_inc(sg["qk_lo"], 1)

            def x1_out(b):
                pool.wait_ge(sg["x1_ready"], b + 1)
                pool.nop(nofuse=True)
                pool.tensor_tensor(x2_all[0:N, b, :], x1[:, :], bias_out[:, :], ALU.add).then_inc(sg["x1_kept"], 1)

            def rsqrt(rs, mean_var, tag, count):
                pool.wait_ge(sg[tag + "_var"], count)
                pool.tensor_tensor(rs, mean_var[:, 1:2], neg_half[:, :], ALU.pow).then_inc(sg[tag + "_rstd"], 1)

            def x2_norm(b):
                rsqrt(rstd2[:, :], mv2[:, :], "n3", b + 1)

            def normalise(b, s):
                pool.wait_ge(sg["c_rcp_ready"], PAIRS * b + s + 1)
                p = probs[:, s % 2]
                r = c_rcp[:, s % 2].unsqueeze(2).to_broadcast([N, 2, SK])
                pool.tensor_tensor(p, p, r, ALU.mult).then_inc(sg["p_normed"], 1)

            residual(0)
            for i, r in ((0, 0), (0, 1), (1, 0), (1, 1)):
                stack_lo(0, i, r)
            rsqrt(rstd[:, 0:1], mv[:, 0, :], "n1", 1)
            rsqrt(rstd[:, 1:2], mv[:, 1, :], "n2", 1)
            x1_out(0)

            def iteration(b, more):
                for s in range(PAIRS):
                    if more and s == 0:
                        for i, r in ((0, 0), (0, 1), (1, 0)):
                            stack_lo(b + 1, i, r)
                    if more and s == 6:
                        rsqrt(rstd[:, 1:2], mv[:, 1, :], "n2", b + 2)
                    normalise(b, s)
                    if more and s == 5:
                        rsqrt(rstd[:, 0:1], mv[:, 0, :], "n1", b + 2)
                    if more and s == 0:
                        stack_lo(b + 1, 1, 1)
                    if more and s == 1:
                        residual(b + 1)
                    if more and s == 6:
                        x1_out(b + 1)
                    if s == 2 and later(b):
                        x2_norm(b - 1)
            iterations(pool, iteration)
            x2_norm(B - 1)

        @block.scalar
        def _(act):
            def hi(dst, src):
                return act.activation(dst, src, ACT.Copy)

            def v_hi(b):
                if later(b):
                    act.wait_ge(sg["a_full"], fill_no("O1", b - 1))
                hi(v_self[:, :, :, 0:HD], v_heads(b)).then_inc(sg["v_self_hi"], 1)

            def stack_hi(b):
                if later(b):
                    act.wait_ge(sg["a_full"], fill_no("Q1", b - 1))
                for i in range(2):
                    for r in range(2):
                        dst = stack[:, i, :, r, 0:4:2, :] if i == 0 else stack[:, i, :, r, 0:2, :]
                        hi(dst.bitcast(F32R), qk_src(b, i, r)).then_inc(sg["qk_hi"], 1)

            def stacked_t(b, f):
                if later(b):
                    act.wait_ge(sg["a_full"], fill_no("S3", b - 1))
                act.wait_ge(sg["a_full"], fill_no(f, b))
                first = 4 * ("A", "B").index(f[1])
                dst = qk_t[("Q", "K").index(f[0])][:, first:first + 4, :]
                hi(dst.rearrange("p a n -> p (a n)"), bank(f)[:, 0:4 * N]).then_inc(sg["qk_stacked_t"], 1)

            def self_exp(b, i):
                act.wait_ge(sg["s_shifted"], 4 * b + 2 * i + 2)
                e = e_self[:, 8 * i:8 * i + 8, :]
                act.activation(e, e, ACT.Exp, scale=SELF_SCALE).then_inc(sg["e_ready"], 1)

            def self_pt(b, i):
                act.wait_ge(sg["a_full"], fill_no(f"T{i}", b))
                if i >= 2:
                    act.wait_ge(sg["a_full"], fill_no("O0", b))
                elif later(b):
                    act.wait_ge(sg["a_full"], fill_no("O1", b - 1))
                dst = pt[0][:, 4 * (i % 2):4 * (i % 2) + 4, :]
                hi(dst.rearrange("p a n -> p (a n)"), bank(f"T{i}")[0:N, 0:4 * N]).then_inc(sg["pt_hi"], 1)

            def ot_hi(b):
                act.wait_ge(sg["a_full"], fill_no("OT", b))
                hi(ot[0][:, :, :].rearrange("p k n -> p (k n)"), bank("OT")[:, 0:KD * N]).then_inc(sg["ot_hi"], 1)

            def ctx_hi(b, k):
                act.wait_ge(sg["c_full"], 2 * b + k + 1)
                if later(b):
                    act.wait_ge(sg["k_full"], PAIRS * b)
                hi(ctxt[0][:, k, 0:SK], ctx_bank(b, k)[:, 0:SK]).then_inc(sg["ctxt_hi"], 1)

            def xn_affine(b):
                act.wait_ge(sg["a_full"], fill_no("NT", b))
                if later(b):
                    act.wait_ge(sg["xnt_lo_ready"], b)
                for k in range(KD):
                    act.activation(xnt_f[:, k, :], bank("NT")[:, k * N:(k + 1) * N], ACT.Identity,
                                   bias=beta[:, k:k + 1], scale=gamma[:, k:k + 1]).then_inc(sg["xn_affine"], 1)

            def q_copy(b, i):
                act.wait_ge(sg["a_full"], fill_no(f"R{i}", b))
                act.activation(q_rows[:, i, :], bank(f"R{i}")[0:N, :], ACT.Copy).then_inc(sg["q_rows"], 1)

            def q_hi(b, i):
                act.wait_ge(sg["a_full"], fill_no(f"Q{i}", b))
                if later(PAIRS * b):
                    act.wait_ge(sg["s_full"], PAIRS * b)
                hi(qt[0][:, 4 * i:4 * i + 4, :].rearrange("p a n -> p (a n)"), bank(f"Q{i}")[:, 0:4 * N]).then_inc(sg["qt_hi"], 1)

            def k_hi(b, p):
                act.wait_ge(sg["k_full"], PAIRS * b + p + 1)
                if later(PAIRS * b + p - 1):
                    act.wait_ge(sg["s_full"], PAIRS * b + p - 1)
                hi(kt[0][:, p % 2, :], ps_o[:, 0:SKP]).then_inc(sg["kt_hi"], 1)

            def v_hi_cross(b, f):
                q, t = int(f[1]), int(f[2])
                act.wait_ge(sg["v_full"], v_no(f, b))
                if later(PAIRS * (b - 1) + 4 * q + 4):
                    act.wait_ge(sg["pv_full"], PAIRS * (b - 1) + 4 * q + 4)
                hi(v[0][:, q, t, :], ps_v[0:SKT, :]).then_inc(sg["v_hi"], 1)

            def exps(b, s):
                act.wait_ge(sg["c_neg_ready"], PAIRS * b + s + 1)
                if later(PAIRS * b + s - 1):
                    act.wait_ge(sg["t_full"], PAIRS * b + s - 1)
                for h in range(2):
                    act.activation(probs[:, s % 2, h, :], ps_s[0:N, h, 0:SK], ACT.Exp, bias=c_neg[:, s % 2, h:h + 1],
                                   scale=CROSS_SCALE, accum_out=c_sum[:, s % 2, h:h + 1]).then_inc(sg["c_exp"], 1)

            def cpt_hi(b, s):
                act.wait_ge(sg["t_full"], PAIRS * b + s + 1)
                if later(PAIRS * b + s):
                    act.wait_ge(sg["pv_full"], PAIRS * b + s)
                hi(cpt[0][:, :, :, :].rearrange("p h t n -> p h (t n)"), ps_t[0:SKT, :, 0:ST * N]).then_inc(sg["cpt_hi"], 1)

            def o_hi(b, s):
                act.wait_ge(sg["pv_full"], PAIRS * b + s + 1)
                if later(b):
                    act.wait_ge(sg["wo_full"], b)
                for h in range(2):
                    r = slice(64 * h, 64 * h + 64)
                    hi(oct_[0][r, s, :], ps_o[r, h * N:(h + 1) * N]).then_inc(sg["oct_hi"], 1)

            def fill_hi(b, f):
                if f in ("QA", "QB", "KA", "KB"):
                    stacked_t(b, f)
                elif f[0] == "T":
                    self_pt(b, int(f[1]))
                elif f[0] == "C":
                    ctx_hi(b, int(f[1]))
                elif f == "OT":
                    ot_hi(b)
                elif f == "NT":
                    xn_affine(b)
                elif f[0] == "R":
                    q_copy(b, int(f[1]))
                elif f[0] == "Q":
                    q_hi(b, int(f[1]))

            stack_hi(0)
            v_hi(0)
            for f in ("QA", "QB", "KA", "KB"):
                fill_hi(0, f)
            self_exp(0, 0)
            self_exp(0, 1)
            fill_hi(0, "T0")
            fill_hi(0, "T1")
            act.wait_ge(sg["padded"], 2)
            fill_hi(0, "C0")
            fill_hi(0, "C1")
            fill_hi(0, "T2")
            fill_hi(0, "T3")
            k_hi(0, 0)
            v_hi_cross(0, "V00")
            k_hi(0, 1)
            v_hi_cross(0, "V01")
            fill_hi(0, "OT")
            fill_hi(0, "NT")
            fill_hi(0, "R0")
            fill_hi(0, "R1")
            fill_hi(0, "Q0")
            fill_hi(0, "Q1")

            def iteration(b, more):
                for s in range(PAIRS):
                    def place(n):
                        if more:
                            for f in FILL_AT.get((s, n), ()):
                                fill_hi(b + 1, f)

                    if more and s == 0:
                        stack_hi(b + 1)
                    if more and s == 2:
                        self_exp(b + 1, 0)
                    place(0)
                    if s + 2 < PAIRS:
                        k_hi(b, s + 2)
                    elif more:
                        k_hi(b + 1, s + 2 - PAIRS)
                    if s != 3:
                        place(1)
                    exps(b, s)
                    if s == 3:
                        place(1)
                    if more and s == 2:
                        self_exp(b + 1, 1)
                    if s == 6:
                        place(2)
                    if s in V_AT and (s < 6 or more):
                        v_hi_cross(b if s < 6 else b + 1, V_AT[s])
                    if s != 6:
                        place(2)
                    if more and s == 0:
                        v_hi(b + 1)
                    place(3)
                    if s >= 2:
                        o_hi(b, s - 2)
                    elif later(b):
                        o_hi(b - 1, s + 6)
                    if s >= 1:
                        cpt_hi(b, s - 1)
                    elif later(b):
                        cpt_hi(b - 1, 7)
                    place(4)
            iterations(act, iteration)
            o_hi(B - 1, 6)
            cpt_hi(B - 1, 7)
            o_hi(B - 1, 7)

        @block.vector
        def _(dve):
            def lo(dst, src, part):
                return dve.tensor_tensor(dst, src, part.bitcast(F32), ALU.subtract)

            def moments(src, st, mean_var, tag, count):
                dve.bn_stats(st, src).then_inc(sg[tag + "_stats"], 1)
                dve.wait_ge(sg[tag + "_stats"], count)
                dve.nop(nofuse=True)
                dve.bn_aggr(mean_var, st).then_inc(sg[tag + "_aggr"], 1)
                dve.wait_ge(sg[tag + "_aggr"], count)
                dve.tensor_scalar(mean_var[:, 1:2], mean_var[:, 1:2], EPS, None, ALU.add).then_inc(sg[tag + "_var"], 1)

            def norm(src, dst, mean_var, rs, tag, count):
                dve.wait_ge(sg[tag + "_rstd"], count)
                return dve.tensor_scalar(dst, src, mean_var[:, 0:1], rs, ALU.subtract, ALU.mult)

            def v_split(b):
                dve.wait_ge(sg["v_self_hi"], b + 1)
                lo(v_self[:, :, :, VS:VW], v_heads(b), v_self[:, :, :, 0:HD]).then_inc(sg["v_self_lo"], 1)

            def self_max(b, f):
                src = bank(f"S{f}")[0:N, 0:4 * N].rearrange("p (a n) -> p a n", a=4)
                dve.wait_ge(sg["a_full"], fill_no(f"S{f}", b))
                dve.reduce_max(s_max[:, f, :], src, X).then_inc(sg["s_max_ready"], 1)
                dve.wait_ge(sg["s_max_ready"], 4 * b + f + 1)
                dve.tensor_tensor(e_self[:, 4 * f:4 * f + 4, :], src,
                                  s_max[:, f, :].unsqueeze(2).to_broadcast([N, 4, N]), ALU.subtract)\
                    .then_inc(sg["s_shifted"], 1)

            def self_pt(b, i):
                dve.wait_ge(sg["pt_hi"], 4 * b + i + 1)
                dst = slice(4 * (i % 2), 4 * (i % 2) + 4)
                lo(pt[1][:, dst, :].rearrange("p a n -> p (a n)"), bank(f"T{i}")[0:N, 0:4 * N],
                   pt[0][:, dst, :].rearrange("p a n -> p (a n)")).then_inc(sg["pt_lo"], 1)

            def o_norm(b, i):
                dve.wait_ge(sg["a_full"], fill_no(f"O{i}", b))
                src = bank(f"O{i}")[0:N, 0:8 * VW].rearrange("p (r b w) -> p r b w", r=2, w=VW)
                if later(2 * b + i):
                    dve.wait_ge(sg["o_normed"], 2 * b + i)
                dve.reciprocal(s_rcp[:, :, :], src[:, :, :, HD]).then_inc(sg["s_rcp_ready"], 1)
                dve.tensor_copy(o_sum[:, :, :, :], src[:, :, :, VS:VW]).then_inc(sg["o_part"], 1)
                dve.wait_ge(sg["o_part"], 2 * b + i + 1)
                dve.tensor_tensor(o_sum[:, :, :, :], o_sum[:, :, :, :], src[:, :, :, 0:HD], ALU.add).then_inc(sg["o_summed"], 1)
                dve.wait_ge(sg["o_summed"], 2 * b + i + 1)
                dve.wait_ge(sg["s_rcp_ready"], 2 * b + i + 1)
                if later(16 * b):
                    dve.wait_ge(sg["o_stored"], 16 * b)
                out = o_self[:, :, :].rearrange("p (r b) w -> p r b w", r=2)[:, :, 4 * i:4 * i + 4, :]
                dve.tensor_tensor(out, o_sum[:, :, :, :], s_rcp[:, :, :].unsqueeze(3).to_broadcast([N, 2, 4, HD]),
                                  ALU.mult).then_inc(sg["o_normed"], 1)

            def ot_lo(b):
                dve.wait_ge(sg["ot_hi"], b + 1)
                lo(ot[1][:, :, :].rearrange("p k n -> p (k n)"), bank("OT")[:, 0:KD * N],
                   ot[0][:, :, :].rearrange("p k n -> p (k n)")).then_inc(sg["ot_lo"], 1)

            def ctx_lo(b, k):
                dve.wait_ge(sg["ctxt_hi"], 2 * b + k + 1)
                lo(ctxt[1][:, k, 0:SK], ctx_bank(b, k)[:, 0:SK], ctxt[0][:, k, 0:SK]).then_inc(sg["ctxt_lo"], 1)

            def residual_moments(b):
                dve.wait_ge(sg["a_full"], fill_no("PJ", b))
                dve.wait_ge(sg["x_res_ready"], b + 1)
                dve.tensor_tensor(res[:, :], bank("PJ")[0:N, 0:D], x_res[:, :], ALU.add).then_inc(sg["res1"], 1)
                dve.wait_ge(sg["res1"], b + 1)
                moments(res[:, :], stats[:, 0, :], mv[:, 0, :], "n1", b + 1)

            def x1_moments(b):
                if later(b):
                    dve.wait_ge(sg["x1_kept"], b)
                norm(res[:, :], x1[:, :], mv[:, 0, :], rstd[:, 0:1], "n1", b + 1).then_inc(sg["x1_ready"], 1)
                dve.wait_ge(sg["x1_ready"], b + 1)
                moments(x1[:, :], stats[:, 1, :], mv[:, 1, :], "n2", b + 1)

            def xn_norm(b):
                if later(b):
                    dve.wait_ge(sg["a_full"], fill_no("NT", b - 1))
                norm(x1[:, :], xn[:, :], mv[:, 1, :], rstd[:, 1:2], "n2", b + 1).then_inc(sg["xn_ready"], 1)

            def xnt_split(b):
                dve.wait_ge(sg["xn_affine"], 2 * b + 2)
                if later(b):
                    dve.wait_ge(sg["a_full"], fill_no("R1", b - 1))
                dve.tensor_copy(xnt[0][:, :, :], xnt_f[:, :, :]).then_inc(sg["xnt_hi_ready"], 1)
                dve.wait_ge(sg["xnt_hi_ready"], b + 1)
                lo(xnt[1][:, :, :], xnt_f[:, :, :], xnt[0][:, :, :]).then_inc(sg["xnt_lo_ready"], 1)

            def q_lo(b, i):
                dve.wait_ge(sg["qt_hi"], 2 * b + i + 1)
                sl = slice(4 * i, 4 * i + 4)
                lo(qt[1][:, sl, :].rearrange("p a n -> p (a n)"), bank(f"Q{i}")[:, 0:4 * N],
                   qt[0][:, sl, :].rearrange("p a n -> p (a n)")).then_inc(sg["qt_lo"], 1)

            def k_lo(b, p):
                dve.wait_ge(sg["kt_hi"], PAIRS * b + p + 1)
                lo(kt[1][:, p % 2, :], ps_o[:, 0:SKP], kt[0][:, p % 2, :]).then_inc(sg["kt_lo"], 1)

            def v_lo_cross(b, f):
                q, t = int(f[1]), int(f[2])
                dve.wait_ge(sg["v_hi"], v_no(f, b))
                lo(v[1][:, q, t, :], ps_v[0:SKT, :], v[0][:, q, t, :]).then_inc(sg["v_lo"], 1)

            def maxima(b, s):
                dve.wait_ge(sg["s_full"], PAIRS * b + s + 1)
                dve.reduce_max(c_max[:, s % 2, :], ps_s[0:N, :, 0:SK], X).then_inc(sg["c_max_ready"], 1)
                dve.wait_ge(sg["c_max_ready"], PAIRS * b + s + 1)
                dve.tensor_scalar(c_neg[:, s % 2, :], c_max[:, s % 2, :], -CROSS_SCALE, None, ALU.mult)\
                    .then_inc(sg["c_neg_ready"], 1)

            def rcp(b, s):
                dve.wait_ge(sg["c_exp"], 2 * (PAIRS * b + s) + 2)
                if later(PAIRS * b + s - 1):
                    dve.wait_ge(sg["p_normed"], PAIRS * b + s - 1)
                dve.reciprocal(c_rcp[:, s % 2, :], c_sum[:, s % 2, :]).then_inc(sg["c_rcp_ready"], 1)

            def cpt_lo(b, s):
                dve.wait_ge(sg["cpt_hi"], PAIRS * b + s + 1)
                dve.tensor_tensor(cpt[1][:, :, :, :].rearrange("p h t n -> p h (t n)"), ps_t[0:SKT, :, 0:ST * N],
                                  cpt[0][:, :, :, :].rearrange("p h t n -> p h (t n)").bitcast(F32), ALU.subtract)\
                    .then_inc(sg["cpt_lo"], 1)

            def o_lo(b, s):
                for h in range(2):
                    dve.wait_ge(sg["oct_hi"], 2 * (PAIRS * b + s) + h + 1)
                    r = slice(64 * h, 64 * h + 64)
                    lo(oct_[1][r, s, :], ps_o[r, h * N:(h + 1) * N], oct_[0][r, s, :]).then_inc(sg["oct_lo"], 1)

            def x2_moments(b):
                dve.wait_ge(sg["wo_full"], b + 1)
                dve.wait_ge(sg["x1_kept"], b + 1)
                dve.scalar_tensor_tensor(res2[:, :], ps_v[0:N, 0:D], gate[:, 0:1], x2_all[0:N, b, :],
                                         op0=ALU.mult, op1=ALU.add).then_inc(sg["res2"], 1)
                dve.wait_ge(sg["res2"], b + 1)
                moments(res2[:, :], stats2[:, :], mv2[:, :], "n3", b + 1)

            def x2_norm(b):
                norm(res2[:, :], x2_all[0:N, b, :], mv2[:, :], rstd2[:, :], "n3", b + 1).then_inc(sg["x2_ready"], 1)

            def fill_lo(b, f):
                if f[0] == "S":
                    self_max(b, int(f[1]))
                elif f[0] == "T":
                    self_pt(b, int(f[1]))
                elif f[0] == "O" and f != "OT":
                    o_norm(b, int(f[1]))
                elif f[0] == "C":
                    ctx_lo(b, int(f[1]))
                elif f == "OT":
                    ot_lo(b)
                elif f == "PJ":
                    residual_moments(b)
                elif f == "NT":
                    xnt_split(b)
                elif f in ("Q0", "Q1"):
                    q_lo(b, int(f[1]))

            for f in ("S0", "S1", "S2", "S3"):
                fill_lo(0, f)
            v_split(0)
            fill_lo(0, "T0")
            fill_lo(0, "T1")
            dve.wait_ge(sg["padded"], 2)
            fill_lo(0, "C0")
            fill_lo(0, "C1")
            fill_lo(0, "O0")
            fill_lo(0, "T2")
            fill_lo(0, "T3")
            k_lo(0, 0)
            fill_lo(0, "O1")
            v_lo_cross(0, "V00")
            k_lo(0, 1)
            v_lo_cross(0, "V01")
            fill_lo(0, "OT")
            fill_lo(0, "PJ")
            x1_moments(0)
            xn_norm(0)
            fill_lo(0, "NT")
            fill_lo(0, "Q0")
            fill_lo(0, "Q1")

            def iteration(b, more):
                for s in range(PAIRS):
                    def place(n):
                        if more:
                            for f in FILL_AT.get((s, n), ()):
                                fill_lo(b + 1, f)

                    maxima(b, s)
                    if more and s == 6:
                        xn_norm(b + 1)
                    if s >= 2:
                        cpt_lo(b, s - 2)
                    elif later(b):
                        cpt_lo(b - 1, s + 6)
                    place(0)
                    if s + 2 < PAIRS:
                        k_lo(b, s + 2)
                    elif more:
                        k_lo(b + 1, s + 2 - PAIRS)
                    if s != 3:
                        place(1)
                    rcp(b, s)
                    if s == 3:
                        place(1)
                    if s == 2 and later(b):
                        x2_moments(b - 1)
                    if s == 6:
                        place(2)
                    if s in V_AT and (s < 6 or more):
                        v_lo_cross(b if s < 6 else b + 1, V_AT[s])
                    if s != 6:
                        place(2)
                    if more and s == 0:
                        v_split(b + 1)
                    place(3)
                    if s >= 2:
                        o_lo(b, s - 2)
                    elif later(b):
                        o_lo(b - 1, s + 6)
                    if more and s == 5:
                        x1_moments(b + 1)
                    place(4)
                    if s == 2 and later(b):
                        x2_norm(b - 1)
            iterations(dve, iteration)
            cpt_lo(B - 1, 6)
            o_lo(B - 1, 6)
            cpt_lo(B - 1, 7)
            o_lo(B - 1, 7)
            x2_moments(B - 1)
            x2_norm(B - 1)
            dve.wait_ge(sg["x2_ready"], B)

        @block.tensor
        def _(pe):
            def free(name, b):
                i = FILLS.index(name)
                if name in ("PJ", "NT"):
                    pe.wait_ge(sg["ctxt_lo"], 2 * b + 1 + (name == "NT"))
                if i >= 2:
                    signal, per, which = LAST_READ[FILLS[i - 2]]
                    pe.wait_ge(sg[signal], per * b + which + 1)
                else:
                    last = [f for j, f in enumerate(FILLS) if j % 2 == i][-1]
                    signal, per, which = LAST_READ[last]
                    if later(b):
                        pe.wait_ge(sg[signal], per * (b - 1) + which + 1)

            def stacked_transpose(b, f):
                i, half = ("Q", "K").index(f[0]), ("A", "B").index(f[1])
                pe.wait_ge(sg["qk_lo"], 4 * b + 2 * i + 2)
                free(f, b)
                for j in range(4):
                    c = i * 1024 + (4 * half + j) * P
                    last = pe.transpose(bank(f)[:, j * N:(j + 1) * N], work[0:N, c:c + P], ident[0:N, 0:N])
                last.then_inc(sg["a_full"], 1)

            def self_scores(b, f):
                pe.wait_ge(sg["qk_stacked_t"], 4 * b + 4)
                free(f"S{f}", b)
                r = slice(64 * (f % 2), 64 * (f % 2) + 64)
                for j in range(4):
                    pr = 4 * (f // 2) + j
                    last = pe.matmul(bank(f"S{f}")[0:N, j * N:(j + 1) * N], qk_t[0][r, pr, :], qk_t[1][r, pr, :],
                                     start=True, stop=True)
                last.then_inc(sg["a_full"], 1)

            def self_pt(b, i):
                pe.wait_ge(sg["e_ready"], 2 * b + i // 2 + 1)
                free(f"T{i}", b)
                for j in range(4):
                    last = pe.transpose(bank(f"T{i}")[0:N, j * N:(j + 1) * N], e_self[:, 4 * i + j, :], ident[0:N, 0:N])
                last.then_inc(sg["a_full"], 1)

            def self_out(b, i):
                pe.wait_ge(sg["pt_lo"], 4 * b + 2 * i + 2)
                pe.wait_ge(sg["v_self_lo"], b + 1)
                if i == 0 and not later(b):
                    pe.wait_ge(sg["v_ones"], 2)
                free(f"O{i}", b)
                for j in range(8):
                    bb, r = 4 * i + j % 4, j // 4
                    out = bank(f"O{i}")[0:N, j * VW:(j + 1) * VW]
                    pe.matmul(out, pt[0][:, j, :], v_self[:, bb, r, :], start=True, stop=False)
                    last = pe.matmul(out[:, 0:VS], pt[1][:, j, :], v_self[:, bb, r, 0:VS], start=False, stop=True)
                last.then_inc(sg["a_full"], 1)

            def o_transpose(b):
                pe.wait_ge(sg["o_rows_loaded"], 16 * (b + 1))
                free("OT", b)
                for k in range(KD):
                    last = pe.transpose(bank("OT")[:, k * N:(k + 1) * N], o_rows[:, k * P:(k + 1) * P], ident[0:N, 0:N])
                last.then_inc(sg["a_full"], 1)

            def ctx_transpose(b, k):
                pe.wait_ge(sg["ctx_loaded"], 16 * (b + 1))
                if later(b):
                    if k == 0:
                        pe.wait_ge(sg["o_summed"], 2 * b + 2)
                    else:
                        pe.wait_ge(sg["ot_lo"], b + 1)
                for t in range(ST):
                    last = pe.transpose(ctx_bank(b, k)[:, t * SKT:(t + 1) * SKT], ctx_raw[:, t, k * P:(k + 1) * P],
                                        ident[0:SKT, 0:SKT])
                last.then_inc(sg["c_full"], 1)

            def out_project(b):
                pe.wait_ge(sg["ot_lo"], b + 1)
                free("PJ", b)
                product_over_width(pe, bank("PJ")[0:N, 0:D], ot, w_proj, slice(0, D)).then_inc(sg["a_full"], 1)

            def xn_transpose(b):
                pe.wait_ge(sg["xn_ready"], b + 1)
                free("NT", b)
                for k in range(KD):
                    last = pe.transpose(bank("NT")[:, k * N:(k + 1) * N], xn[:, k * P:(k + 1) * P], ident[0:N, 0:N])
                last.then_inc(sg["a_full"], 1)

            def q_project(b, i):
                pe.wait_ge(sg["xnt_lo_ready"], b + 1)
                free(f"R{i}", b)
                product_over_width(pe, bank(f"R{i}")[0:N, :], xnt, w_q, slice(512 * i, 512 * i + 512)).then_inc(sg["a_full"], 1)

            def q_transpose(b, i):
                pe.wait_ge(sg["q_rows"], 2 * b + i + 1)
                free(f"Q{i}", b)
                for j in range(4):
                    last = pe.transpose(bank(f"Q{i}")[:, j * N:(j + 1) * N], q_rows[:, i, j * P:(j + 1) * P], ident[0:N, 0:N])
                last.then_inc(sg["a_full"], 1)

            def k_project(b, p):
                pe.wait_ge(sg["ctxt_lo"], 2 * b + 2)
                if later(PAIRS * b + p):
                    pe.wait_ge(sg["kt_lo"], PAIRS * b + p)
                if later(PAIRS * b + p - 4):
                    pe.wait_ge(sg["oct_lo"], 2 * (PAIRS * b + p - 4))
                m = slice(p * P, (p + 1) * P)
                for k in range(KD):
                    last = product(pe, ps_o[:, 0:SKP], tuple(t[:, k, m] for t in w_k), tuple(t[:, k, :] for t in ctxt),
                                   start=k == 0, stop=k == KD - 1)
                last.then_inc(sg["k_full"], 1)

            def v_project(b, f):
                q, t = int(f[1]), int(f[2])
                if f == "V10" and later(b):
                    pe.wait_ge(sg["res2"], b)
                if later(v_no(f, b) - 1):
                    pe.wait_ge(sg["v_lo"], v_no(f, b) - 1)
                rows = slice(t * SKT, (t + 1) * SKT)
                for k in range(KD):
                    last = product(pe, ps_v[0:SKT, :], tuple(c[:, k, rows] for c in ctxt),
                                   tuple(w[:, k, 512 * q:512 * q + 512] for w in w_v), start=k == 0, stop=k == KD - 1)
                last.then_inc(sg["v_full"], 1)

            def scores(b, s):
                pe.wait_ge(sg["qt_lo"], 2 * b + 2)
                pe.wait_ge(sg["kt_lo"], PAIRS * b + s + 1)
                if later(2 * (PAIRS * b + s)):
                    pe.wait_ge(sg["c_exp"], 2 * (PAIRS * b + s))
                for h in range(2):
                    r = slice(64 * h, 64 * h + 64)
                    last = product(pe, ps_s[0:N, h, 0:SKP], tuple(t[r, s, :] for t in qt),
                                   tuple(t[r, s % 2, :] for t in kt))
                last.then_inc(sg["s_full"], 1)

            def p_transpose(b, s):
                pe.wait_ge(sg["p_normed"], PAIRS * b + s + 1)
                if later(PAIRS * b + s):
                    pe.wait_ge(sg["cpt_lo"], PAIRS * b + s)
                for h in range(2):
                    for t in range(ST):
                        last = pe.transpose(ps_t[0:SKT, h, t * N:(t + 1) * N],
                                            probs[:, s % 2, h, t * SKT:(t + 1) * SKT], ident[0:N, 0:N])
                last.then_inc(sg["t_full"], 1)

            def pv(b, s, k_done):
                pe.wait_ge(sg["cpt_lo"], PAIRS * b + s + 1)
                pe.wait_ge(sg["v_lo"], v_no("V02" if s < 4 else "V12", b))
                pe.wait_ge(sg["kt_lo"], k_done)
                if later(PAIRS * b + s):
                    pe.wait_ge(sg["oct_lo"], 2 * (PAIRS * b + s))
                c = slice((s % 4) * P, (s % 4 + 1) * P)
                for t in range(ST):
                    last = product(pe, ps_o[:, 0:2 * N], tuple(w[:, s // 4, t, c] for w in v),
                                   tuple(w[:, :, t, :] for w in cpt), start=t == 0, stop=t == ST - 1)
                last.then_inc(sg["pv_full"], 1)

            def cross_out(b):
                pe.wait_ge(sg["v_lo"], v_before_output(b))
                pe.wait_ge(sg["oct_lo"], 2 * PAIRS * (b + 1))
                for k in range(PAIRS):
                    last = product(pe, ps_v[0:N, 0:D], tuple(t[:, k, :] for t in oct_), tuple(t[:, k, :] for t in w_o),
                                   start=k == 0, stop=k == PAIRS - 1)
                last.then_inc(sg["wo_full"], 1)

            def fill(b, f):
                if f in ("QA", "QB", "KA", "KB"):
                    stacked_transpose(b, f)
                elif f[0] == "S":
                    self_scores(b, int(f[1]))
                elif f[0] == "T":
                    self_pt(b, int(f[1]))
                elif f == "OT":
                    o_transpose(b)
                elif f[0] == "O":
                    self_out(b, int(f[1]))
                elif f in ("C0", "C1"):
                    ctx_transpose(b, int(f[1]))
                elif f == "PJ":
                    out_project(b)
                elif f == "NT":
                    xn_transpose(b)
                elif f[0] == "R":
                    q_project(b, int(f[1]))
                else:
                    q_transpose(b, int(f[1]))

            for f in FILLS[:FILLS.index("T1") + 1] + ["C0", "C1", "O0", "T2"]:
                fill(0, f)
            k_project(0, 0)
            fill(0, "T3")
            fill(0, "O1")
            k_project(0, 1)
            v_project(0, "V00")
            v_project(0, "V01")
            fill(0, "OT")
            fill(0, "PJ")
            fill(0, "NT")
            for f in ("R0", "R1", "Q0", "Q1"):
                fill(0, f)

            def iteration(b, more):
                for s in range(PAIRS):
                    def place(n):
                        if more:
                            for f in FILL_AT.get((s, n), ()):
                                fill(b + 1, f)

                    k_done = PAIRS * b + min(s + 3, PAIRS if not more else s + 3)
                    scores(b, s)
                    place(0)
                    if s + 2 < PAIRS:
                        k_project(b, s + 2)
                    elif more:
                        k_project(b + 1, s + 2 - PAIRS)
                    place(1)
                    if s == 2 and later(b):
                        cross_out(b - 1)
                    if s != 2 and s in V_AT and (s < 6 or more):
                        v_project(b if s < 6 else b + 1, V_AT[s])
                    place(2)
                    if s >= 1:
                        p_transpose(b, s - 1)
                    elif later(b):
                        p_transpose(b - 1, 7)
                    if s == 2:
                        v_project(b, V_AT[s])
                    place(3)
                    if s >= 2:
                        pv(b, s - 2, k_done)
                    elif later(b):
                        pv(b - 1, s + 6, k_done)
                    place(4)
            iterations(pe, iteration)
            p_transpose(B - 1, 7)
            pv(B - 1, 6, PAIRS * B)
            pv(B - 1, 7, PAIRS * B)
            cross_out(B - 1)


def ffn_block(nc, sg, A, x2_all, ident, out):
    UNITS = 2 * MH
    with ExitStack() as ctx:
        def sb(name, shape, dt=F32):
            return ctx.enter_context(nc.sbuf_tensor(name, shape, dt))

        def pair(name, shape):
            return split_pair(nc, ctx, name, shape)


        raw = sb("ffn_raw", [P, MH, 6, P])
        w = pair("ffn_w", [P, MH, 6, P])
        x2t = pair("x2t", [P, KD, TOK])
        gw_raw = sb("gw_raw", [P, KD, EXP])
        gw = pair("gw", [P, KD, EXP])
        logits = sb("logits", [N, B, EXP])
        top = sb("top", [N, B, 8])
        top_i = sb("top_i", [N, B, 8], U32)
        top_f = sb("top_f", [N, B, 2])
        gap = sb("gap", [N, B])
        gap_e = sb("gap_e", [N, B])
        w_top = sb("w_top", [N, 2, B])
        eid = sb("eid", [N, EXP])
        pick = sb("pick", [N, 2, B, EXP])
        w_tok = sb("w_tok", [N, B, EXP])
        w_bc = sb("w_bc", [P, EXP, TOK])
        s_act = sb("s_act", [P, 2, HALF])
        g = sb("g", [P, 2, HALF])
        gs = pair("gs", [P, 2, HALF])
        y_sb = sb("y_sb", [P, KD, TOK])
        res = sb("ffn_res", [N, B, D])
        stats = sb("ffn_stats", [N, B, 6])
        mv = sb("ffn_mv", [N, B, 2])
        rstd = sb("ffn_rstd", [N, B])
        var = sb("ffn_var", [N, B])
        neg_half = sb("ffn_neg_half", [N, B])
        y_out = sb("y_out", [N, B, D])

        ps_y = ctx.enter_context(nc.psum_tensor("ps_y", [P, 4, 512], F32))
        ps_h = ctx.enter_context(nc.psum_tensor("ps_h", [P, 4, 512], F32))
        block = ctx.enter_context(nc.Block())

        def half(i):
            return slice(i * HALF, (i + 1) * HALF)

        @block.sync
        def _(sp):
            def load(w1, w2, w3):
                for i, src in ((0, w1), (2, w2)):
                    for k in range(KD):
                        sp.dma_start(raw[:, :, i + k, :], src[k * P:(k + 1) * P, :].rearrange("p (m c) -> p m c", m=MH))\
                            .then_inc(sg["raw_loaded"], 16)
                sp.dma_start(raw[:, :, 4:6, :].rearrange("p m o c -> p m (o c)"),
                             w3.rearrange("(m p) d -> p m d", p=P)).then_inc(sg["raw_loaded"], 16)

            sp.dma_start(gw_raw[:, :, :], A["gate_w"].rearrange("(k p) e -> p k e", p=P)).then_inc(sg["gw_loaded"], 16)
            load(A["sw1"], A["sw2"], A["sw3"])

            def expert_load(e):
                sp.wait_ge(sg["w_lo"], MH * e)
                load(*(A[n][bass.ds(e - 1, 1)].rearrange("a d h -> (a d) h") for n in ("ew1", "ew2", "ew3")))
            with sp.Fori(1, EXP + 1) as e:
                expert_load(e)
            for b in range(B):
                sp.wait_ge(sg["y_ready"], b + 1)
                sp.dma_start(out[b], y_out[:, b, :]).then_inc(sg["stored"], 16)
            sp.wait_ge(sg["stored"], 16 * B)

        def split_at(j):
            return {0: (0, 2), 2: (0, 3), 4: (1, 0), 6: (1, 1)}.get(j)

        def unit_no(e, j):
            return UNITS * e + j

        def w_split_free(eng, e, m):
            eng.wait_ge(sg["down_done"], unit_no(e - 1, 2 * m + 1) + 1)

        @block.gpsimd
        def _(pool):
            pool.iota(top_i[:, 0, :], [[1, EXP]], base=0, channel_multiplier=0).then_inc(sg["iota"], 1)
            pool.wait_ge(sg["iota"], 1)
            pool.memset(neg_half[:, :], -0.5).then_inc(sg["iota"], 1)
            pool.wait_ge(sg["iota"], 2)
            pool.tensor_copy(eid[:, :], top_i[:, 0, :]).then_inc(sg["eid_ready"], 1)

            def unit(e, j):
                u = unit_no(e, j)
                if later(e):
                    pool.wait_ge(sg["g_ready"], u + 1)
                    pool.wait_ge(sg["w_bc_ready"], 2 * EXP)
                    pool.nop(nofuse=True)
                    pool.tensor_tensor(g[:, j % 2, :], g[:, j % 2, :], w_bc[:, e - 1, half(j % 2)], ALU.mult)\
                        .then_inc(sg["g_weighted"], 1)
                pool.wait_ge(sg["g_hi"], u + 1)
                pool.tensor_tensor(gs[1][:, j % 2, :], g[:, j % 2, :], gs[0][:, j % 2, :].bitcast(F32), ALU.subtract)\
                    .then_inc(sg["g_lo"], 1)

            def expert(e):
                for j in range(UNITS):
                    unit(e, j)
            expert(0)
            with pool.Fori(1, EXP + 1) as e:
                expert(e)
            pool.wait_ge(sg["y_var"], 1)
            pool.tensor_tensor(rstd[:, :], var[:, :], neg_half[:, :], ALU.pow).then_inc(sg["y_rstd"], 1)

        @block.scalar
        def _(act):
            def hi(dst, src):
                return act.activation(dst, src, ACT.Copy)

            for i in range(4):
                k, hf = i // 2, i % 2
                act.wait_ge(sg["x2t_full"], i + 1)
                hi(x2t[0][:, k, half(hf)], ps_h[:, i, 0:HALF]).then_inc(sg["x2t_hi"], 1)
            act.wait_ge(sg["gw_loaded"], 16)
            hi(gw[0][:, :, :], gw_raw[:, :, :]).then_inc(sg["gw_hi"], 1)
            act.wait_ge(sg["raw_loaded"], 80)
            for m in range(MH):
                hi(w[0][:, m], raw[:, m]).then_inc(sg["w_hi"], 1)
            act.wait_ge(sg["gap_ready"], 1)
            act.activation(gap_e[:, :], gap[:, :], ACT.Exp).then_inc(sg["gap_exp"], 1)

            def unit(e, j, more):
                u = unit_no(e, j)
                act.wait_ge(sg["h_full"], u + 1)
                if later(u - 1):
                    act.wait_ge(sg["g_ready"], u - 1)
                act.activation(s_act[:, j % 2, :], ps_h[:, 2 * (j % 2), 0:HALF], ACT.Silu).then_inc(sg["silu"], 1)
                sp = split_at(j)
                if sp and (sp[0] == 0 or more) and (sp[0] == 1 or later(e)):
                    en, m = e + sp[0], sp[1]
                    act.wait_ge(sg["raw_loaded"], 80 * (en + 1))
                    w_split_free(act, en, m)
                    hi(w[0][:, m], raw[:, m]).then_inc(sg["w_hi"], 1)
                if later(e):
                    act.wait_ge(sg["g_weighted"], unit_no(e - 1, j) + 1)
                else:
                    act.wait_ge(sg["g_ready"], u + 1)
                if later(u - 1):
                    act.wait_ge(sg["down_done"], u - 1)
                hi(gs[0][:, j % 2, :], g[:, j % 2, :]).then_inc(sg["g_hi"], 1)

            def expert(e, more=True):
                for j in range(UNITS):
                    unit(e, j, more)
            expert(0)
            for f in range(EXP * 2):
                act.wait_ge(sg["wt_full"], f + 1)
                act.activation(w_bc[:, f // 2, half(f % 2)], ps_h[:, f % 4, 0:HALF], ACT.Copy).then_inc(sg["w_bc_ready"], 1)
            with act.Fori(1, EXP) as e:
                expert(e)
            expert(EXP, False)
            for i in range(4):
                act.wait_ge(sg["y_done"], 1)
                act.activation(y_sb[:, i // 2, half(i % 2)], ps_y[:, i, 0:HALF], ACT.Copy).then_inc(sg["y_copied"], 1)

        @block.vector
        def _(dve):
            def lo(dst, src, part):
                return dve.tensor_tensor(dst, src, part.bitcast(F32), ALU.subtract)

            for i in range(4):
                k, hf = i // 2, i % 2
                dve.wait_ge(sg["x2t_hi"], i + 1)
                lo(x2t[1][:, k, half(hf)], ps_h[:, i, 0:HALF], x2t[0][:, k, half(hf)]).then_inc(sg["x2t_lo"], 1)
            dve.wait_ge(sg["gw_hi"], 1)
            lo(gw[1][:, :, :], gw_raw[:, :, :], gw[0][:, :, :]).then_inc(sg["gw_lo"], 1)
            for m in range(MH):
                dve.wait_ge(sg["w_hi"], m + 1)
                lo(w[1][:, m], raw[:, m], w[0][:, m]).then_inc(sg["w_lo"], 1)

            dve.wait_ge(sg["eid_ready"], 1)
            dve.wait_ge(sg["logits_full"], 1)
            dve.tensor_copy(logits[:, :, :].rearrange("p b e -> p (b e)"), ps_y[0:N, 0, 0:B * EXP]).then_inc(sg["gating"], 1)
            dve.wait_ge(sg["gating"], 1)
            for b in range(B):
                dve.max(top[:, b, :], logits[:, b, :]).then_inc(sg["top_ready"], 1)
                dve.wait_ge(sg["top_ready"], b + 1)
                dve.max_index(top_i[:, b, :], top[:, b, :], logits[:, b, :]).then_inc(sg["gating"], 1)
            dve.wait_ge(sg["gating"], 1 + B)
            dve.tensor_copy(top_f[:, :, :], top_i[:, :, 0:2]).then_inc(sg["gating"], 1)
            dve.tensor_tensor(gap[:, :], top[:, :, 1], top[:, :, 0], ALU.subtract).then_inc(sg["gap_ready"], 1)
            dve.wait_ge(sg["gap_exp"], 1)
            dve.tensor_scalar(w_top[:, 0, :], gap_e[:, :], 1.0, None, ALU.add).then_inc(sg["gating"], 1)
            dve.wait_ge(sg["gating"], 3 + B)
            dve.reciprocal(w_top[:, 0, :], w_top[:, 0, :]).then_inc(sg["gating"], 1)
            dve.wait_ge(sg["gating"], 4 + B)
            dve.tensor_tensor(w_top[:, 1, :], w_top[:, 0, :], gap_e[:, :], ALU.mult).then_inc(sg["gating"], 1)
            for c in range(2):
                dve.tensor_tensor(pick[:, c], eid[:, :].unsqueeze(1).to_broadcast([N, B, EXP]),
                                  top_f[:, :, c].unsqueeze(2).to_broadcast([N, B, EXP]), ALU.is_equal)\
                    .then_inc(sg["gating"], 1)
            dve.wait_ge(sg["gating"], 7 + B)
            for c in range(2):
                dve.tensor_tensor(pick[:, c], pick[:, c], w_top[:, c, :].unsqueeze(2).to_broadcast([N, B, EXP]), ALU.mult)\
                    .then_inc(sg["gating"], 1)
            dve.wait_ge(sg["gating"], 9 + B)
            dve.tensor_tensor(w_tok[:, :, :], pick[:, 0], pick[:, 1], ALU.add).then_inc(sg["w_tok_ready"], 1)

            def unit(e, j, more):
                u = unit_no(e, j)
                dve.wait_ge(sg["silu"], u + 1)
                if later(u - 1):
                    dve.wait_ge(sg["g_lo"], u - 1)
                dve.tensor_tensor(g[:, j % 2, :], s_act[:, j % 2, :], ps_h[:, 2 * (j % 2) + 1, 0:HALF], ALU.mult)\
                    .then_inc(sg["g_ready"], 1)
                sp = split_at(j)
                if sp and (sp[0] == 0 or more) and (sp[0] == 1 or later(e)):
                    en, m = e + sp[0], sp[1]
                    dve.wait_ge(sg["w_hi"], MH * en + m + 1)
                    lo(w[1][:, m], raw[:, m], w[0][:, m]).then_inc(sg["w_lo"], 1)

            def expert(e, more=True):
                for j in range(UNITS):
                    unit(e, j, more)
            expert(0)
            with dve.Fori(1, EXP) as e:
                expert(e)
            expert(EXP, False)

            for b in range(B):
                dve.wait_ge(sg["yt_full"], b + 1)
                dve.tensor_tensor(res[:, b, :], ps_h[0:N, b % 4, 0:D], x2_all[0:N, b, :], ALU.add).then_inc(sg["y_res"], 1)
                dve.wait_ge(sg["y_res"], b + 1)
                dve.bn_stats(stats[:, b, :], res[:, b, :]).then_inc(sg["y_stats"], 1)
            for b in range(B):
                dve.wait_ge(sg["y_stats"], b + 1)
                dve.bn_aggr(mv[:, b, :], stats[:, b, :]).then_inc(sg["y_aggr"], 1)
            dve.wait_ge(sg["y_aggr"], B)
            dve.tensor_scalar(var[:, :], mv[:, :, 1], EPS, None, ALU.add).then_inc(sg["y_var"], 1)
            dve.wait_ge(sg["y_rstd"], 1)
            for b in range(B):
                dve.tensor_scalar(y_out[:, b, :], res[:, b, :], mv[:, b, 0:1], rstd[:, b:b + 1], ALU.subtract, ALU.mult)\
                    .then_inc(sg["y_ready"], 1)

        @block.tensor
        def _(pe):
            for i in range(4):
                k, hf = i // 2, i % 2
                for j in range(4):
                    last = pe.transpose(ps_h[:, i, j * N:(j + 1) * N], x2_all[0:N, 4 * hf + j, k * P:(k + 1) * P],
                                        ident[0:N, 0:N])
                last.then_inc(sg["x2t_full"], 1)
            pe.wait_ge(sg["x2t_lo"], 4)
            pe.wait_ge(sg["gw_lo"], 1)
            for b in range(B):
                t = slice(b * N, (b + 1) * N)
                for k in range(KD):
                    last = product(pe, ps_y[0:N, 0, b * EXP:(b + 1) * EXP], tuple(c[:, k, t] for c in x2t),
                                   tuple(c[:, k, :] for c in gw), start=k == 0, stop=k == KD - 1)
            last.then_inc(sg["logits_full"], 1)

            def up(e, j):
                u, m = unit_no(e, j), j // 2
                pe.wait_ge(sg["w_lo"], MH * e + m + 1)
                if later(u - 1):
                    pe.wait_ge(sg["g_ready"], u - 1)
                for i in range(2):
                    for k in range(KD):
                        last = product(pe, ps_h[:, 2 * (j % 2) + i, 0:HALF], tuple(c[:, m, 2 * i + k, :] for c in w),
                                       tuple(c[:, k, half(j % 2)] for c in x2t), start=k == 0, stop=k == KD - 1)
                last.then_inc(sg["h_full"], 1)

            def down(e, j, first=False, final=False):
                u, m = unit_no(e, j), j // 2
                pe.wait_ge(sg["g_lo"], u + 1)
                if first:
                    pe.wait_ge(sg["gating"], 1)
                for o in range(2):
                    last = product(pe, ps_y[:, 2 * o + j % 2, 0:HALF], tuple(c[:, m, 4 + o, :] for c in w),
                                   tuple(c[:, j % 2, :] for c in gs), start=first, stop=final, skip_group_check=True)
                last.then_inc(sg["down_done"], 1)

            def expert(e):
                for j in range(UNITS):
                    up(e, j)
                    if j >= 2:
                        down(e, j - 2, first=isinstance(e, int) and e == 0 and j < 4)
                    elif later(e - 1):
                        down(e - 1, j + UNITS - 2)

            expert(0)
            down(0, UNITS - 2)
            down(0, UNITS - 1)
            pe.wait_ge(sg["w_tok_ready"], 1)
            pe.wait_ge(sg["g_ready"], UNITS)
            for f in range(EXP * 2):
                if later(f - 3):
                    pe.wait_ge(sg["w_bc_ready"], f - 3)
                for i in range(4):
                    b = 4 * (f % 2) + i
                    last = pe.transpose(ps_h[:, f % 4, i * N:(i + 1) * N],
                                        w_tok[:, b, f // 2:f // 2 + 1].to_broadcast([N, P]), ident[0:N, 0:N])
                last.then_inc(sg["wt_full"], 1)
            pe.wait_ge(sg["w_bc_ready"], 2 * EXP)
            expert(1)
            with pe.Fori(2, EXP + 1) as e:
                expert(e)
            for j in (UNITS - 2, UNITS - 1):
                down(EXP, j, final=True)
            pe.wait_ge(sg["down_done"], UNITS * (EXP + 1))
            pe.transpose(ps_h[0:N, 3, 0:N], ident[0:N, 0:N], ident[0:N, 0:N]).then_inc(sg["y_done"], 1)
            pe.wait_ge(sg["y_copied"], 4)
            for b in range(B):
                if later(b - 3):
                    pe.wait_ge(sg["y_res"], b - 3)
                for k in range(KD):
                    last = pe.transpose(ps_h[0:N, b % 4, k * P:(k + 1) * P], y_sb[:, k, b * N:(b + 1) * N], ident[:, :])
                last.then_inc(sg["yt_full"], 1)


def decoder_layer(nc, A, out):
    with ExitStack() as outer:
        x2_all = outer.enter_context(nc.sbuf_tensor("x2_all", [P, B, D], F32))
        ident = outer.enter_context(nc.sbuf_tensor("ident", [P, P], F32))
        signals = [Signals(nc, outer, block) for block in ("prep", "attn", "ffn")]
        with ExitStack() as ctx:
            consts = {n: ctx.enter_context(nc.sbuf_tensor("const_" + n, shape, F32)) for n, shape in
                      (("proj_b", [N, D]), ("b_out", [N, D]), ("gate", [N, 1]), ("neg_half", [N, 1]),
                       ("gamma", [P, KD]), ("beta", [P, KD]))}
            weights = [split_pair(nc, ctx, name, shape) for name, shape in
                       (("w_k", [P, KD, INNER]), ("w_v", [P, KD, INNER]), ("w_q", [P, KD, INNER]),
                        ("w_o", [P, PAIRS, D]), ("w_proj", [P, KD, D]))]
            qk_rot = ctx.enter_context(nc.sbuf_tensor("qk_rot", [N, B, 2 * D], F32))
            v_all = ctx.enter_context(nc.sbuf_tensor("v_all", [N, B, D], F32))
            preparation_block(nc, signals[0], A, ident, consts, weights, qk_rot, v_all)
            attention_block(nc, signals[1], A, x2_all, ident, consts, weights, qk_rot, v_all)
        ffn_block(nc, signals[2], A, x2_all, ident, out)


def rope_table():
    inv = (np.float32(1.0) / np.float32(10000.0) ** (np.arange(0, HD, 2, dtype=np.float32) / np.float32(HD))).astype(np.float32)
    f = np.arange(N, dtype=np.float32)[:, None] * inv[None, :]
    cos, sin = np.cos(f), np.sin(f)
    return np.stack([np.concatenate([cos, cos], 1), np.concatenate([-sin, sin], 1)], 1).astype(np.float32)


_INS = {"x": "x", "ctx_1024": "ctx", "L0_attn_qkv_w": "qkv_w", "L0_attn_qkv_b": "qkv_b", "L0_attn_proj_w": "proj_w",
        "L0_attn_proj_b": "proj_b", "L0_xattn_ln_gamma": "gamma", "L0_xattn_ln_beta": "beta", "L0_xattn_w_q": "w_q",
        "L0_xattn_w_kv": "w_kv", "L0_xattn_w_out": "w_out", "L0_xattn_b_out": "b_out", "L0_xattn_gate": "gate",
        "L0_ffn_gate_w": "gate_w", "L0_ffn_ew1": "ew1", "L0_ffn_ew2": "ew2", "L0_ffn_ew3": "ew3",
        "L0_ffn_sw1": "sw1", "L0_ffn_sw2": "sw2", "L0_ffn_sw3": "sw3"}


def kernel(**inputs):
    import concourse.bacc as _bacc
    from concourse import mybir as _mybir
    from concourse.bass_utils import run_bass_kernel_spmd as _run

    nc = _bacc.Bacc("TRN2", target_bir_lowering=False, num_devices=1)
    arrays, args = {}, {}
    for name, short in _INS.items():
        a = np.ascontiguousarray(inputs[name])
        arrays[f"in_{name}_dram"] = a
        args[short] = nc.dram_tensor(f"in_{name}_dram", a.shape, _mybir.dt.from_np(a.dtype), kind="ExternalInput").ap()
    table = rope_table()
    arrays["in_rope_dram"] = table
    args["rope"] = nc.dram_tensor("in_rope_dram", table.shape, _mybir.dt.from_np(table.dtype), kind="ExternalInput").ap()
    out = nc.dram_tensor("out_0_dram", (B, N, D), _mybir.dt.from_np(np.dtype("float32")), kind="ExternalOutput").ap()
    decoder_layer(nc, args, out)
    r = _run(nc, [arrays], core_ids=[0])
    return r.results[0]["out_0_dram"]
```

```python
from contextlib import ExitStack

import numpy as np

import concourse.bass as bass
from concourse import mybir

F32 = mybir.dt.float32
F32R = mybir.dt.float32r
U32 = mybir.dt.uint32
ALU = mybir.AluOpType
ACT = mybir.ActivationFunctionType
X = mybir.AxisListType.X

B, N, D = 8, 112, 256
P = 128
KD = D // P
H, HD = 16, 16
CH, CHD = 16, 64
INNER = CH * CHD
SK, ST = 375, 3
SKT = SK // ST
SKP = SK + 1
PAIRS = CH // 2
EXP = 8
HID = 2 * D
MH = HID // P
TOK = B * N
HALF = TOK // 2
VS = HD + 2
VW = VS + HD
EPS = 1e-5
SELF_SCALE = float(HD) ** -0.5
CROSS_SCALE = float(CHD) ** -0.5

FILLS = ["QA", "QB", "KA", "KB", "S0", "S1", "S2", "S3", "T0", "T1", "O0", "T2", "T3", "O1",
         "OT", "PJ", "NT", "R0", "R1", "Q0", "Q1"]
LAST_READ = {
    "QA": ("qk_stacked_t", 4, 0), "QB": ("qk_stacked_t", 4, 1), "KA": ("qk_stacked_t", 4, 2),
    "KB": ("qk_stacked_t", 4, 3),
    "S0": ("e_ready", 4, 0), "S1": ("e_ready", 4, 1), "S2": ("e_ready", 4, 2), "S3": ("e_ready", 4, 3),
    "T0": ("pt_lo", 4, 0), "T1": ("pt_lo", 4, 1), "T2": ("pt_lo", 4, 2), "T3": ("pt_lo", 4, 3),
    "O0": ("o_summed", 2, 0), "O1": ("o_summed", 2, 1), "OT": ("ot_lo", 1, 0),
    "PJ": ("res1", 1, 0),
    "NT": ("xn_affine", 2, 1), "R0": ("q_rows", 2, 0), "R1": ("q_rows", 2, 1), "Q0": ("qt_lo", 2, 0), "Q1": ("qt_lo", 2, 1),
}
V_FILLS = ["V00", "V01", "V02", "V10", "V11", "V12"]
FILL_AT = {(0, 2): ["QA"], (0, 3): ["QB"], (0, 4): ["KA"], (1, 0): ["KB"], (1, 2): ["S0"], (1, 3): ["S1"],
           (2, 0): ["S2"], (2, 1): ["S3"], (2, 3): ["T0"], (2, 4): ["T1"], (3, 1): ["O0", "T2"],
           (3, 2): ["T3"], (3, 4): ["O1"], (5, 1): ["OT", "C0"], (5, 3): ["C1", "PJ"],
           (6, 3): ["NT"], (7, 0): ["R0", "R1"], (7, 1): ["Q0"], (7, 2): ["Q1"]}
V_AT = {0: "V02", 2: "V10", 3: "V11", 4: "V12", 6: "V00", 7: "V01"}


def fill_no(name, b):
    return len(FILLS) * b + FILLS.index(name) + 1


def v_no(name, b):
    return len(V_FILLS) * b + V_FILLS.index(name) + 1


def v_before_output(b):
    return v_no("V02", b + 1) if not isinstance(b, int) or b + 1 < B else v_no("V12", b)


class Signals:

    def __init__(self, nc, ctx, block):
        self.nc, self.ctx, self.block, self.sems = nc, ctx, block, {}

    def __getitem__(self, name):
        if name not in self.sems:
            self.sems[name] = self.ctx.enter_context(self.nc.semaphore(self.block + "_" + name))
        return self.sems[name]


def later(count):
    return not isinstance(count, int) or count > 0


def product(eng, out, lhs, rhs, start=True, stop=True, **kw):
    (lh, ll), (rh, rl) = lhs, rhs
    eng.matmul(out, ll, rh, start=start, stop=False, **kw)
    eng.matmul(out, lh, rl, start=False, stop=False, **kw)
    return eng.matmul(out, lh, rh, start=False, stop=stop, **kw)


def split_pair(nc, ctx, name, shape):
    return tuple(ctx.enter_context(nc.sbuf_tensor(f"{name}_{part}", shape, F32R)) for part in ("hi", "lo"))


def product_over_width(pe, out, lhs, w, cols):
    for k in range(KD):
        last = product(pe, out, tuple(t[:, k, :] for t in lhs), tuple(t[:, k, cols] for t in w),
                       start=k == 0, stop=k == KD - 1)
    return last


def preparation_block(nc, sg, A, ident, consts, weights, qk_rot, v_all):
    w_k, w_v, w_q, w_o, w_proj = weights
    with ExitStack() as ctx:
        def sb(name, shape, dt=F32):
            return ctx.enter_context(nc.sbuf_tensor(name, shape, dt))

        w_qkv = split_pair(nc, ctx, "w_qkv", [P, KD, 3 * D])
        raw = sb("raw", [P, 8, D])
        rope_sb = sb("rope_sb", [N, 2, HD])
        bias_qkv = sb("bias_qkv", [N, 3 * D])
        x_in = sb("x_in", [N, B, D])
        xt = [split_pair(nc, ctx, f"xt{i}", [P, KD, N]) for i in range(2)]
        qk = sb("qk", [N, 2, 2 * D])
        sin_part = sb("sin_part", [N, 2, 2 * D])
        ps_w = ctx.enter_context(nc.psum_tensor("ps_w", [P, 2, 512], F32))
        ps_x = ctx.enter_context(nc.psum_tensor("ps_x", [P, 2, 512], F32))
        ps_qk = ctx.enter_context(nc.psum_tensor("ps_qk", [P, 2, 512], F32))
        ps_v = ctx.enter_context(nc.psum_tensor("ps_v", [P, 2, 512], F32))
        plain = [(w_o, A["w_out"]), (w_k, A["w_kv"][:, 0:INNER]), (w_v, A["w_kv"][:, INNER:2 * INNER]), (w_q, A["w_q"])]
        plain_raw = [sb(f"plain_raw{i}", [P, 2048]) for i in range(4)]
        heads, hw = 2 * H, HD // 2

        def plain_parts(i, half):
            (hi_w, lo_w), _ = plain[i]
            cols = slice(1024 * half, 1024 * half + 1024)
            return (lo_w[:, :, :].rearrange("p k n -> p (k n)")[:, cols], plain_raw[i][:, cols],
                    hi_w[:, :, :].rearrange("p k n -> p (k n)")[:, cols].bitcast(F32))

        block = ctx.enter_context(nc.Block())

        @block.sync
        def _(sp):
            sp.dma_start(raw[:, 0:6, :], A["qkv_w"].rearrange("(o p) d -> p o d", p=P)).then_inc(sg["raw0"], 16)
            for i, entries in enumerate((slice(0, 2), slice(2, B))):
                sp.dma_start(x_in[:, entries, :], A["x"][entries].rearrange("b n d -> n b d")).then_inc(sg[f"x_loaded{i}"], 16)
            for i, (_, src) in enumerate(plain):
                src = src.rearrange("(k p) n -> p k n", p=P)
                sp.dma_start(plain_raw[i][:, :].rearrange("p (k n) -> p k n", k=src.shape[1]), src)\
                    .then_inc(sg[f"plain{i}"], 16)
            sp.dma_start(raw[:, 6:8, :], A["proj_w"].rearrange("(o p) d -> p o d", p=P)).then_inc(sg["raw1"], 16)

        @block.gpsimd
        def _(pool):
            def plain_lo(i, half):
                dst, src, part = plain_parts(i, half)
                pool.wait_ge(sg["plain_hi"], i + 1)
                pool.tensor_tensor(dst, src, part, ALU.subtract).then_inc(sg["plain_lo"], 1)

            pool.dma_start(rope_sb[:, :, :], A["rope"]).then_inc(sg["consts"], 16)
            pool.dma_start(bias_qkv[:, :], A["qkv_b"].partition_broadcast(N)).then_inc(sg["consts"], 16)
            pool.memset(ident[:, :], 0.0).then_inc(sg["zeroed"], 1)
            pool.wait_ge(sg["zeroed"], 1)
            pool.affine_select(out=ident[:, :], in_=ident[:, :], compare_op=ALU.not_equal, fill=1.0, base=0,
                               pattern=[[-1, P]], channel_multiplier=1).then_inc(sg["ident"], 1)
            for name in ("proj_b", "b_out", "gate"):
                pool.dma_start(consts[name][:, :], A[name].partition_broadcast(N)).then_inc(sg["consts2"], 16)
            for name in ("gamma", "beta"):
                pool.dma_start(consts[name][:, :], A[name].rearrange("(k p) -> p k", p=P),
                               allow_slow_non_contiguous=True).then_inc(sg["consts2"], 16)
            pool.memset(consts["neg_half"][:, :], -0.5).then_inc(sg["neg_half"], 1)
            pool.wait_ge(sg["consts"], 32)
            for b0 in range(B // 2):
                for i in range(2):
                    pool.wait_ge(sg["qk_biased"], 2 * b0 + i + 1)
                    if later(b0):
                        pool.wait_ge(sg["rotated"], 2 * b0 + i - 1)
                    t = qk[:, i, :].rearrange("p (h w) -> p h w", w=HD)
                    out = sin_part[:, i, :].rearrange("p (h w) -> p h w", w=HD)
                    for dst, src in ((0, hw), (hw, 0)):
                        sin = rope_sb[:, 1, dst:dst + hw].unsqueeze(1).to_broadcast([N, heads, hw])
                        pool.tensor_tensor(out[:, :, dst:dst + hw], t[:, :, src:src + hw], sin, ALU.mult)\
                            .then_inc(sg["sin_part"], 1)
                if b0 in (1, 2):
                    plain_lo(0, b0 - 1)
            for half in range(2):
                plain_lo(1, half)
            pool.wait_ge(sg["consts2"], 5 * 16)

        @block.scalar
        def _(act):
            def hi(dst, src):
                return act.activation(dst, src, ACT.Copy)

            def xt_hi(b, i):
                act.wait_ge(sg["xt_full"], b + 1)
                if later(b - 1):
                    act.wait_ge(sg["v_full"], b - 1)
                hi(xt[i][0][:, :, :].rearrange("p k n -> p (k n)"), ps_x[:, i, 0:KD * N]).then_inc(sg["xt_hi"], 1)

            for i in range(4):
                k, half = i % 2, i // 2
                act.wait_ge(sg["w_full"], i + 1)
                if half == 0:
                    hi(w_qkv[0][:, k, 0:512], ps_w[:, k, :]).then_inc(sg["w_hi"], 1)
                else:
                    hi(w_qkv[0][:, k, 512:768], ps_w[:, k, 0:256]).then_inc(sg["w_hi"], 1)
            def plain_hi(i):
                (w, _), _ = plain[i]
                act.wait_ge(sg[f"plain{i}"], 16)
                hi(w[:, :, :].rearrange("p k n -> p (k n)"), plain_raw[i][:, :]).then_inc(sg["plain_hi"], 1)

            for b0 in range(B // 2):
                for i in range(2):
                    xt_hi(2 * b0 + i, i)
                if b0 >= 1:
                    plain_hi(b0 - 1)
            plain_hi(3)
            for k in range(KD):
                act.wait_ge(sg["w_full"], 5 + k)
                hi(w_proj[0][:, k, :], ps_w[:, k, 256:512]).then_inc(sg["w_hi"], 1)
            act.wait_ge(sg["consts2"], 5 * 16)
            act.activation(consts["gate"][:, :], consts["gate"][:, :], ACT.Tanh).then_inc(sg["gate_ready"], 1)

        @block.vector
        def _(dve):
            def lo(dst, src, part):
                return dve.tensor_tensor(dst, src, part.bitcast(F32), ALU.subtract)

            for i in range(4):
                k, half = i % 2, i // 2
                cols = slice(512 * half, 512 * half + 512 // (1 + half))
                dve.wait_ge(sg["w_hi"], i + 1)
                lo(w_qkv[1][:, k, cols], ps_w[:, k, 0:512 // (1 + half)], w_qkv[0][:, k, cols]).then_inc(sg["wt_lo"], 1)

            def xt_lo(b, i):
                dve.wait_ge(sg["xt_hi"], b + 1)
                lo(xt[i][1][:, :, :].rearrange("p k n -> p (k n)"), ps_x[:, i, 0:KD * N],
                   xt[i][0][:, :, :].rearrange("p k n -> p (k n)")).then_inc(sg["xt_lo"], 1)

            def add_bias(b, i):
                dve.wait_ge(sg["qk_full"], b + 1)
                dve.tensor_tensor(qk[:, i, :], ps_qk[0:N, i, :], bias_qkv[:, 0:2 * D], ALU.add)\
                    .then_inc(sg["qk_biased"], 1)
                dve.wait_ge(sg["v_full"], b + 1)
                dve.tensor_tensor(v_all[:, b, :], ps_v[0:N, i, 0:D], bias_qkv[:, 2 * D:3 * D], ALU.add)\
                    .then_inc(sg["v_biased"], 1)

            def rotate(b, i):
                cos = rope_sb[:, 0, :].unsqueeze(1).to_broadcast([N, heads, HD])
                dve.wait_ge(sg["sin_part"], 2 * b + 2)
                dve.tensor_tensor(qk[:, i, :].rearrange("p (h w) -> p h w", w=HD),
                                  qk[:, i, :].rearrange("p (h w) -> p h w", w=HD), cos, ALU.mult)\
                    .then_inc(sg["cos_part"], 1)
                dve.wait_ge(sg["cos_part"], b + 1)
                dve.tensor_tensor(qk_rot[:, b, :], qk[:, i, :], sin_part[:, i, :], ALU.add).then_inc(sg["rotated"], 1)

            def plain_lo(i, half):
                dst, src, part = plain_parts(i, half)
                dve.wait_ge(sg["plain_hi"], i + 1)
                dve.tensor_tensor(dst, src, part, ALU.subtract).then_inc(sg["plain_lo"], 1)

            xt_lo(0, 0)
            xt_lo(1, 1)
            dve.wait_ge(sg["consts"], 32)
            for b0 in range(B // 2):
                for i in range(2):
                    add_bias(2 * b0 + i, i)
                if b0 < B // 2 - 1:
                    for i in range(2):
                        xt_lo(2 * b0 + 2 + i, i)
                if b0 >= 2:
                    plain_lo(2, b0 - 2)
                for i in range(2):
                    rotate(2 * b0 + i, i)
                dve.wait_ge(sg["rotated"], 2 * b0 + 2)
            for half in range(2):
                plain_lo(3, half)
            for k in range(KD):
                dve.wait_ge(sg["w_hi"], 5 + k)
                lo(w_proj[1][:, k, :], ps_w[:, k, 256:512], w_proj[0][:, k, :]).then_inc(sg["wt_lo"], 1)
            dve.wait_ge(sg["gate_ready"], 1)
            dve.tensor_scalar(consts["b_out"][:, :], consts["b_out"][:, :], consts["gate"][:, 0:1], None, ALU.mult)\
                .then_inc(sg["bias_out_gated"], 1)

        @block.tensor
        def _(pe):
            pe.wait_ge(sg["raw0"], 16)
            pe.wait_ge(sg["ident"], 1)
            for i in range(4):
                k, half = i % 2, i // 2
                if later(i - 1):
                    pe.wait_ge(sg["wt_lo"], i - 1)
                for j in range(4 if half == 0 else 2):
                    last = pe.transpose(ps_w[:, k, j * P:(j + 1) * P], raw[:, 4 * half + j, k * P:(k + 1) * P], ident[:, :])
                last.then_inc(sg["w_full"], 1)

            def x_transpose(b, i):
                if later(b - 1):
                    pe.wait_ge(sg["xt_lo"], b - 1)
                for k in range(KD):
                    last = pe.transpose(ps_x[:, i, k * N:(k + 1) * N], x_in[:, b, k * P:(k + 1) * P], ident[0:N, 0:N])
                last.then_inc(sg["xt_full"], 1)

            def project(b, i):
                pe.wait_ge(sg["xt_lo"], b + 1)
                if later(b - 1):
                    pe.wait_ge(sg["qk_biased"], b - 1)
                if later(b - 1):
                    pe.wait_ge(sg["v_biased"], b - 1)
                product_over_width(pe, ps_qk[0:N, i, :], xt[i], w_qkv, slice(0, 512)).then_inc(sg["qk_full"], 1)
                product_over_width(pe, ps_v[0:N, i, 0:D], xt[i], w_qkv, slice(512, 768)).then_inc(sg["v_full"], 1)

            pe.wait_ge(sg["x_loaded0"], 16)
            for i in range(2):
                x_transpose(i, i)
            pe.wait_ge(sg["wt_lo"], 4)
            pe.wait_ge(sg["x_loaded1"], 16)
            for b0 in range(B // 2):
                if b0 < B // 2 - 1:
                    for i in range(2):
                        x_transpose(2 * b0 + 2 + i, i)
                for i in range(2):
                    project(2 * b0 + i, i)
            pe.wait_ge(sg["raw1"], 16)
            for k in range(KD):
                for j in range(2):
                    last = pe.transpose(ps_w[:, k, 256 + j * P:256 + (j + 1) * P], raw[:, 6 + j, k * P:(k + 1) * P], ident[:, :])
                last.then_inc(sg["w_full"], 1)



def load_expert(sp, raw, w1, w2, w3, loaded):
    for i, src in ((0, w1), (2, w2)):
        for k in range(KD):
            sp.dma_start(raw[:, :, i + k, :], src[k * P:(k + 1) * P, :].rearrange("p (m c) -> p m c", m=MH)).then_inc(loaded, 16)
    sp.dma_start(raw[:, :, 4:6, :].rearrange("p m o c -> p m (o c)"), w3.rearrange("(m p) d -> p m d", p=P)).then_inc(loaded, 16)


def attention_block(nc, sg, A, x2_all, ident, consts, weights, qk_rot, v_all, raw, ffn_sg):
    w_k, w_v, w_q, w_o, w_proj = weights
    bias_proj, bias_out, gate, gamma, beta, neg_half = (consts[n] for n in ("proj_b", "b_out", "gate", "gamma", "beta",
                                                                           "neg_half"))
    with ExitStack() as ctx:
        def sb(name, shape, dt=F32):
            return ctx.enter_context(nc.sbuf_tensor(name, shape, dt))

        def pair(name, shape):
            return split_pair(nc, ctx, name, shape)


        x_cur = sb("x_cur", [N, D])
        x_res = sb("x_res", [N, D])
        v_self = sb("v_self", [N, B, 2, VW], F32R)
        work = sb("work", [N, 2048])
        qk_t = (sb("q_stacked_t", [P, B, N], F32R), sb("k_stacked_t", [P, B, N], F32R))
        s_max = sb("s_max", [N, 4, 4])
        s_neg = sb("s_neg", [N, 4, 4])
        o_sum = sb("o_sum", [N, 2, 4, HD])
        s_rcp = sb("s_rcp", [N, 2, 4])
        pt = pair("pt", [N, 8, N])
        o_self = sb("o_self", [N, 2 * B, HD])
        o_rows = sb("o_rows", [N, D])
        o_dram = nc.dram_tensor("o_shuffle", (B, 2 * B, N, HD), F32).ap()
        ot = pair("ot", [P, KD, N])
        res = sb("res", [N, D])
        xn = sb("xn", [N, D])
        x1 = sb("x1", [N, D])
        stats = sb("stats", [N, 2, 6])
        mv = sb("mv", [N, 2, 2])
        rstd = sb("rstd", [N, 2])
        xnt_f = sb("xnt_f", [P, KD, N])
        xnt = pair("xnt", [P, KD, N])
        ctx_raw = sb("ctx_raw", [SKT, ST, D])
        ctxt = pair("ctxt", [P, KD, SKP])
        qt = pair("qt", [P, PAIRS, N])
        kt = pair("kt", [P, 2, SKP])
        v = pair("v", [SKT, 2, ST, 512])
        probs = sb("probs", [N, 2, 2, SK])
        c_max = sb("c_max", [N, 2, 2])
        c_neg = sb("c_neg", [N, 2, 2])
        c_sum = sb("c_sum", [N, 2, 2])
        c_rcp = sb("c_rcp", [N, 2, 2])
        cpt = pair("cpt", [SKT, 2, ST, N])
        oct_ = pair("oct", [P, PAIRS, N])
        res2 = sb("res2", [N, D])
        stats2 = sb("stats2", [N, 6])
        mv2 = sb("mv2", [N, 2])
        rstd2 = sb("rstd2", [N, 1])

        ps_s = ctx.enter_context(nc.psum_tensor("ps_s", [P, 2, 512], F32))
        ps_t = ctx.enter_context(nc.psum_tensor("ps_t", [P, 2, 512], F32))
        ps_o = ctx.enter_context(nc.psum_tensor("ps_o", [P, 512], F32))
        ps_v = ctx.enter_context(nc.psum_tensor("ps_vx", [P, 512], F32))
        ps_a = ctx.enter_context(nc.psum_tensor("ps_a", [P, 2, 512], F32))

        def bank(name):
            if name[0] == "C":
                return ps_a[:, FILLS.index({"C0": "PJ", "C1": "NT"}[name]) % 2, :]
            return ps_a[:, FILLS.index(name) % 2, :]

        def ctx_bank(b, k):
            return bank(f"C{k}") if later(b) else ps_s[:, k, :]

        stack = work[:, :].rearrange("p (t b r c w) -> p t b r c w", t=2, b=B, r=2, c=4)
        e_self = work[:, 0:2 * B * N].rearrange("p (s n) -> p s n", s=2 * B)
        q_rows = work[:, 0:1024].rearrange("p (i n) -> p i n", i=2)
        block = ctx.enter_context(nc.Block())

        def qk_src(b, i, r):
            return qk_rot[:, :, bass.ds(i * D + (2 * b + r) * HD, HD)].unsqueeze(2).to_broadcast([N, B, 2, HD])

        def v_heads(b):
            return v_all[:, :, bass.ds(2 * HD * b, 2 * HD)].rearrange("p b (r w) -> p b r w", r=2)

        def iterations(eng, iteration):
            iteration(0, True)
            with eng.Fori(1, B - 1) as b:
                iteration(b, True)
            iteration(B - 1, False)

        @block.sync
        def _(sp):
            def entry(b):
                if later(b):
                    sp.wait_ge(sg["c_full"], 2 * b)
                sp.dma_start(ctx_raw[:, :, :], A["ctx"][bass.ds(b, 1)].rearrange("a (t p) d -> p (a t) d", p=SKT))\
                    .then_inc(sg["ctx_loaded"], 16)
                if later(b):
                    sp.wait_ge(sg["x_res_ready"], b)
                sp.dma_start(x_cur[:, :], A["x"][bass.ds(b, 1)].rearrange("a n d -> (a n) d")).then_inc(sg["x_loaded"], 16)
                sp.wait_ge(sg["o_normed"], 2 * b + 2)
                sp.dma_start(o_dram[bass.ds(b, 1)].rearrange("a k q w -> q (a k) w"), o_self[:, :, :])\
                    .then_inc(sg["o_stored"], 16)
                sp.wait_ge(sg["o_stored"], 16 * (b + 1))
                if later(b):
                    sp.wait_ge(sg["a_full"], fill_no("OT", b - 1))
                sp.dma_start(o_rows[:, :], o_dram[bass.ds(b, 1)].rearrange("a k (i l) w -> (a k i) (l w)", l=D // HD))\
                    .then_inc(sg["o_rows_loaded"], 16)
            for b in range(B):
                entry(b)
            sp.wait_ge(sg["qk_hi"], 4 * B)
            sp.wait_ge(sg["qk_lo"], 3 * B)
            sp.wait_ge(sg["k_lo"], B)
            load_expert(sp, raw, A["sw1"], A["sw2"], A["sw3"], ffn_sg["raw_loaded"])

        @block.gpsimd
        def _(pool):
            for i, value in ((HD, 1.0), (HD + 1, 0.0)):
                pool.memset(v_self[:, :, :, i:i + 1].bitcast(F32), value).then_inc(sg["v_ones"], 1)
            for t in ctxt:
                pool.memset(t[:, :, SK:SKP].bitcast(F32), 0.0).then_inc(sg["padded"], 1)

            def residual(b):
                pool.wait_ge(sg["x_loaded"], 16 * (b + 1))
                if later(b):
                    pool.wait_ge(sg["res1"], b)
                pool.tensor_tensor(x_res[:, :], x_cur[:, :], bias_proj[:, :], ALU.add).then_inc(sg["x_res_ready"], 1)

            def stack_lo(b, i, r):
                pool.wait_ge(sg["qk_hi"], 4 * b + 2 * i + r + 1)
                src = qk_src(b, i, r)
                hi = stack[:, i, :, r, 0:1, :].to_broadcast([N, B, 2, HD])
                dst = stack[:, i, :, r, 1:4:2, :] if i == 0 else stack[:, i, :, r, 2:4, :]
                pool.tensor_tensor(dst.bitcast(F32R), src, hi, ALU.subtract).then_inc(sg["qk_lo"], 1)

            def x1_out(b):
                pool.wait_ge(sg["x1_ready"], b + 1)
                pool.nop(nofuse=True)
                pool.tensor_tensor(x2_all[0:N, b, :], x1[:, :], bias_out[:, :], ALU.add).then_inc(sg["x1_kept"], 1)

            def rsqrt(rs, mean_var, tag, count):
                pool.wait_ge(sg[tag + "_var"], count)
                pool.tensor_tensor(rs, mean_var[:, 1:2], neg_half[:, :], ALU.pow).then_inc(sg[tag + "_rstd"], 1)

            def x2_norm(b):
                rsqrt(rstd2[:, :], mv2[:, :], "n3", b + 1)

            def normalise(b, s):
                pool.wait_ge(sg["c_rcp_ready"], PAIRS * b + s + 1)
                p = probs[:, s % 2]
                r = c_rcp[:, s % 2].unsqueeze(2).to_broadcast([N, 2, SK])
                pool.tensor_tensor(p, p, r, ALU.mult).then_inc(sg["p_normed"], 1)

            for i, r in ((0, 0), (0, 1), (1, 0)):
                stack_lo(0, i, r)
            residual(0)
            rsqrt(rstd[:, 0:1], mv[:, 0, :], "n1", 1)
            rsqrt(rstd[:, 1:2], mv[:, 1, :], "n2", 1)
            x1_out(0)

            def iteration(b, more):
                for s in range(PAIRS):
                    if more and s == 0:
                        for i, r in ((0, 0), (0, 1), (1, 0)):
                            stack_lo(b + 1, i, r)
                    if more and s == 6:
                        rsqrt(rstd[:, 1:2], mv[:, 1, :], "n2", b + 2)
                    normalise(b, s)
                    if more and s == 5:
                        rsqrt(rstd[:, 0:1], mv[:, 0, :], "n1", b + 2)
                    if more and s == 1:
                        residual(b + 1)
                    if more and s == 6:
                        x1_out(b + 1)
                    if s == 2 and later(b):
                        x2_norm(b - 1)
            iterations(pool, iteration)
            x2_norm(B - 1)

        @block.scalar
        def _(act):
            def hi(dst, src):
                return act.activation(dst, src, ACT.Copy)

            def v_hi(b):
                if later(b):
                    act.wait_ge(sg["a_full"], fill_no("O1", b - 1))
                hi(v_self[:, :, :, 0:HD], v_heads(b)).then_inc(sg["v_self_hi"], 1)

            def stack_hi(b):
                if later(b):
                    act.wait_ge(sg["a_full"], fill_no("Q1", b - 1))
                for i in range(2):
                    for r in range(2):
                        dst = stack[:, i, :, r, 0:4:2, :] if i == 0 else stack[:, i, :, r, 0:2, :]
                        hi(dst.bitcast(F32R), qk_src(b, i, r)).then_inc(sg["qk_hi"], 1)

            def stacked_t(b, f):
                if later(b):
                    act.wait_ge(sg["a_full"], fill_no("S3", b - 1))
                act.wait_ge(sg["a_full"], fill_no(f, b))
                first = 4 * ("A", "B").index(f[1])
                dst = qk_t[("Q", "K").index(f[0])][:, first:first + 4, :]
                hi(dst.rearrange("p a n -> p (a n)"), bank(f)[:, 0:4 * N]).then_inc(sg["qk_stacked_t"], 1)

            def self_exp(b, f):
                act.wait_ge(sg["s_neg_ready"], 4 * b + f + 1)
                for j in range(4):
                    last = act.activation(e_self[:, 4 * f + j, :], bank(f"S{f}")[0:N, j * N:(j + 1) * N], ACT.Exp,
                                          bias=s_neg[:, f, j:j + 1], scale=SELF_SCALE)
                last.then_inc(sg["e_ready"], 1)

            def self_pt(b, i):
                act.wait_ge(sg["a_full"], fill_no(f"T{i}", b))
                if i >= 2:
                    act.wait_ge(sg["a_full"], fill_no("O0", b))
                elif later(b):
                    act.wait_ge(sg["a_full"], fill_no("O1", b - 1))
                dst = pt[0][:, 4 * (i % 2):4 * (i % 2) + 4, :]
                hi(dst.rearrange("p a n -> p (a n)"), bank(f"T{i}")[0:N, 0:4 * N]).then_inc(sg["pt_hi"], 1)

            def ot_hi(b):
                act.wait_ge(sg["a_full"], fill_no("OT", b))
                hi(ot[0][:, :, :].rearrange("p k n -> p (k n)"), bank("OT")[:, 0:KD * N]).then_inc(sg["ot_hi"], 1)

            def ctx_hi(b, k):
                act.wait_ge(sg["c_full"], 2 * b + k + 1)
                if later(b):
                    act.wait_ge(sg["k_full"], PAIRS * b)
                hi(ctxt[0][:, k, 0:SK], ctx_bank(b, k)[:, 0:SK]).then_inc(sg["ctxt_hi"], 1)

            def xn_affine(b):
                act.wait_ge(sg["a_full"], fill_no("NT", b))
                if later(b):
                    act.wait_ge(sg["xnt_lo_ready"], b)
                for k in range(KD):
                    act.activation(xnt_f[:, k, :], bank("NT")[:, k * N:(k + 1) * N], ACT.Identity,
                                   bias=beta[:, k:k + 1], scale=gamma[:, k:k + 1]).then_inc(sg["xn_affine"], 1)

            def q_copy(b, i):
                act.wait_ge(sg["a_full"], fill_no(f"R{i}", b))
                act.activation(q_rows[:, i, :], bank(f"R{i}")[0:N, :], ACT.Copy).then_inc(sg["q_rows"], 1)

            def q_hi(b, i):
                act.wait_ge(sg["a_full"], fill_no(f"Q{i}", b))
                if later(PAIRS * b):
                    act.wait_ge(sg["s_full"], PAIRS * b)
                hi(qt[0][:, 4 * i:4 * i + 4, :].rearrange("p a n -> p (a n)"), bank(f"Q{i}")[:, 0:4 * N]).then_inc(sg["qt_hi"], 1)

            def k_hi(b, p):
                act.wait_ge(sg["k_full"], PAIRS * b + p + 1)
                if later(PAIRS * b + p - 1):
                    act.wait_ge(sg["s_full"], PAIRS * b + p - 1)
                hi(kt[0][:, p % 2, :], ps_o[:, 0:SKP]).then_inc(sg["kt_hi"], 1)

            def v_hi_cross(b, f):
                q, t = int(f[1]), int(f[2])
                act.wait_ge(sg["v_full"], v_no(f, b))
                if later(PAIRS * (b - 1) + 4 * q + 4):
                    act.wait_ge(sg["pv_full"], PAIRS * (b - 1) + 4 * q + 4)
                hi(v[0][:, q, t, :], ps_v[0:SKT, :]).then_inc(sg["v_hi"], 1)

            def exps(b, s):
                act.wait_ge(sg["c_neg_ready"], PAIRS * b + s + 1)
                if later(PAIRS * b + s - 1):
                    act.wait_ge(sg["t_full"], PAIRS * b + s - 1)
                for h in range(2):
                    act.activation(probs[:, s % 2, h, :], ps_s[0:N, h, 0:SK], ACT.Exp, bias=c_neg[:, s % 2, h:h + 1],
                                   scale=CROSS_SCALE, accum_out=c_sum[:, s % 2, h:h + 1]).then_inc(sg["c_exp"], 1)

            def cpt_hi(b, s):
                act.wait_ge(sg["t_full"], PAIRS * b + s + 1)
                if later(PAIRS * b + s):
                    act.wait_ge(sg["pv_full"], PAIRS * b + s)
                hi(cpt[0][:, :, :, :].rearrange("p h t n -> p h (t n)"), ps_t[0:SKT, :, 0:ST * N]).then_inc(sg["cpt_hi"], 1)

            def o_hi(b, s):
                act.wait_ge(sg["pv_full"], PAIRS * b + s + 1)
                if later(b):
                    act.wait_ge(sg["wo_full"], b)
                for h in range(2):
                    r = slice(64 * h, 64 * h + 64)
                    hi(oct_[0][r, s, :], ps_o[r, h * N:(h + 1) * N]).then_inc(sg["oct_hi"], 1)

            def fill_hi(b, f):
                if f in ("QA", "QB", "KA", "KB"):
                    stacked_t(b, f)
                elif f[0] == "S":
                    self_exp(b, int(f[1]))
                elif f[0] == "T":
                    self_pt(b, int(f[1]))
                elif f[0] == "C":
                    ctx_hi(b, int(f[1]))
                elif f == "OT":
                    ot_hi(b)
                elif f == "NT":
                    xn_affine(b)
                elif f[0] == "R":
                    q_copy(b, int(f[1]))
                elif f[0] == "Q":
                    q_hi(b, int(f[1]))

            stack_hi(0)
            v_hi(0)
            for f in ("QA", "QB", "KA", "KB"):
                fill_hi(0, f)
            for f in ("S0", "S1", "S2", "S3"):
                fill_hi(0, f)
            fill_hi(0, "T0")
            fill_hi(0, "T1")
            act.wait_ge(sg["padded"], 2)
            fill_hi(0, "C0")
            fill_hi(0, "C1")
            fill_hi(0, "T2")
            fill_hi(0, "T3")
            k_hi(0, 0)
            v_hi_cross(0, "V00")
            fill_hi(0, "OT")
            k_hi(0, 1)
            v_hi_cross(0, "V01")
            fill_hi(0, "NT")
            fill_hi(0, "R0")
            fill_hi(0, "R1")
            fill_hi(0, "Q0")
            fill_hi(0, "Q1")

            def iteration(b, more):
                for s in range(PAIRS):
                    def place(n):
                        if more:
                            for f in FILL_AT.get((s, n), ()):
                                fill_hi(b + 1, f)

                    if more and s == 0:
                        stack_hi(b + 1)
                    if s == 2:
                        exps(b, s)
                    place(0)
                    if s + 2 < PAIRS:
                        k_hi(b, s + 2)
                    elif more:
                        k_hi(b + 1, s + 2 - PAIRS)
                    if s == 3:
                        exps(b, s)
                    place(1)
                    if s not in (2, 3):
                        exps(b, s)
                    if s == 6:
                        place(3)
                    if s == 7:
                        place(2)
                    if s in V_AT and (s < 6 or more):
                        v_hi_cross(b if s < 6 else b + 1, V_AT[s])
                    if s != 7:
                        place(2)
                    if more and s == 0:
                        v_hi(b + 1)
                    if s not in (1, 6):
                        place(3)
                    if s >= 2:
                        o_hi(b, s - 2)
                    elif later(b):
                        o_hi(b - 1, s + 6)
                    if s == 1:
                        place(3)
                    if s >= 1:
                        cpt_hi(b, s - 1)
                    elif later(b):
                        cpt_hi(b - 1, 7)
                    place(4)
            iterations(act, iteration)
            o_hi(B - 1, 6)
            cpt_hi(B - 1, 7)
            o_hi(B - 1, 7)

        @block.vector
        def _(dve):
            def lo(dst, src, part):
                return dve.tensor_tensor(dst, src, part.bitcast(F32), ALU.subtract)

            def moments(src, st, mean_var, tag, count):
                dve.bn_stats(st, src).then_inc(sg[tag + "_stats"], 1)
                dve.wait_ge(sg[tag + "_stats"], count)
                dve.nop(nofuse=True)
                dve.bn_aggr(mean_var, st).then_inc(sg[tag + "_aggr"], 1)
                dve.wait_ge(sg[tag + "_aggr"], count)
                dve.tensor_scalar(mean_var[:, 1:2], mean_var[:, 1:2], EPS, None, ALU.add).then_inc(sg[tag + "_var"], 1)

            def norm(src, dst, mean_var, rs, tag, count):
                dve.wait_ge(sg[tag + "_rstd"], count)
                return dve.tensor_scalar(dst, src, mean_var[:, 0:1], rs, ALU.subtract, ALU.mult)

            def stack_lo(b):
                dve.wait_ge(sg["qk_hi"], 4 * b + 4)
                lo(stack[:, 1, :, 1, 2:4, :].bitcast(F32R), qk_src(b, 1, 1),
                   stack[:, 1, :, 1, 0:1, :].bitcast(F32R).to_broadcast([N, B, 2, HD])).then_inc(sg["k_lo"], 1)

            def v_split(b):
                dve.wait_ge(sg["v_self_hi"], b + 1)
                lo(v_self[:, :, :, VS:VW], v_heads(b), v_self[:, :, :, 0:HD]).then_inc(sg["v_self_lo"], 1)

            def self_max(b, f):
                src = bank(f"S{f}")[0:N, 0:4 * N].rearrange("p (a n) -> p a n", a=4)
                dve.wait_ge(sg["a_full"], fill_no(f"S{f}", b))
                dve.reduce_max(s_max[:, f, :], src, X).then_inc(sg["s_max_ready"], 1)
                dve.wait_ge(sg["s_max_ready"], 4 * b + f + 1)
                dve.tensor_scalar(s_neg[:, f, :], s_max[:, f, :], -SELF_SCALE, None, ALU.mult).then_inc(sg["s_neg_ready"], 1)

            def self_pt(b, i):
                dve.wait_ge(sg["pt_hi"], 4 * b + i + 1)
                dst = slice(4 * (i % 2), 4 * (i % 2) + 4)
                lo(pt[1][:, dst, :].rearrange("p a n -> p (a n)"), bank(f"T{i}")[0:N, 0:4 * N],
                   pt[0][:, dst, :].rearrange("p a n -> p (a n)")).then_inc(sg["pt_lo"], 1)

            def o_norm(b, i):
                dve.wait_ge(sg["a_full"], fill_no(f"O{i}", b))
                src = bank(f"O{i}")[0:N, 0:8 * VW].rearrange("p (r b w) -> p r b w", r=2, w=VW)
                if later(2 * b + i):
                    dve.wait_ge(sg["o_normed"], 2 * b + i)
                dve.reciprocal(s_rcp[:, :, :], src[:, :, :, HD]).then_inc(sg["s_rcp_ready"], 1)
                dve.tensor_copy(o_sum[:, :, :, :], src[:, :, :, VS:VW]).then_inc(sg["o_part"], 1)
                dve.wait_ge(sg["o_part"], 2 * b + i + 1)
                dve.tensor_tensor(o_sum[:, :, :, :], o_sum[:, :, :, :], src[:, :, :, 0:HD], ALU.add).then_inc(sg["o_summed"], 1)
                dve.wait_ge(sg["o_summed"], 2 * b + i + 1)
                dve.wait_ge(sg["s_rcp_ready"], 2 * b + i + 1)
                if later(16 * b):
                    dve.wait_ge(sg["o_stored"], 16 * b)
                out = o_self[:, :, :].rearrange("p (r b) w -> p r b w", r=2)[:, :, 4 * i:4 * i + 4, :]
                dve.tensor_tensor(out, o_sum[:, :, :, :], s_rcp[:, :, :].unsqueeze(3).to_broadcast([N, 2, 4, HD]),
                                  ALU.mult).then_inc(sg["o_normed"], 1)

            def ot_lo(b):
                dve.wait_ge(sg["ot_hi"], b + 1)
                lo(ot[1][:, :, :].rearrange("p k n -> p (k n)"), bank("OT")[:, 0:KD * N],
                   ot[0][:, :, :].rearrange("p k n -> p (k n)")).then_inc(sg["ot_lo"], 1)

            def ctx_lo(b, k):
                dve.wait_ge(sg["ctxt_hi"], 2 * b + k + 1)
                lo(ctxt[1][:, k, 0:SK], ctx_bank(b, k)[:, 0:SK], ctxt[0][:, k, 0:SK]).then_inc(sg["ctxt_lo"], 1)

            def residual_moments(b):
                dve.wait_ge(sg["a_full"], fill_no("PJ", b))
                dve.wait_ge(sg["x_res_ready"], b + 1)
                dve.tensor_tensor(res[:, :], bank("PJ")[0:N, 0:D], x_res[:, :], ALU.add).then_inc(sg["res1"], 1)
                dve.wait_ge(sg["res1"], b + 1)
                moments(res[:, :], stats[:, 0, :], mv[:, 0, :], "n1", b + 1)

            def x1_moments(b):
                if later(b):
                    dve.wait_ge(sg["x1_kept"], b)
                norm(res[:, :], x1[:, :], mv[:, 0, :], rstd[:, 0:1], "n1", b + 1).then_inc(sg["x1_ready"], 1)
                dve.wait_ge(sg["x1_ready"], b + 1)
                moments(x1[:, :], stats[:, 1, :], mv[:, 1, :], "n2", b + 1)

            def xn_norm(b):
                if later(b):
                    dve.wait_ge(sg["a_full"], fill_no("NT", b - 1))
                norm(x1[:, :], xn[:, :], mv[:, 1, :], rstd[:, 1:2], "n2", b + 1).then_inc(sg["xn_ready"], 1)

            def xnt_split(b):
                dve.wait_ge(sg["xn_affine"], 2 * b + 2)
                if later(b):
                    dve.wait_ge(sg["a_full"], fill_no("R1", b - 1))
                dve.tensor_copy(xnt[0][:, :, :], xnt_f[:, :, :]).then_inc(sg["xnt_hi_ready"], 1)
                dve.wait_ge(sg["xnt_hi_ready"], b + 1)
                lo(xnt[1][:, :, :], xnt_f[:, :, :], xnt[0][:, :, :]).then_inc(sg["xnt_lo_ready"], 1)

            def q_lo(b, i):
                dve.wait_ge(sg["qt_hi"], 2 * b + i + 1)
                sl = slice(4 * i, 4 * i + 4)
                lo(qt[1][:, sl, :].rearrange("p a n -> p (a n)"), bank(f"Q{i}")[:, 0:4 * N],
                   qt[0][:, sl, :].rearrange("p a n -> p (a n)")).then_inc(sg["qt_lo"], 1)

            def k_lo(b, p):
                dve.wait_ge(sg["kt_hi"], PAIRS * b + p + 1)
                lo(kt[1][:, p % 2, :], ps_o[:, 0:SKP], kt[0][:, p % 2, :]).then_inc(sg["kt_lo"], 1)

            def v_lo_cross(b, f):
                q, t = int(f[1]), int(f[2])
                dve.wait_ge(sg["v_hi"], v_no(f, b))
                lo(v[1][:, q, t, :], ps_v[0:SKT, :], v[0][:, q, t, :]).then_inc(sg["v_lo"], 1)

            def maxima(b, s):
                dve.wait_ge(sg["s_full"], PAIRS * b + s + 1)
                dve.reduce_max(c_max[:, s % 2, :], ps_s[0:N, :, 0:SK], X).then_inc(sg["c_max_ready"], 1)
                dve.wait_ge(sg["c_max_ready"], PAIRS * b + s + 1)
                dve.tensor_scalar(c_neg[:, s % 2, :], c_max[:, s % 2, :], -CROSS_SCALE, None, ALU.mult)\
                    .then_inc(sg["c_neg_ready"], 1)

            def rcp(b, s):
                dve.wait_ge(sg["c_exp"], 2 * (PAIRS * b + s) + 2)
                if later(PAIRS * b + s - 1):
                    dve.wait_ge(sg["p_normed"], PAIRS * b + s - 1)
                dve.reciprocal(c_rcp[:, s % 2, :], c_sum[:, s % 2, :]).then_inc(sg["c_rcp_ready"], 1)

            def cpt_lo(b, s):
                dve.wait_ge(sg["cpt_hi"], PAIRS * b + s + 1)
                dve.tensor_tensor(cpt[1][:, :, :, :].rearrange("p h t n -> p h (t n)"), ps_t[0:SKT, :, 0:ST * N],
                                  cpt[0][:, :, :, :].rearrange("p h t n -> p h (t n)").bitcast(F32), ALU.subtract)\
                    .then_inc(sg["cpt_lo"], 1)

            def late_cpt_lo(b, s):
                cpt_lo(*((b, s - 2) if s >= 2 else (b - 1, s + 6)))

            def o_lo(b, s):
                for h in range(2):
                    dve.wait_ge(sg["oct_hi"], 2 * (PAIRS * b + s) + h + 1)
                    r = slice(64 * h, 64 * h + 64)
                    lo(oct_[1][r, s, :], ps_o[r, h * N:(h + 1) * N], oct_[0][r, s, :]).then_inc(sg["oct_lo"], 1)

            def x2_moments(b):
                dve.wait_ge(sg["wo_full"], b + 1)
                dve.wait_ge(sg["x1_kept"], b + 1)
                dve.scalar_tensor_tensor(res2[:, :], ps_v[0:N, 0:D], gate[:, 0:1], x2_all[0:N, b, :],
                                         op0=ALU.mult, op1=ALU.add).then_inc(sg["res2"], 1)
                dve.wait_ge(sg["res2"], b + 1)
                moments(res2[:, :], stats2[:, :], mv2[:, :], "n3", b + 1)

            def x2_norm(b):
                norm(res2[:, :], x2_all[0:N, b, :], mv2[:, :], rstd2[:, :], "n3", b + 1).then_inc(sg["x2_ready"], 1)

            def fill_lo(b, f):
                if f[0] == "S":
                    self_max(b, int(f[1]))
                elif f[0] == "T":
                    self_pt(b, int(f[1]))
                elif f[0] == "O" and f != "OT":
                    o_norm(b, int(f[1]))
                elif f[0] == "C":
                    ctx_lo(b, int(f[1]))
                elif f == "OT":
                    ot_lo(b)
                elif f == "PJ":
                    residual_moments(b)
                elif f == "NT":
                    xnt_split(b)
                elif f in ("Q0", "Q1"):
                    q_lo(b, int(f[1]))

            stack_lo(0)
            for f in ("S0", "S1", "S2", "S3"):
                fill_lo(0, f)
            v_split(0)
            fill_lo(0, "T0")
            fill_lo(0, "T1")
            dve.wait_ge(sg["padded"], 2)
            fill_lo(0, "C0")
            fill_lo(0, "C1")
            fill_lo(0, "O0")
            fill_lo(0, "T2")
            fill_lo(0, "T3")
            k_lo(0, 0)
            fill_lo(0, "O1")
            v_lo_cross(0, "V00")
            fill_lo(0, "OT")
            fill_lo(0, "PJ")
            x1_moments(0)
            xn_norm(0)
            k_lo(0, 1)
            v_lo_cross(0, "V01")
            fill_lo(0, "NT")
            fill_lo(0, "Q0")
            fill_lo(0, "Q1")

            def iteration(b, more):
                for s in range(PAIRS):
                    def place(n):
                        if more:
                            for f in FILL_AT.get((s, n), ()):
                                fill_lo(b + 1, f)

                    lo_first = s == 6 or (s == 1 and later(b)) or (not more and s >= 5)
                    if lo_first:
                        late_cpt_lo(b, s)
                    if more and s == 6:
                        x1_moments(b + 1)
                    maxima(b, s)
                    if more and s == 6:
                        xn_norm(b + 1)
                    if s == 2:
                        place(0)
                    if not lo_first and (s >= 2 or later(b)):
                        late_cpt_lo(b, s)
                    if s == 2:
                        place(1)
                        rcp(b, s)
                    else:
                        place(0)
                    if s + 2 < PAIRS:
                        k_lo(b, s + 2)
                    elif more:
                        k_lo(b + 1, s + 2 - PAIRS)
                    if more and s == 0:
                        stack_lo(b + 1)
                    if s == 3:
                        rcp(b, s)
                    if s != 2:
                        place(1)
                    if s not in (2, 3):
                        rcp(b, s)
                    if s == 2 and later(b):
                        x2_moments(b - 1)
                    if s == 6:
                        place(3)
                    if s == 7:
                        place(2)
                    if s in V_AT and (s < 6 or more):
                        v_lo_cross(b if s < 6 else b + 1, V_AT[s])
                    if s != 7:
                        place(2)
                    if more and s == 0:
                        v_split(b + 1)
                    if s != 6:
                        place(3)
                    if s >= 2:
                        o_lo(b, s - 2)
                    elif later(b):
                        o_lo(b - 1, s + 6)
                    place(4)
                    if s == 2 and later(b):
                        x2_norm(b - 1)
            iterations(dve, iteration)
            cpt_lo(B - 1, 6)
            o_lo(B - 1, 6)
            cpt_lo(B - 1, 7)
            o_lo(B - 1, 7)
            x2_moments(B - 1)
            x2_norm(B - 1)
            dve.wait_ge(sg["x2_ready"], B)

        @block.tensor
        def _(pe):
            def free(name, b):
                i = FILLS.index(name)
                if name in ("PJ", "NT"):
                    pe.wait_ge(sg["ctxt_lo"], 2 * b + 1 + (name == "NT"))
                if i >= 2:
                    signal, per, which = LAST_READ[FILLS[i - 2]]
                    pe.wait_ge(sg[signal], per * b + which + 1)
                else:
                    last = [f for j, f in enumerate(FILLS) if j % 2 == i][-1]
                    signal, per, which = LAST_READ[last]
                    if later(b):
                        pe.wait_ge(sg[signal], per * (b - 1) + which + 1)

            def stacked_transpose(b, f):
                i, half = ("Q", "K").index(f[0]), ("A", "B").index(f[1])
                pe.wait_ge(sg["qk_lo"], 3 * b + 2 + i)
                if i:
                    pe.wait_ge(sg["k_lo"], b + 1)
                free(f, b)
                for j in range(4):
                    c = i * 1024 + (4 * half + j) * P
                    last = pe.transpose(bank(f)[:, j * N:(j + 1) * N], work[0:N, c:c + P], ident[0:N, 0:N])
                last.then_inc(sg["a_full"], 1)

            def self_scores(b, f):
                pe.wait_ge(sg["qk_stacked_t"], 4 * b + 4)
                free(f"S{f}", b)
                r = slice(64 * (f % 2), 64 * (f % 2) + 64)
                for j in range(4):
                    pr = 4 * (f // 2) + j
                    last = pe.matmul(bank(f"S{f}")[0:N, j * N:(j + 1) * N], qk_t[0][r, pr, :], qk_t[1][r, pr, :],
                                     start=True, stop=True)
                last.then_inc(sg["a_full"], 1)

            def self_pt(b, i):
                pe.wait_ge(sg["e_ready"], 4 * b + i + 1)
                free(f"T{i}", b)
                for j in range(4):
                    last = pe.transpose(bank(f"T{i}")[0:N, j * N:(j + 1) * N], e_self[:, 4 * i + j, :], ident[0:N, 0:N])
                last.then_inc(sg["a_full"], 1)

            def self_out(b, i):
                pe.wait_ge(sg["pt_lo"], 4 * b + 2 * i + 2)
                pe.wait_ge(sg["v_self_lo"], b + 1)
                if i == 0 and not later(b):
                    pe.wait_ge(sg["v_ones"], 2)
                free(f"O{i}", b)
                for j in range(8):
                    bb, r = 4 * i + j % 4, j // 4
                    out = bank(f"O{i}")[0:N, j * VW:(j + 1) * VW]
                    pe.matmul(out, pt[0][:, j, :], v_self[:, bb, r, :], start=True, stop=False)
                    last = pe.matmul(out[:, 0:VS], pt[1][:, j, :], v_self[:, bb, r, 0:VS], start=False, stop=True)
                last.then_inc(sg["a_full"], 1)

            def o_transpose(b):
                pe.wait_ge(sg["o_rows_loaded"], 16 * (b + 1))
                free("OT", b)
                for k in range(KD):
                    last = pe.transpose(bank("OT")[:, k * N:(k + 1) * N], o_rows[:, k * P:(k + 1) * P], ident[0:N, 0:N])
                last.then_inc(sg["a_full"], 1)

            def ctx_transpose(b, k):
                pe.wait_ge(sg["ctx_loaded"], 16 * (b + 1))
                if later(b):
                    if k == 0:
                        pe.wait_ge(sg["o_summed"], 2 * b + 2)
                    else:
                        pe.wait_ge(sg["ot_lo"], b + 1)
                for t in range(ST):
                    last = pe.transpose(ctx_bank(b, k)[:, t * SKT:(t + 1) * SKT], ctx_raw[:, t, k * P:(k + 1) * P],
                                        ident[0:SKT, 0:SKT])
                last.then_inc(sg["c_full"], 1)

            def out_project(b):
                pe.wait_ge(sg["ot_lo"], b + 1)
                free("PJ", b)
                product_over_width(pe, bank("PJ")[0:N, 0:D], ot, w_proj, slice(0, D)).then_inc(sg["a_full"], 1)

            def xn_transpose(b):
                pe.wait_ge(sg["xn_ready"], b + 1)
                free("NT", b)
                for k in range(KD):
                    last = pe.transpose(bank("NT")[:, k * N:(k + 1) * N], xn[:, k * P:(k + 1) * P], ident[0:N, 0:N])
                last.then_inc(sg["a_full"], 1)

            def q_project(b, i):
                pe.wait_ge(sg["xnt_lo_ready"], b + 1)
                free(f"R{i}", b)
                product_over_width(pe, bank(f"R{i}")[0:N, :], xnt, w_q, slice(512 * i, 512 * i + 512)).then_inc(sg["a_full"], 1)

            def q_transpose(b, i):
                pe.wait_ge(sg["q_rows"], 2 * b + i + 1)
                free(f"Q{i}", b)
                for j in range(4):
                    last = pe.transpose(bank(f"Q{i}")[:, j * N:(j + 1) * N], q_rows[:, i, j * P:(j + 1) * P], ident[0:N, 0:N])
                last.then_inc(sg["a_full"], 1)

            def k_project(b, p):
                pe.wait_ge(sg["ctxt_lo"], 2 * b + 2)
                if later(PAIRS * b + p):
                    pe.wait_ge(sg["kt_lo"], PAIRS * b + p)
                if later(PAIRS * b + p - 4):
                    pe.wait_ge(sg["oct_lo"], 2 * (PAIRS * b + p - 4))
                m = slice(p * P, (p + 1) * P)
                for k in range(KD):
                    last = product(pe, ps_o[:, 0:SKP], tuple(t[:, k, m] for t in w_k), tuple(t[:, k, :] for t in ctxt),
                                   start=k == 0, stop=k == KD - 1)
                last.then_inc(sg["k_full"], 1)

            def v_project(b, f):
                q, t = int(f[1]), int(f[2])
                if f == "V10" and later(b):
                    pe.wait_ge(sg["res2"], b)
                if later(v_no(f, b) - 1):
                    pe.wait_ge(sg["v_lo"], v_no(f, b) - 1)
                rows = slice(t * SKT, (t + 1) * SKT)
                for k in range(KD):
                    last = product(pe, ps_v[0:SKT, :], tuple(c[:, k, rows] for c in ctxt),
                                   tuple(w[:, k, 512 * q:512 * q + 512] for w in w_v), start=k == 0, stop=k == KD - 1)
                last.then_inc(sg["v_full"], 1)

            def scores(b, s):
                pe.wait_ge(sg["qt_lo"], 2 * b + 2)
                pe.wait_ge(sg["kt_lo"], PAIRS * b + s + 1)
                if later(2 * (PAIRS * b + s)):
                    pe.wait_ge(sg["c_exp"], 2 * (PAIRS * b + s))
                for h in range(2):
                    r = slice(64 * h, 64 * h + 64)
                    last = product(pe, ps_s[0:N, h, 0:SKP], tuple(t[r, s, :] for t in qt),
                                   tuple(t[r, s % 2, :] for t in kt))
                last.then_inc(sg["s_full"], 1)

            def p_transpose(b, s):
                pe.wait_ge(sg["p_normed"], PAIRS * b + s + 1)
                if later(PAIRS * b + s):
                    pe.wait_ge(sg["cpt_lo"], PAIRS * b + s)
                for h in range(2):
                    for t in range(ST):
                        last = pe.transpose(ps_t[0:SKT, h, t * N:(t + 1) * N],
                                            probs[:, s % 2, h, t * SKT:(t + 1) * SKT], ident[0:N, 0:N])
                last.then_inc(sg["t_full"], 1)

            def pv(b, s, k_done):
                pe.wait_ge(sg["cpt_lo"], PAIRS * b + s + 1)
                pe.wait_ge(sg["v_lo"], v_no("V02" if s < 4 else "V12", b))
                pe.wait_ge(sg["kt_lo"], k_done)
                if later(PAIRS * b + s):
                    pe.wait_ge(sg["oct_lo"], 2 * (PAIRS * b + s))
                c = slice((s % 4) * P, (s % 4 + 1) * P)
                for t in range(ST):
                    last = product(pe, ps_o[:, 0:2 * N], tuple(w[:, s // 4, t, c] for w in v),
                                   tuple(w[:, :, t, :] for w in cpt), start=t == 0, stop=t == ST - 1)
                last.then_inc(sg["pv_full"], 1)

            def cross_out(b, pairs=range(PAIRS)):
                if 0 in pairs:
                    pe.wait_ge(sg["v_lo"], v_before_output(b))
                pe.wait_ge(sg["oct_lo"], 2 * (PAIRS * b + pairs[-1] + 1))
                for k in pairs:
                    last = product(pe, ps_v[0:N, 0:D], tuple(t[:, k, :] for t in oct_), tuple(t[:, k, :] for t in w_o),
                                   start=k == 0, stop=k == PAIRS - 1)
                if PAIRS - 1 in pairs:
                    last.then_inc(sg["wo_full"], 1)

            def fill(b, f):
                if f in ("QA", "QB", "KA", "KB"):
                    stacked_transpose(b, f)
                elif f[0] == "S":
                    self_scores(b, int(f[1]))
                elif f[0] == "T":
                    self_pt(b, int(f[1]))
                elif f == "OT":
                    o_transpose(b)
                elif f[0] == "O":
                    self_out(b, int(f[1]))
                elif f in ("C0", "C1"):
                    ctx_transpose(b, int(f[1]))
                elif f == "PJ":
                    out_project(b)
                elif f == "NT":
                    xn_transpose(b)
                elif f[0] == "R":
                    q_project(b, int(f[1]))
                else:
                    q_transpose(b, int(f[1]))

            for f in FILLS[:FILLS.index("T1") + 1] + ["C0", "C1", "O0", "T2"]:
                fill(0, f)
            k_project(0, 0)
            fill(0, "T3")
            fill(0, "O1")
            v_project(0, "V00")
            fill(0, "OT")
            fill(0, "PJ")
            k_project(0, 1)
            v_project(0, "V01")
            fill(0, "NT")
            for f in ("R0", "R1", "Q0", "Q1"):
                fill(0, f)

            def iteration(b, more):
                for s in range(PAIRS):
                    def place(n):
                        if more:
                            for f in FILL_AT.get((s, n), ()):
                                fill(b + 1, f)

                    k_done = PAIRS * b + min(s + 3, PAIRS if not more else s + 3)
                    scores(b, s)
                    place(0)
                    if s + 2 < PAIRS:
                        k_project(b, s + 2)
                    elif more:
                        k_project(b + 1, s + 2 - PAIRS)
                    place(1)
                    if s == 2 and later(b):
                        cross_out(b - 1)
                    if s != 2 and s in V_AT and (s < 6 or more):
                        v_project(b if s < 6 else b + 1, V_AT[s])
                    place(2)
                    if s >= 1:
                        p_transpose(b, s - 1)
                    elif later(b):
                        p_transpose(b - 1, 7)
                    if s == 2:
                        v_project(b, V_AT[s])
                    place(3)
                    if s >= 2:
                        pv(b, s - 2, k_done)
                    elif s < 2 and later(b):
                        pv(b - 1, s + 6, k_done)
                    place(4)
            iterations(pe, iteration)
            p_transpose(B - 1, 7)
            pv(B - 1, 6, PAIRS * B)
            cross_out(B - 1, range(0, 6))
            pv(B - 1, 7, PAIRS * B)
            cross_out(B - 1, range(6, PAIRS))


def ffn_block(nc, sg, A, x2_all, ident, raw, out):
    UNITS = 2 * MH
    with ExitStack() as ctx:
        def sb(name, shape, dt=F32):
            return ctx.enter_context(nc.sbuf_tensor(name, shape, dt))

        def pair(name, shape):
            return split_pair(nc, ctx, name, shape)


        w = pair("ffn_w", [P, MH, 6, P])
        x2t = pair("x2t", [P, KD, TOK])
        gw_raw = sb("gw_raw", [P, KD, EXP])
        gw = pair("gw", [P, KD, EXP])
        logits_t = sb("logits_t", [EXP, 2, HALF])
        logits = sb("logits", [N, B, EXP])
        top = sb("top", [N, B, 8])
        top_i = sb("top_i", [N, B, 8], U32)
        top_f = sb("top_f", [N, B, 2])
        gap = sb("gap", [N, B])
        gap_e = sb("gap_e", [N, B])
        w_top = sb("w_top", [N, 2, B])
        eid = sb("eid", [N, EXP])
        pick = sb("pick", [N, 2, B, EXP])
        w_tok = sb("w_tok", [N, B, EXP])
        w_bc = sb("w_bc", [P, EXP, TOK])
        s_act = sb("s_act", [P, 2, HALF])
        g = sb("g", [P, 2, HALF])
        gs = pair("gs", [P, 2, HALF])
        y_sb = sb("y_sb", [P, KD, TOK])
        res = sb("ffn_res", [N, B, D])
        stats = sb("ffn_stats", [N, B, 6])
        mv = sb("ffn_mv", [N, B, 2])
        rstd = sb("ffn_rstd", [N, B])
        var = sb("ffn_var", [N, B])
        shift = sb("ffn_shift", [N, B])
        neg_half = sb("ffn_neg_half", [N, B])
        euler = sb("euler", [N, B])
        y_out = sb("y_out", [N, B, D])

        ps_y = ctx.enter_context(nc.psum_tensor("ps_y", [P, 4, 512], F32))
        ps_h = ctx.enter_context(nc.psum_tensor("ps_h", [P, 4, 512], F32))
        block = ctx.enter_context(nc.Block())

        def half(i):
            return slice(i * HALF, (i + 1) * HALF)

        @block.sync
        def _(sp):
            sp.dma_start(gw_raw[:, :, :], A["gate_w"].rearrange("(k p) e -> p k e", p=P)).then_inc(sg["gw_loaded"], 16)

            def expert_load(e):
                sp.wait_ge(sg["w_lo"], MH * e)
                w1, w2, w3 = (A[n][bass.ds(e - 1, 1)].rearrange("a d h -> (a d) h") for n in ("ew1", "ew2", "ew3"))
                load_expert(sp, raw, w1, w2, w3, sg["raw_loaded"])
            with sp.Fori(1, EXP + 1) as e:
                expert_load(e)
            for pair in range(4):
                if pair % 2 == 0:
                    sp.wait_ge(sg["y_ready"], pair + 2)
                else:
                    sp.wait_ge(sg["y_ready_act"], pair + 1)
                sp.dma_start(out[2 * pair:2 * pair + 2].rearrange("b n d -> n b d"), y_out[:, 2 * pair:2 * pair + 2, :])\
                    .then_inc(sg["stored"], 16)
            sp.wait_ge(sg["stored"], 16 * 4)

        def split_at(j):
            return {0: (0, 2), 2: (0, 3), 4: (1, 0), 6: (1, 1)}.get(j)

        def unit_no(e, j):
            return UNITS * e + j

        def w_split_free(eng, e, m):
            eng.wait_ge(sg["down_done"], unit_no(e - 1, 2 * m + 1) + 1)

        @block.gpsimd
        def _(pool):
            pool.iota(top_i[:, 0, :], [[1, EXP]], base=0, channel_multiplier=0).then_inc(sg["iota"], 1)
            pool.wait_ge(sg["iota"], 1)
            pool.memset(neg_half[:, :], -0.5).then_inc(sg["iota"], 1)
            pool.memset(euler[:, :], float(np.e)).then_inc(sg["iota"], 1)
            pool.wait_ge(sg["iota"], 3)
            pool.tensor_copy(eid[:, :], top_i[:, 0, :]).then_inc(sg["eid_ready"], 1)

            def unit(e, j):
                u = unit_no(e, j)
                if later(e):
                    pool.wait_ge(sg["g_ready"], u + 1)
                    pool.wait_ge(sg["w_bc_ready"], 2 * EXP)
                    pool.nop(nofuse=True)
                    pool.tensor_tensor(g[:, j % 2, :], g[:, j % 2, :], w_bc[:, e - 1, half(j % 2)], ALU.mult)\
                        .then_inc(sg["g_weighted"], 1)
                pool.wait_ge(sg["g_hi"], u + 1)
                pool.tensor_tensor(gs[1][:, j % 2, :], g[:, j % 2, :], gs[0][:, j % 2, :].bitcast(F32), ALU.subtract)\
                    .then_inc(sg["g_lo"], 1)

            def expert(e):
                for j in range(UNITS):
                    unit(e, j)
                    if isinstance(e, int) and j == 4:
                        pool.wait_ge(sg["gap_ready"], 1)
                        pool.tensor_tensor(gap_e[:, :], euler[:, :], gap[:, :], ALU.pow).then_inc(sg["gap_exp"], 1)
            expert(0)
            with pool.Fori(1, EXP + 1) as e:
                expert(e)
            for hf in range(2):
                h = slice(4 * hf, 4 * hf + 4)
                pool.wait_ge(sg["y_var"], hf + 1)
                pool.tensor_tensor(rstd[:, h], var[:, h], neg_half[:, h], ALU.pow).then_inc(sg["y_rstd"], 1)

        @block.scalar
        def _(act):
            def hi(dst, src):
                return act.activation(dst, src, ACT.Copy)

            for i in range(4):
                k, hf = i // 2, i % 2
                act.wait_ge(sg["x2t_full"], i + 1)
                hi(x2t[0][:, k, half(hf)], ps_h[:, i, 0:HALF]).then_inc(sg["x2t_hi"], 1)
            act.wait_ge(sg["gw_loaded"], 16)
            hi(gw[0][:, :, :], gw_raw[:, :, :]).then_inc(sg["gw_hi"], 1)
            act.wait_ge(sg["raw_loaded"], 80)
            for m in range(MH):
                hi(w[0][:, m], raw[:, m]).then_inc(sg["w_hi"], 1)
                if m == 1:
                    act.wait_ge(sg["logits_t_full"], 1)
                    act.activation(logits_t[:, :, :], ps_y[0:EXP, 0:2, 0:HALF], ACT.Copy).then_inc(sg["logits_t_ready"], 1)

            def unit(e, j, more):
                u = unit_no(e, j)
                act.wait_ge(sg["h_full"], u + 1)
                if later(u - 1):
                    act.wait_ge(sg["g_ready"], u - 1)
                act.activation(s_act[:, j % 2, :], ps_h[:, 2 * (j % 2), 0:HALF], ACT.Silu).then_inc(sg["silu"], 1)
                sp = split_at(j)
                if sp and (sp[0] == 0 or more) and (sp[0] == 1 or later(e)):
                    en, m = e + sp[0], sp[1]
                    act.wait_ge(sg["raw_loaded"], 80 * (en + 1))
                    w_split_free(act, en, m)
                    hi(w[0][:, m], raw[:, m]).then_inc(sg["w_hi"], 1)
                if later(e):
                    act.wait_ge(sg["g_weighted"], unit_no(e - 1, j) + 1)
                else:
                    act.wait_ge(sg["g_ready"], u + 1)
                if later(u - 1):
                    act.wait_ge(sg["down_done"], u - 1)
                hi(gs[0][:, j % 2, :], g[:, j % 2, :]).then_inc(sg["g_hi"], 1)

            def expert(e, more=True):
                for j in range(UNITS):
                    unit(e, j, more)
            expert(0)
            for f in range(EXP * 2):
                act.wait_ge(sg["wt_full"], f + 1)
                act.activation(w_bc[:, f // 2, half(f % 2)], ps_h[:, f % 4, 0:HALF], ACT.Copy).then_inc(sg["w_bc_ready"], 1)
            with act.Fori(1, EXP) as e:
                expert(e)
            expert(EXP, False)
            for hf in range(2):
                act.wait_ge(sg["down_done"], UNITS * (EXP + 1) - 1 + hf)
                act.activation(y_sb[:, 0, half(hf)], ps_y[:, hf, 0:HALF], ACT.Copy).then_inc(sg["y_copied"], 1)
            for hf in range(2):
                for b in range(4 * hf + 2, 4 * hf + 4):
                    act.wait_ge(sg["y_shift"], hf + 1)
                    act.activation(y_out[:, b, :], res[:, b, :], ACT.Identity, bias=shift[:, b:b + 1],
                                   scale=rstd[:, b:b + 1]).then_inc(sg["y_ready_act"], 1)

        @block.vector
        def _(dve):
            def lo(dst, src, part):
                return dve.tensor_tensor(dst, src, part.bitcast(F32), ALU.subtract)

            for i in range(4):
                k, hf = i // 2, i % 2
                dve.wait_ge(sg["x2t_hi"], i + 1)
                lo(x2t[1][:, k, half(hf)], ps_h[:, i, 0:HALF], x2t[0][:, k, half(hf)]).then_inc(sg["x2t_lo"], 1)
            dve.wait_ge(sg["gw_hi"], 1)
            lo(gw[1][:, :, :], gw_raw[:, :, :], gw[0][:, :, :]).then_inc(sg["gw_lo"], 1)
            for m in range(MH):
                dve.wait_ge(sg["w_hi"], m + 1)
                lo(w[1][:, m], raw[:, m], w[0][:, m]).then_inc(sg["w_lo"], 1)

            def gating(j):
                if j == 0:
                    dve.wait_ge(sg["eid_ready"], 1)
                    dve.wait_ge(sg["logits_full"], 1)
                    dve.tensor_copy(logits[:, :, :].rearrange("p b e -> p (b e)"), ps_y[0:N, 2, 0:B * EXP])\
                        .then_inc(sg["gating"], 1)
                    dve.wait_ge(sg["gating"], 1)
                elif j < 5:
                    for b in (2 * j - 2, 2 * j - 1):
                        dve.max(top[:, b, :], logits[:, b, :]).then_inc(sg["top_ready"], 1)
                        dve.wait_ge(sg["top_ready"], b + 1)
                        dve.max_index(top_i[:, b, :], top[:, b, :], logits[:, b, :]).then_inc(sg["gating"], 1)
                    if j == 4:
                        dve.wait_ge(sg["gating"], 1 + B)
                        dve.tensor_copy(top_f[:, :, :], top_i[:, :, 0:2]).then_inc(sg["gating"], 1)
                        dve.tensor_tensor(gap[:, :], top[:, :, 1], top[:, :, 0], ALU.subtract).then_inc(sg["gap_ready"], 1)
                elif j == 5:
                    dve.wait_ge(sg["gap_exp"], 1)
                    dve.tensor_scalar(w_top[:, 0, :], gap_e[:, :], 1.0, None, ALU.add).then_inc(sg["gating"], 1)
                    dve.wait_ge(sg["gating"], 3 + B)
                    dve.reciprocal(w_top[:, 0, :], w_top[:, 0, :]).then_inc(sg["gating"], 1)
                    dve.wait_ge(sg["gating"], 4 + B)
                    dve.tensor_tensor(w_top[:, 1, :], w_top[:, 0, :], gap_e[:, :], ALU.mult).then_inc(sg["gating"], 1)
                    for c in range(2):
                        dve.tensor_tensor(pick[:, c], eid[:, :].unsqueeze(1).to_broadcast([N, B, EXP]),
                                          top_f[:, :, c].unsqueeze(2).to_broadcast([N, B, EXP]), ALU.is_equal)\
                            .then_inc(sg["gating"], 1)
                    dve.wait_ge(sg["gating"], 7 + B)
                    for c in range(2):
                        dve.tensor_tensor(pick[:, c], pick[:, c], w_top[:, c, :].unsqueeze(2).to_broadcast([N, B, EXP]),
                                          ALU.mult).then_inc(sg["gating"], 1)
                    dve.wait_ge(sg["gating"], 9 + B)
                    dve.tensor_tensor(w_tok[:, :, :], pick[:, 0], pick[:, 1], ALU.add).then_inc(sg["w_tok_ready"], 1)

            def unit(e, j, more):
                u = unit_no(e, j)
                dve.wait_ge(sg["silu"], u + 1)
                if later(u - 1):
                    dve.wait_ge(sg["g_lo"], u - 1)
                dve.tensor_tensor(g[:, j % 2, :], s_act[:, j % 2, :], ps_h[:, 2 * (j % 2) + 1, 0:HALF], ALU.mult)\
                    .then_inc(sg["g_ready"], 1)
                sp = split_at(j)
                if sp and (sp[0] == 0 or more) and (sp[0] == 1 or later(e)):
                    en, m = e + sp[0], sp[1]
                    dve.wait_ge(sg["w_hi"], MH * en + m + 1)
                    lo(w[1][:, m], raw[:, m], w[0][:, m]).then_inc(sg["w_lo"], 1)

            def expert(e, more=True):
                for j in range(UNITS):
                    unit(e, j, more)
                    if isinstance(e, int) and e == 0:
                        gating(j)
            expert(0)
            with dve.Fori(1, EXP) as e:
                expert(e)
            expert(EXP, False)

            for hf in range(2):
                dve.wait_ge(sg["down_done"], UNITS * (EXP + 1) - 1 + hf)
                dve.tensor_copy(y_sb[:, 1, half(hf)], ps_y[:, 2 + hf, 0:HALF]).then_inc(sg["y_copied_dve"], 1)

            def residual(hf):
                for b in range(4 * hf, 4 * hf + 4):
                    dve.wait_ge(sg["yt_full"], b + 1)
                    dve.tensor_tensor(res[:, b, :], ps_h[0:N, b % 4, 0:D], x2_all[0:N, b, :], ALU.add).then_inc(sg["y_res"], 1)
                    dve.wait_ge(sg["y_res"], b + 1)
                    dve.bn_stats(stats[:, b, :], res[:, b, :]).then_inc(sg["y_stats"], 1)
                for b in range(4 * hf, 4 * hf + 4):
                    dve.wait_ge(sg["y_stats"], b + 1)
                    dve.bn_aggr(mv[:, b, :], stats[:, b, :]).then_inc(sg["y_aggr"], 1)
                dve.wait_ge(sg["y_aggr"], 4 * hf + 4)
                h = slice(4 * hf, 4 * hf + 4)
                dve.tensor_scalar(var[:, h], mv[:, h, 1], EPS, None, ALU.add).then_inc(sg["y_var"], 1)

            def normalise(hf):
                h = slice(4 * hf, 4 * hf + 4)
                dve.wait_ge(sg["y_rstd"], hf + 1)
                dve.scalar_tensor_tensor(shift[:, h], mv[:, h, 0], -1.0, rstd[:, h], op0=ALU.mult, op1=ALU.mult)\
                    .then_inc(sg["y_shift"], 1)
                for b in range(4 * hf, 4 * hf + 2):
                    dve.tensor_scalar(y_out[:, b, :], res[:, b, :], mv[:, b, 0:1], rstd[:, b:b + 1], ALU.subtract, ALU.mult)\
                        .then_inc(sg["y_ready"], 1)
            residual(0)
            residual(1)
            normalise(0)
            normalise(1)

        @block.tensor
        def _(pe):
            for i in range(4):
                k, hf = i // 2, i % 2
                for j in range(4):
                    last = pe.transpose(ps_h[:, i, j * N:(j + 1) * N], x2_all[0:N, 4 * hf + j, k * P:(k + 1) * P],
                                        ident[0:N, 0:N])
                last.then_inc(sg["x2t_full"], 1)
            pe.wait_ge(sg["x2t_lo"], 4)
            pe.wait_ge(sg["gw_lo"], 1)
            for hf in range(2):
                for k in range(KD):
                    last = product(pe, ps_y[0:EXP, hf, 0:HALF], tuple(c[:, k, :] for c in gw),
                                   tuple(c[:, k, half(hf)] for c in x2t), start=k == 0, stop=k == KD - 1)
            last.then_inc(sg["logits_t_full"], 1)

            def logits_transpose():
                pe.wait_ge(sg["logits_t_ready"], 1)
                for b in range(B):
                    last = pe.transpose(ps_y[0:N, 2, b * EXP:(b + 1) * EXP],
                                        logits_t[:, b // 4, (b % 4) * N:(b % 4 + 1) * N], ident[0:EXP, 0:EXP])
                last.then_inc(sg["logits_full"], 1)

            def up(e, j):
                u, m = unit_no(e, j), j // 2
                pe.wait_ge(sg["w_lo"], MH * e + m + 1)
                if isinstance(e, int) and (e, j) == (1, 1):
                    pe.wait_ge(sg["w_bc_ready"], 2 * EXP)
                if later(u - 1):
                    pe.wait_ge(sg["g_ready"], u - 1)
                for i in range(2):
                    for k in range(KD):
                        last = product(pe, ps_h[:, 2 * (j % 2) + i, 0:HALF], tuple(c[:, m, 2 * i + k, :] for c in w),
                                       tuple(c[:, k, half(j % 2)] for c in x2t), start=k == 0, stop=k == KD - 1)
                last.then_inc(sg["h_full"], 1)

            def down(e, j, first=False, final=False):
                u, m = unit_no(e, j), j // 2
                pe.wait_ge(sg["g_lo"], u + 1)
                if first:
                    pe.wait_ge(sg["gating"], 1)
                for o in range(2):
                    last = product(pe, ps_y[:, 2 * o + j % 2, 0:HALF], tuple(c[:, m, 4 + o, :] for c in w),
                                   tuple(c[:, j % 2, :] for c in gs), start=first, stop=final, skip_group_check=True)
                last.then_inc(sg["down_done"], 1)

            def expert(e):
                for j in range(UNITS):
                    up(e, j)
                    if isinstance(e, int) and e == 0 and j == 0:
                        logits_transpose()
                    if j >= 2:
                        down(e, j - 2, first=isinstance(e, int) and e == 0 and j < 4)
                    elif later(e - 1):
                        down(e - 1, j + UNITS - 2)

            expert(0)
            down(0, UNITS - 2)
            pe.wait_ge(sg["w_tok_ready"], 1)
            for f in range(EXP * 2):
                if f == 0:
                    pe.wait_ge(sg["g_ready"], UNITS - 1)
                if f == 2:
                    pe.wait_ge(sg["g_ready"], UNITS)
                if f == 4:
                    down(0, UNITS - 1)
                if later(f - 3):
                    pe.wait_ge(sg["w_bc_ready"], f - 3)
                for i in range(4):
                    b = 4 * (f % 2) + i
                    last = pe.transpose(ps_h[:, f % 4, i * N:(i + 1) * N],
                                        w_tok[:, b, f // 2:f // 2 + 1].to_broadcast([N, P]), ident[0:N, 0:N])
                last.then_inc(sg["wt_full"], 1)
            pe.wait_ge(sg["w_bc_ready"], 2 * EXP - 2)
            expert(1)
            with pe.Fori(2, EXP + 1) as e:
                expert(e)
            for j in (UNITS - 2, UNITS - 1):
                down(EXP, j, final=True)
            for b in range(B):
                pe.wait_ge(sg["y_copied"], b // 4 + 1)
                pe.wait_ge(sg["y_copied_dve"], b // 4 + 1)
                if b < 4:
                    pe.wait_ge(sg["g_ready"], UNITS * (EXP + 1))
                else:
                    pe.wait_ge(sg["y_res"], b - 3)
                for k in range(KD):
                    last = pe.transpose(ps_h[0:N, b % 4, k * P:(k + 1) * P], y_sb[:, k, b * N:(b + 1) * N], ident[:, :])
                last.then_inc(sg["yt_full"], 1)


def decoder_layer(nc, A, out):
    with ExitStack() as outer:
        x2_all = outer.enter_context(nc.sbuf_tensor("x2_all", [P, B, D], F32))
        ident = outer.enter_context(nc.sbuf_tensor("ident", [P, P], F32))
        store = outer.enter_context(nc.sbuf_tensor("store", [P, B, 2 * D], F32))
        raw = store[:, :, :].rearrange("p b c -> p (b c)")[:, 0:MH * 6 * P].rearrange("p (m s c) -> p m s c", m=MH, s=6)
        signals = [Signals(nc, outer, block) for block in ("prep", "attn", "ffn")]
        with ExitStack() as ctx:
            consts = {n: ctx.enter_context(nc.sbuf_tensor("const_" + n, shape, F32)) for n, shape in
                      (("proj_b", [N, D]), ("b_out", [N, D]), ("gate", [N, 1]), ("neg_half", [N, 1]),
                       ("gamma", [P, KD]), ("beta", [P, KD]))}
            weights = [split_pair(nc, ctx, name, shape) for name, shape in
                       (("w_k", [P, KD, INNER]), ("w_v", [P, KD, INNER]), ("w_q", [P, KD, INNER]),
                        ("w_o", [P, PAIRS, D]), ("w_proj", [P, KD, D]))]
            qk_rot = store[0:N, :, :]
            v_all = ctx.enter_context(nc.sbuf_tensor("v_all", [N, B, D], F32))
            preparation_block(nc, signals[0], A, ident, consts, weights, qk_rot, v_all)
            attention_block(nc, signals[1], A, x2_all, ident, consts, weights, qk_rot, v_all, raw, signals[2])
        ffn_block(nc, signals[2], A, x2_all, ident, raw, out)


def rope_table():
    inv = (np.float32(1.0) / np.float32(10000.0) ** (np.arange(0, HD, 2, dtype=np.float32) / np.float32(HD))).astype(np.float32)
    f = np.arange(N, dtype=np.float32)[:, None] * inv[None, :]
    cos, sin = np.cos(f), np.sin(f)
    return np.stack([np.concatenate([cos, cos], 1), np.concatenate([-sin, sin], 1)], 1).astype(np.float32)


_INS = {"x": "x", "ctx_1024": "ctx", "L0_attn_qkv_w": "qkv_w", "L0_attn_qkv_b": "qkv_b", "L0_attn_proj_w": "proj_w",
        "L0_attn_proj_b": "proj_b", "L0_xattn_ln_gamma": "gamma", "L0_xattn_ln_beta": "beta", "L0_xattn_w_q": "w_q",
        "L0_xattn_w_kv": "w_kv", "L0_xattn_w_out": "w_out", "L0_xattn_b_out": "b_out", "L0_xattn_gate": "gate",
        "L0_ffn_gate_w": "gate_w", "L0_ffn_ew1": "ew1", "L0_ffn_ew2": "ew2", "L0_ffn_ew3": "ew3",
        "L0_ffn_sw1": "sw1", "L0_ffn_sw2": "sw2", "L0_ffn_sw3": "sw3"}


def kernel(**inputs):
    import concourse.bacc as _bacc
    from concourse import mybir as _mybir
    from concourse.bass_utils import run_bass_kernel_spmd as _run

    nc = _bacc.Bacc("TRN2", target_bir_lowering=False, num_devices=1)
    arrays, args = {}, {}
    for name, short in _INS.items():
        a = np.ascontiguousarray(inputs[name])
        arrays[f"in_{name}_dram"] = a
        args[short] = nc.dram_tensor(f"in_{name}_dram", a.shape, _mybir.dt.from_np(a.dtype), kind="ExternalInput").ap()
    table = rope_table()
    arrays["in_rope_dram"] = table
    args["rope"] = nc.dram_tensor("in_rope_dram", table.shape, _mybir.dt.from_np(table.dtype), kind="ExternalInput").ap()
    out = nc.dram_tensor("out_0_dram", (B, N, D), _mybir.dt.from_np(np.dtype("float32")), kind="ExternalOutput").ap()
    decoder_layer(nc, args, out)
    r = _run(nc, [arrays], core_ids=[0])
    return r.results[0]["out_0_dram"]
```
